# Optimizing a Trainium2 kernel written in Bass

```python
import numpy as np
import jax
import jax.numpy as jnp

def _softmax(x, axis=-1):
    return jax.nn.softmax(x, axis=axis)

def _gelu(x):
    return jax.nn.gelu(x, approximate=True)

def _silu(x):
    return jax.nn.silu(x)

def _sigmoid(x):
    return jax.nn.sigmoid(x)

def _layernorm(x, axis=-1, eps=1e-05):
    m = jnp.mean(x, axis=axis, keepdims=True)
    v = jnp.var(x, axis=axis, keepdims=True)
    return (x - m) / jnp.sqrt(v + eps)

def _scatter_add(tgt, idx, src, axis=0):
    return tgt.at[idx].add(src)

def _segment_sum(src, seg, n):
    return jax.ops.segment_sum(src, seg, n)
kernel_name = 'mk_lm_tower_d1_tok_ids512_r4_9efc51'

def setup_inputs(seed: int=0):
    np.random.seed(seed)
    _w = jnp.asarray

    def _rec_inputs():
        import jax
        import jax.numpy as jnp
        _rk = jax.random.key(seed)
        x = jax.random.randint(jax.random.fold_in(_rk, 1), (32, 128), 0, 22, jnp.int32)
        itok_BS_0_21 = jax.random.randint(jax.random.fold_in(_rk, 21), (32, 128), 0, 22, jnp.int32)
        return (x, itok_BS_0_21)
    x, itok_BS_0_21 = _rec_inputs()

    def _L0_tok_setup():
        import jax, jax.numpy as jnp
        import numpy as np
        NEG = -100000000.0

        def nw_value(theta, A):
            N, M = theta.shape
            ii = jnp.arange(N + 1)
            neg1 = jnp.full((1,), NEG, theta.dtype)
            prev2 = jnp.full((N + 1,), NEG, theta.dtype).at[0].set(0.0)
            prev = jnp.full((N + 1,), NEG, theta.dtype)

            def step(carry, d):
                prev, prev2 = carry
                jj = d - ii
                valid = (ii >= 1) & (ii <= N) & (jj >= 1) & (jj <= M)
                th = theta[jnp.clip(ii - 1, 0, N - 1), jnp.clip(jj - 1, 0, M - 1)]
                diag = jnp.concatenate([neg1, prev2[:-1]])
                up = jnp.concatenate([neg1, prev[:-1]]) + A
                left = prev + A
                v = jax.nn.logsumexp(jnp.stack([diag, up, left]), axis=0)
                new = jnp.where(valid, th + v, NEG)
                return ((new, prev), None)
            (last, _), _ = jax.lax.scan(step, (prev, prev2), jnp.arange(2, N + M + 1))
            return last[N]
        key = jax.random.key(seed)
        ks = jax.random.split(key, 7)
        B, N, M = (16, 128, 128)
        n_alpha, n_input, n_embed = (22, 128, 128)
        return {'x': jax.random.randint(ks[0], (B, N), 0, n_alpha, dtype=jnp.int32), 'y': jax.random.randint(ks[1], (B, M), 0, n_alpha, dtype=jnp.int32), 'W_embed': jax.random.normal(ks[2], (n_alpha, n_input), jnp.float32) * 0.1, 'W_proj': jax.random.normal(ks[3], (n_input, n_embed), jnp.float32) * 0.05, 'b_proj': jax.random.normal(ks[4], (n_embed,), jnp.float32) * 0.01, 'W_gap': jax.random.normal(ks[5], (2 * n_embed,), jnp.float32) * 0.05, 'b_gap': jax.random.normal(ks[6], (1,), jnp.float32) * 0.01}
    _L0_tok_all = _L0_tok_setup()
    _L0_tok_in = {k: v for k, v in _L0_tok_all.items() if k in ('W_embed', 'W_proj', 'b_proj', 'W_gap', 'b_gap')}
    del _L0_tok_all

    def _L0_attn_setup():
        import jax, jax.numpy as jnp
        import numpy as np
        EPS = 1e-05

        def _layernorm(x):
            mu = x.mean(axis=-1, keepdims=True)
            var = x.var(axis=-1, keepdims=True)
            return (x - mu) / jnp.sqrt(var + EPS)
        key = jax.random.key(seed)
        k1, k2, k3, k4, k5 = jax.random.split(key, 5)
        B, T, E, H = (8, 512, 128, 8)
        d = E // H
        return {'input1': jax.random.normal(k1, (B, T, E), dtype=jnp.float32), 'Wq': jax.random.normal(k2, (H, d), dtype=jnp.float32) * 0.1, 'Wk': jax.random.normal(k3, (H, d), dtype=jnp.float32) * 0.1, 'Wv': jax.random.normal(k4, (H, d, d), dtype=jnp.float32) * 0.1, 'Wm': jax.random.normal(k5, (E, E), dtype=jnp.float32) * 0.05}
    _L0_attn_all = _L0_attn_setup()
    _L0_attn_in = {k: v for k, v in _L0_attn_all.items() if k in ('Wq', 'Wk', 'Wv', 'Wm')}
    del _L0_attn_all

    def _L0_ffn_setup():
        import jax, jax.numpy as jnp
        import numpy as np
        B, S, D, F, E, K = (4, 512, 128, 512, 8, 2)
        key = jax.random.key(seed)
        kx, kg, kw, kv, k2 = jax.random.split(key, 5)
        scale = 0.02
        return {'x': jax.random.normal(kx, (B, S, D), dtype=jnp.float32), 'Wg': jax.random.normal(kg, (D, E), dtype=jnp.float32) * scale, 'W': jax.random.normal(kw, (E, D, F), dtype=jnp.float32) * scale, 'V': jax.random.normal(kv, (E, D, F), dtype=jnp.float32) * scale, 'W2': jax.random.normal(k2, (E, F, D), dtype=jnp.float32) * scale}
    _L0_ffn_all = _L0_ffn_setup()
    _L0_ffn_in = {k: v for k, v in _L0_ffn_all.items() if k in ('Wg', 'W', 'V', 'W2')}
    del _L0_ffn_all
    return {'x': x, 'itok_BS_0_21': itok_BS_0_21, 'L0_tok_W_embed': _L0_tok_in['W_embed'], 'L0_tok_W_proj': _L0_tok_in['W_proj'], 'L0_tok_b_proj': _L0_tok_in['b_proj'], 'L0_tok_W_gap': _L0_tok_in['W_gap'], 'L0_tok_b_gap': _L0_tok_in['b_gap'], 'L0_attn_Wq': _L0_attn_in['Wq'], 'L0_attn_Wk': _L0_attn_in['Wk'], 'L0_attn_Wv': _L0_attn_in['Wv'], 'L0_attn_Wm': _L0_attn_in['Wm'], 'L0_ffn_Wg': _L0_ffn_in['Wg'], 'L0_ffn_W': _L0_ffn_in['W'], 'L0_ffn_V': _L0_ffn_in['V'], 'L0_ffn_W2': _L0_ffn_in['W2']}

def reference(x, itok_BS_0_21, L0_tok_W_embed, L0_tok_W_proj, L0_tok_b_proj, L0_tok_W_gap, L0_tok_b_gap, L0_attn_Wq, L0_attn_Wk, L0_attn_Wv, L0_attn_Wm, L0_ffn_Wg, L0_ffn_W, L0_ffn_V, L0_ffn_W2):
    import jax
    import jax.numpy as jnp

    def _L0_tok_ref(x, y, W_embed, W_proj, b_proj, W_gap, b_gap):
        import jax, jax.numpy as jnp
        import numpy as np
        NEG = -100000000.0

        def nw_value(theta, A):
            N, M = theta.shape
            ii = jnp.arange(N + 1)
            neg1 = jnp.full((1,), NEG, theta.dtype)
            prev2 = jnp.full((N + 1,), NEG, theta.dtype).at[0].set(0.0)
            prev = jnp.full((N + 1,), NEG, theta.dtype)

            def step(carry, d):
                prev, prev2 = carry
                jj = d - ii
                valid = (ii >= 1) & (ii <= N) & (jj >= 1) & (jj <= M)
                th = theta[jnp.clip(ii - 1, 0, N - 1), jnp.clip(jj - 1, 0, M - 1)]
                diag = jnp.concatenate([neg1, prev2[:-1]])
                up = jnp.concatenate([neg1, prev[:-1]]) + A
                left = prev + A
                v = jax.nn.logsumexp(jnp.stack([diag, up, left]), axis=0)
                new = jnp.where(valid, th + v, NEG)
                return ((new, prev), None)
            (last, _), _ = jax.lax.scan(step, (prev, prev2), jnp.arange(2, N + M + 1))
            return last[N]
        zx = jnp.take(W_embed, x, axis=0) @ W_proj + b_proj
        zy = jnp.take(W_embed, y, axis=0) @ W_proj + b_proj
        theta = jnp.einsum('bid,bjd->bij', zx, zy)
        merged = jnp.concatenate([zx.mean(axis=1), zy.mean(axis=1)], axis=1)
        A = merged @ W_gap + b_gap[0]
        aln = jax.vmap(jax.grad(nw_value, argnums=0))(theta, A)
        return aln

    def _L0_attn_ref(input1, Wq, Wk, Wv, Wm):
        import jax, jax.numpy as jnp
        import numpy as np
        EPS = 1e-05

        def _layernorm(x):
            mu = x.mean(axis=-1, keepdims=True)
            var = x.var(axis=-1, keepdims=True)
            return (x - mu) / jnp.sqrt(var + EPS)
        B, T, E = input1.shape
        H, d = Wq.shape
        xn = _layernorm(input1)
        xh = xn.reshape(B, T, H, d)
        Q = jnp.einsum('bthd,hd->bht', xh, Wq)
        K = jnp.einsum('bthd,hd->bht', xh, Wk)
        V = jnp.einsum('bthd,hde->bhte', xh, Wv)
        A = -(Q[:, :, :, None] - K[:, :, None, :]) ** 2
        P = jax.nn.softmax(A / d ** 0.5, axis=-1)
        O = jnp.einsum('bhts,bhse->bhte', P, V)
        head_result = O.transpose(0, 2, 1, 3).reshape(B, T, E)
        return head_result @ Wm + input1

    def _L0_ffn_ref(x, Wg, W, V, W2):
        import jax, jax.numpy as jnp
        import numpy as np
        B, S, D, F, E, K = (4, 512, 128, 512, 8, 2)
        gate_logits = jnp.einsum('bsd,de->bse', x, Wg)
        topv, topi = jax.lax.top_k(gate_logits, K)
        w = jax.nn.softmax(topv, axis=-1)
        gw = jnp.sum(w[..., None] * jax.nn.one_hot(topi, E, dtype=x.dtype), axis=-2)
        y = jnp.zeros_like(x)
        n_experts = W.shape[0]
        for e in range(n_experts):
            h = jax.nn.silu(jnp.einsum('bsd,df->bsf', x, W[e])) * jnp.einsum('bsd,df->bsf', x, V[e])
            y = y + gw[..., e:e + 1] * jnp.einsum('bsf,fd->bsd', h, W2[e])
        return y
    h = _L0_tok_ref(x, itok_BS_0_21, L0_tok_W_embed, L0_tok_W_proj, L0_tok_b_proj, L0_tok_W_gap, L0_tok_b_gap)
    h = h + _L0_attn_ref(_layernorm(h, axis=-1), L0_attn_Wq, L0_attn_Wk, L0_attn_Wv, L0_attn_Wm)
    h = h + _L0_ffn_ref(_layernorm(h, axis=-1), L0_ffn_Wg, L0_ffn_W, L0_ffn_V, L0_ffn_W2)
    return h

_drawn_inputs = setup_inputs


def setup_inputs(seed=0):
    import zlib

    import numpy as np

    out = dict(_drawn_inputs(seed))
    spreads = {}
    factors = {'L0_tok_b_proj': 6.236,
     'L0_tok_W_gap': 8.0,
     'L0_attn_Wq': 8.0,
     'L0_attn_Wk': 5.256,
     'L0_attn_Wm': 2.684,
     'L0_ffn_Wg': 7.444,
     'L0_ffn_W': 6.984,
     'L0_ffn_V': 6.877,
     'L0_ffn_W2': 6.869}
    for name, (base, spread) in spreads.items():
        noise = np.random.default_rng([zlib.crc32(name.encode()), seed]).standard_normal(out[name].shape)
        drawn = base * np.exp(spread * noise) if base else spread * noise
        out[name] = jnp.asarray(drawn.astype(out[name].dtype))
    for name, factor in factors.items():
        out[name] = (out[name] * factor).astype(out[name].dtype)
    return out
```

```python
import concourse.bass as bass
from concourse import mybir
from contextlib import ExitStack


def tower(nc, tok, we_t, w_proj, b_proj, w_gap, b_gap, iota22, wq_pl, wk_pl, wv_bd, w_m, w_g, w_up, v_up, w_down,
          eye, below, head_mask, q_const, k_const, rank8, region0, out):
    f32 = mybir.dt.float32
    i32 = mybir.dt.int32
    ALU = mybir.AluOpType
    ACT = mybir.ActivationFunctionType
    AX = mybir.AxisListType

    NB, T, E = 32, 128, 128
    NV = we_t.shape[1]
    H = T // 2
    ROWS = 26
    BLKS = 5
    STEPS = ROWS * BLKS
    GR = 2
    NG = ROWS // GR
    NEG = -100000000.0
    X0 = 2.0 ** -60
    LNX0 = 60.0 * 0.6931471805599453

    ctx = ExitStack()
    with ctx:
        def sb(name, shape, dt=f32):
            return ctx.enter_context(nc.sbuf_tensor(name, shape, dt))

        def pb(name, shape, dt=f32):
            return ctx.enter_context(nc.psum_tensor(name, shape, dt))

        def sem(name):
            return ctx.enter_context(nc.semaphore(name))

        th_dram = nc.dram_tensor("th_dram", (2, NB, T, T), f32).ap()
        l_dram = nc.dram_tensor("l_dram", (2, NB, T, T), f32).ap()

        v_dram = nc.dram_tensor("v_dram", (NB,), f32).ap()
        REG = NB * T + 128
        NX, F = 8, 512
        FC = F // 128
        NH, HD = 8, 16
        NQ = NB // 4
        TILES = 2 * NB * T // 128 + NX
        ROW = E + 2
        EPS = 1e-5
        xd_dram = nc.dram_tensor("xd_dram", (NX * REG + 128, ROW), f32).ap()
        y_dram = nc.dram_tensor("y_dram", (2 * NB * T, E), f32).ap()
        wet_sb = sb("wet_sb", [E, NV])
        wproj_sb = sb("wproj_sb", [E, E])
        bproj_sb = sb("bproj_sb", [E, 1])
        wgap_sb = sb("wgap_sb", [E, 2])
        bgap_sb = sb("bgap_sb", [128, 1])
        iota_sb = sb("iota_sb", [NV, 1])
        zt = sb("zt", [E, NV])
        gm = sb("gm", [NV, NV])
        uv = sb("uv", [NV, 2])
        cnt = sb("cnt", [NV, 2, 4, NB])
        gap = sb("gap", [128, 1])
        vtot = sb("vtot", [128, NB])
        nvt = sb("nvt", [128, NB])
        thf = sb("thf", [T, NB, T])
        big = sb("big", [128, 2 * STEPS * H + 2 * (STEPS + 2) * (H + 1)])

        at = [0]

        def cut(n):
            at[0] += n
            return big[:, at[0] - n:at[0]]

        TH = cut(STEPS * H).rearrange("p (s j) -> p s j", j=H)
        TAS = cut(STEPS * H).rearrange("p (s j) -> p s j", j=H)
        M = cut((STEPS + 2) * (H + 1)).rearrange("p (s j) -> p s j", j=H + 1)
        X = cut((STEPS + 2) * (H + 1)).rearrange("p (s j) -> p s j", j=H + 1)
        at[0] = 0
        toki = cut(2 * NB * T)[0:NV, :].bitcast(i32)
        oh = cut(2 * NB * T)[0:NV, :]
        at[0] = 2 * STEPS * H + (STEPS + 2) * (H + 1)
        gy = cut(NB * T)[0:NV, :]
        thr = cut(NB * T).rearrange("p (b j) -> p b j", j=T)
        C = sb("C", [128, 2, H])
        N = sb("N", [128, ROWS, H])
        C3 = sb("C3", [128, ROWS, 3, H])
        U = sb("U", [128, 2, 2, H])
        V = sb("V", [128, 2, H])
        LNX = sb("LNX", [128, ROWS, H + 1])
        x0row = sb("x0row", [128, H + 1])
        lrow = sb("lrow", [128, H + 1])

        ar = 2 * STEPS * H
        lb = big[:, 0:NB * T].rearrange("p (b j) -> p b j", j=T)
        h0 = big[:, STEPS * H:STEPS * H + NB * T].rearrange("p (b j) -> p b j", j=T)
        wup_sb = big[:, ar:ar + NX * F].rearrange("p (e f) -> p e f", f=F)
        vup_sb = big[:, ar + NX * F:ar + 2 * NX * F].rearrange("p (e f) -> p e f", f=F)
        wdn_sb = big[:, ar + 2 * NX * F:ar + 3 * NX * F].rearrange("p (e f) -> p e f", f=F)
        h1 = thf
        spare = [big[:, NB * T:STEPS * H], big[:, STEPS * H + NB * T:2 * STEPS * H], big[:, ar + 3 * NX * F:]]
        used = [0, 0, 0]

        def carve(k, n):
            used[k] += n
            assert used[k] <= spare[k].shape[1], (k, used, spare[k].shape)
            return spare[k][:, used[k] - n:used[k]]

        def quads(k, n=512):
            return carve(k, n)

        x1 = [carve(0, 512).rearrange("p (b j) -> p b j", j=T) for _ in range(2)]
        xn = [carve(0, 512).rearrange("p (b j) -> p b j", j=T) for _ in range(2)]
        xnt = [carve(0, 512) for _ in range(2)]
        on = [carve(0, 512).rearrange("p (b j) -> p b j", j=T) for _ in range(2)]
        sq = [carve(1, 1024) for _ in range(2)]
        pt = [carve(1, 1024) for _ in range(2)]
        kx = [carve(2, 1024) for _ in range(2)]
        va = [carve(2, 4 * NH * (HD + 1)).rearrange("p (b h d) -> p b h d", h=NH, d=HD + 1) for _ in range(2)]
        ont = [carve(2, 512) for _ in range(2)]
        x3t = carve(2, 512)
        pay = sb("pay", [128, 4, 2, ROW])
        qs = [sb(f"qs{k}", [128, 128]) for k in range(2)]
        mv = sb("mv", [128, 4, 2])
        st6 = sb("st6", [128, 4, 6])
        r1 = sb("r1", [128, 2, 4])
        var = sb("var", [128, 2, 4])
        lnv = sb("lnv", [128, 2, 4])
        nwt = sb("nwt", [128, 2, 4])
        mn = sb("mn", [128, 2, NH])
        rc = sb("rc", [128, 2, NH])
        lg = sb("lg", [128, 4, NX])
        lg2 = sb("lg2", [128, 4, NX])
        eq = sb("eq", [128, 4, NX])
        ohk = sb("ohk", [128, 2, 4, NX])
        msk = sb("msk", [128, 4, NX])
        top = sb("top", [128, 2, 4])
        first = sb("first", [128, 4])
        gate = sb("gate", [128, 2, 4])
        rank = sb("rank", [128, 4, NX])
        slotf = sb("slotf", [128, 2, 4])
        slot = sb("slot", [128, NQ, 2, 4], i32)
        run = sb("run", [128, NB + 1, NX])
        tokid = sb("tokid", [128, 2, NB], i32)
        tokf = sb("tokf", [128, 2, NB])
        padt = sb("padt", [128, ROW])
        wq_sb = sb("wq_sb", [E, 4, 128])
        wk_sb = sb("wk_sb", [E, 4, 128])
        wv_sb = sb("wv_sb", [E, E])
        wm_sb = sb("wm_sb", [E, E])
        wg_sb = sb("wg_sb", [E, NX])
        eye_sb = sb("eye_sb", [128, 128])
        below_sb = sb("below_sb", [128, 128])
        ones_sb = sb("ones_sb", [128, 128])
        mask_sb = sb("mask_sb", [128, NH])
        sc_sb = sb("sc_sb", [128, 1])
        mc_sb = sb("mc_sb", [128, 1])
        rank8_sb = sb("rank8_sb", [128, NX])
        region_sb = sb("region_sb", [128, NX])
        tl = sb("tl", [128, 8, NX])
        tili = sb("tili", [128, 4, TILES + 8], i32)
        tilf = sb("tilf", [128, 6, TILES])
        tilesf = sb("tilesf", [128, TILES])
        past = sb("past", [128, TILES, NX])
        used = [0, 0, 0]
        xrow = [carve(1, ROW) for _ in range(4)]
        xcol = [carve(1, T) for _ in range(2)]
        yrow = [carve(1, E) for _ in range(4)]
        act_up = [carve(0, F) for _ in range(2)]
        hid = [carve(0, F) for _ in range(2)]
        hidt = [carve(0, F) for _ in range(2)]
        dest = sb("dest", [128, 4], i32)

        ps = pb("ps", [128, 8, 512])

        s_in = sem("s_in")
        s_tok = sem("s_tok")
        s_oh = sem("s_oh")
        s_cnt = sem("s_cnt")
        s_small = sem("s_small")
        s_smallv = sem("s_smallv")
        s_gyp = sem("s_gyp")
        s_gy = sem("s_gy")
        s_thp = sem("s_thp")
        s_thf = sem("s_thf")
        s_thr = sem("s_thr")
        s_thd = sem("s_thd")
        s_th = [sem(f"s_th{c}") for c in range(BLKS)]
        s_pad = sem("s_pad")
        s_gap = sem("s_gap")
        s_tas = sem("s_tas")
        s_init = sem("s_init")
        s_gauge = sem("s_gauge")
        s_lin = sem("s_lin")
        s_diff = sem("s_diff")
        s_coef = sem("s_coef")
        s_lnrow = sem("s_lnrow")
        s_ren = sem("s_ren")
        s_lnx = sem("s_lnx")
        s_l = sem("s_l")
        s_lst = sem("s_lst")
        s_ld = sem("s_ld")
        s_vst = sem("s_vst")
        s_v = sem("s_v")
        s_nv = sem("s_nv")
        s_e1 = sem("s_e1")
        s_e2 = sem("s_e2")
        s_e3 = sem("s_e3")
        s_out = sem("s_out")
        s_const = sem("s_const")
        s_consts = sem("s_consts")
        s_wts = sem("s_wts")
        s_ldq = [sem(f"s_ldq{q}") for q in range(NQ)]
        s_h0 = sem("s_h0")
        s_dv = sem("s_dv")
        s_xn = sem("s_xn")
        s_var = sem("s_var")
        s_lnv = sem("s_lnv")
        s_root = sem("s_root")
        s_hx = sem("s_hx")
        s_xntp = sem("s_xntp")
        s_xnt = sem("s_xnt")
        s_vp = sem("s_vp")
        s_va = sem("s_va")
        s_qkp = sem("s_qkp")
        s_qk = sem("s_qk")
        s_d = sem("s_d")
        s_sq = sem("s_sq")
        s_mn = sem("s_mn")
        s_sub = sem("s_sub")
        s_p = sem("s_p")
        s_ptp = sem("s_ptp")
        s_pta = sem("s_pta")
        s_ptd = sem("s_ptd")
        s_o = sem("s_o")
        s_on = sem("s_on")
        s_ontp = sem("s_ontp")
        s_ont = sem("s_ont")
        s_rp = sem("s_rp")
        s_h1 = sem("s_h1")
        s_x3 = sem("s_x3")
        s_x3c = sem("s_x3c")
        s_x3tp = sem("s_x3tp")
        s_x3t = sem("s_x3t")
        s_lgp = sem("s_lgp")
        s_df = sem("s_df")
        s_ex = sem("s_ex")
        s_msk = sem("s_msk")
        s_rkp = sem("s_rkp")
        s_slot = sem("s_slot")
        s_pay = sem("s_pay")
        s_pad0 = sem("s_pad0")
        s_table = sem("s_table")
        s_padw = sem("s_padw")
        s_xr = [sem(f"s_xr{k}") for k in range(4)]
        s_xc = sem("s_xc")
        s_xcp = sem("s_xcp")
        s_up = sem("s_up")
        s_silu = sem("s_silu")
        s_hid = sem("s_hid")
        s_htp = sem("s_htp")
        s_ht = sem("s_ht")
        s_dn = sem("s_dn")
        s_y = sem("s_y")
        s_dest = sem("s_dest")
        s_ys = [sem(f"s_ys{k}") for k in range(4)]
        s_yl = [sem(f"s_yl{q}") for q in range(NQ)]
        s_fin = sem("s_fin")
        s_sc = [sem(f"s_sc{k}") for k in range(8)]
        block = ctx.enter_context(nc.Block())

        def need(eng, s, n):
            if n > 0:
                eng.wait_ge(s, n)

        def shifted(t, row, rows, second):
            a = t[:, bass.ds(row, rows), 0:H]
            return bass.AP(tensor=a.tensor, offset=a.offset, ap=[a.ap[0], [H + 1, rows], [1, second], [1, H]])

        def cells(t, s, lo, hi):
            return t[:, bass.ds(s, 1), lo:hi].rearrange("p s j -> p (s j)")

        def span(c, h):
            lo, hi = max(c * ROWS, h), min((c + 1) * ROWS, T + h)
            return lo, hi

        def lane_rows(t, d, h, lo, hi):
            a = t[d, :, lo - h:hi - h, :] if d == 0 else t[d, :, T - (hi - h):T - (lo - h), :][:, ::-1, :]
            return a[:, :, H * h:H * h + H]

        def at_tile(k):
            return slice(k, k + 1) if isinstance(k, int) else bass.ds(k, 1)

        def round_of(k, c):
            return 16 * (k // 4 + 1) if isinstance(k, int) else (k - c) * 4 + 16

        @block.sync
        def _(sp):
            for dst, src in ((wet_sb[:], we_t), (wproj_sb[:], w_proj), (bproj_sb[:], b_proj),
                             (wgap_sb[:], w_gap), (bgap_sb[:], b_gap), (iota_sb[:], iota22)):
                sp.dma_start(dst, src).then_inc(s_in, 16)
            for dst, src in ((wq_sb[:], wq_pl.rearrange("g e c -> e g c")), (wk_sb[:], wk_pl.rearrange("g e c -> e g c")),
                             (wv_sb[:], wv_bd), (wm_sb[:], w_m), (wg_sb[:], w_g), (eye_sb[:], eye), (below_sb[:], below),
                             (mask_sb[:], head_mask), (sc_sb[:], q_const), (mc_sb[:], k_const),
                             (rank8_sb[:], rank8), (region_sb[:], region0)):
                sp.dma_start(dst, src).then_inc(s_const, 16)
            sp.dma_start(toki, tok.partition_broadcast(NV)).then_inc(s_tok, 16)
            for q in range(8):
                sp.wait_ge(s_thf, q + 1)
                b = slice(4 * q, 4 * q + 4)
                sp.dma_start(th_dram[0, b].rearrange("b i j -> i b j"), thf[:, b, :]).then_inc(s_thd, 16)
                sp.wait_ge(s_thr, q + 1)
                sp.dma_start(th_dram[1, b].rearrange("b i j -> i b j"), thr[:, b, :]).then_inc(s_thd, 16)
            sp.wait_ge(s_thd, 16 * 16)
            for c in range(BLKS):
                for h in range(2):
                    lo, hi = span(c, h)
                    for d in range(2):
                        lane = 64 * h + 32 * d
                        sp.dma_start(TH[lane:lane + 32, lo:hi, :],
                                     lane_rows(th_dram, d, h, lo, hi)).then_inc(s_th[c], 16)
            for c in range(BLKS):
                sp.wait_ge(s_l, c + 1)
                for h in range(2):
                    lo, hi = span(c, h)
                    for d in range(2):
                        lane = 64 * h + 32 * d
                        sp.dma_start(lane_rows(l_dram, d, h, lo, hi),
                                     LNX[lane:lane + 32, lo - c * ROWS:hi - c * ROWS, 1:H + 1]).then_inc(s_lst, 16)
            sp.dma_start(v_dram.rearrange("(b o) -> b o", o=1),
                         LNX[64:96, T - (BLKS - 1) * ROWS, H:H + 1]).then_inc(s_vst, 16)
            sp.wait_ge(s_lst, 16 * 4 * BLKS)
            sp.wait_ge(s_vst, 16)
            sp.dma_start(vtot[:, :], v_dram.partition_broadcast(128)).then_inc(s_v, 16)
            for q in range(NQ):
                b = slice(4 * q, 4 * q + 4)
                sp.dma_start(h0[:, b, :], l_dram[0, b].rearrange("b i j -> i b j")).then_inc(s_ldq[q], 16)
                sp.dma_start(lb[:, b, :], l_dram[1, b].rearrange("b i j -> i b j")).then_inc(s_ldq[q], 16)
            sp.dma_start(wup_sb, w_up.rearrange("e d f -> d e f")).then_inc(s_wts, 16)
            sp.dma_start(vup_sb, v_up.rearrange("e d f -> d e f")).then_inc(s_wts, 16)
            sp.dma_start(wdn_sb.rearrange("p e (c n) -> p e c n", n=E),
                         w_down.rearrange("e (c p) n -> p e c n", p=128)).then_inc(s_wts, 16)
            sp.wait_ge(s_pad0, 2)
            sp.dma_start(xd_dram[NX * REG:NX * REG + 128, :], padt[:]).then_inc(s_padw, 16)
            sp.wait_ge(s_table, 1)
            for e in range(NX):
                row = sp.value_load(tili[0:1, 2, e:e + 1], min_val=0, max_val=NX * REG)
                sp.dma_start(xd_dram[bass.ds(row, 128), :], padt[:]).then_inc(s_padw, 16)
            for k in range(8):
                sp.wait_ge(s_sc[k], 16 * NQ)
            sp.wait_ge(s_padw, 16 * (NX + 1))

            def load(k, c):
                row = sp.value_load(tili[0:1, 0, bass.ds(k, 1)] if not isinstance(k, int) else tili[0:1, 0, k:k + 1],
                                    min_val=0, max_val=NX * REG)
                if not (isinstance(k, int) and k < 4):
                    sp.wait_ge(s_xc, k - 3)
                    sp.wait_ge(s_y, k - 3)
                    sp.wait_ge(s_dest, k - 3)
                sp.dma_start(xrow[c], xd_dram[bass.ds(row, 128), :]).then_inc(s_xr[c], 16)

            for k in range(4):
                load(k, k)
            with sp.Fori(4, TILES, 4) as t:
                for c in range(4):
                    load(t + c, c)
            for c in range(4):
                sp.wait_ge(s_ys[c], 16 * (TILES // 4))
            for q in range(NQ):
                b = slice(4 * q, 4 * q + 4)
                y = y_dram.rearrange("(k b t) e -> k t b e", k=2, t=T)
                sp.dma_start(lb[:, b, :], y[0][:, b, :]).then_inc(s_yl[q], 16)
                sp.dma_start(h0[:, b, :], y[1][:, b, :]).then_inc(s_yl[q], 16)
            for q in range(NQ):
                b = slice(4 * q, 4 * q + 4)
                sp.wait_ge(s_fin, 2 * q + 2)
                sp.dma_start(out[b].rearrange("b i j -> i b j"), h1[:, b, :]).then_inc(s_out, 16)
            sp.wait_ge(s_out, 16 * NQ)

        @block.tensor
        def _(pe):
            pe.wait_ge(s_in, 16 * 6)
            nc.tensor.matmul(ps[:, 0, 0:NV], wproj_sb[:], wet_sb[:], start=True, stop=True).then_inc(s_small, 1)
            pe.wait_ge(s_smallv, 1)
            nc.tensor.matmul(ps[0:NV, 1, 0:NV], zt[:], zt[:], start=True, stop=True)
            nc.tensor.matmul(ps[0:NV, 2, 0:2], zt[:], wgap_sb[:], start=True, stop=True).then_inc(s_small, 1)
            pe.wait_ge(s_smallv, 2)
            pe.wait_ge(s_oh, 2)
            for q in range(8):
                nc.tensor.matmul(ps[0:NV, q, :], gm[:], oh[:, NB * T + 512 * q:NB * T + 512 * q + 512],
                                 start=True, stop=True).then_inc(s_gyp, 1)
            for q in range(8):
                pe.wait_ge(s_gy, q + 1)
                for k in range(4):
                    b = 4 * q + k
                    m = nc.tensor.matmul(ps[:, q, T * k:T * k + T], oh[:, b * T:b * T + T], gy[:, b * T:b * T + T],
                                         start=True, stop=True)
                m.then_inc(s_thp, 1)
            pe.wait_ge(s_cnt, 3)
            pe.wait_ge(s_thf, 1)
            pe.wait_ge(s_thr, 1)
            nc.tensor.matmul(ps[:, 0, 0:1], cnt[:, 0].rearrange("p r b -> p (r b)"), uv[:, 0:1], start=True, stop=False)
            nc.tensor.matmul(ps[:, 0, 0:1], cnt[:, 1].rearrange("p r b -> p (r b)"), uv[:, 1:2],
                             start=False, stop=True).then_inc(s_small, 1)

            def front(q):
                r = q % 2
                pe.wait_ge(s_xn, q + 1)
                need(pe, s_x3t, q - 1)
                need(pe, s_ont, q - 1)
                for k in range(4):
                    m = nc.tensor.transpose(ps[:, 0, T * k:T * k + T], xn[r][:, k, :], eye_sb[:])
                m.then_inc(s_xntp, 1)
                pe.wait_ge(s_xnt, q + 1)
                need(pe, s_h1, q - 1)
                for k in range(4):
                    m = nc.tensor.matmul(ps[:, 1, T * k:T * k + T], xnt[r][:, T * k:T * k + T], wv_sb[:],
                                         start=True, stop=True)
                m.then_inc(s_vp, 1)
                need(pe, s_slot, q - 1)
                for n, w in ((0, wq_sb), (1, wk_sb)):
                    for k in range(4):
                        m = nc.tensor.matmul(ps[:, 2, T * n:T * n + T], w[:, k, :], xnt[r][:, T * k:T * k + T],
                                             start=(k == 0), stop=(k == 3))
                m.then_inc(s_qkp, 1)

            def distances(n):
                q, k = n // 4, n % 4
                g = slice(32 * k, 32 * k + 32)
                pe.wait_ge(s_qk, q + 1)
                need(pe, s_sq, n)
                need(pe, s_mn, n)
                for c in range(2):
                    m = nc.tensor.matmul(ps[:, 3 + c, :], qs[q % 2][g, :], kx[q % 2][g, 512 * c:512 * c + 512],
                                         start=True, stop=True)
                m.then_inc(s_d, 1)

            def attend(n):
                q, k = n // 4, n % 4
                pe.wait_ge(s_p, n + 1)
                need(pe, s_pta, n)
                need(pe, s_ptd, n)
                for h in range(NH):
                    m = nc.tensor.transpose(ps[:, 5 + h // 4, T * (h % 4):T * (h % 4) + T],
                                            sq[n % 2][:, T * h:T * h + T], eye_sb[:])
                m.then_inc(s_ptp, 1)
                pe.wait_ge(s_pta, n + 1)
                pe.wait_ge(s_ptd, n + 1)
                pe.wait_ge(s_va, q + 1)
                need(pe, s_on, n)
                for h in range(NH):
                    m = nc.tensor.matmul(ps[:, 7, (HD + 1) * h:(HD + 1) * (h + 1)], pt[n % 2][:, T * h:T * h + T],
                                         va[q % 2][:, k, h, :], start=True, stop=True)
                m.then_inc(s_o, 1)

            def merge(q):
                r = q % 2
                pe.wait_ge(s_on, 4 * q + 4)
                need(pe, s_xnt, q + 1)
                for k in range(4):
                    m = nc.tensor.transpose(ps[:, 0, T * k:T * k + T], on[r][:, k, :], eye_sb[:])
                m.then_inc(s_ontp, 1)
                pe.wait_ge(s_ont, q + 1)
                pe.wait_ge(s_va, q + 1)
                for k in range(4):
                    m = nc.tensor.matmul(ps[:, 1, T * k:T * k + T], ont[r][:, T * k:T * k + T], wm_sb[:],
                                         start=True, stop=True)
                m.then_inc(s_rp, 1)

            def route(q):
                pe.wait_ge(s_x3, q + 1)
                pe.wait_ge(s_ont, q + 1)
                for k in range(4):
                    m = nc.tensor.transpose(ps[:, 0, T * k:T * k + T], pay[:, k, 0, 0:E], eye_sb[:])
                m.then_inc(s_x3tp, 1)
                pe.wait_ge(s_x3t, q + 1)
                pe.wait_ge(s_qk, q + 1)
                for k in range(4):
                    m = nc.tensor.matmul(ps[:, 2, 256 + NX * k:256 + NX * k + NX], x3t[:, T * k:T * k + T], wg_sb[:],
                                         start=True, stop=True)
                m.then_inc(s_lgp, 1)
                pe.wait_ge(s_msk, q + 1)
                nc.tensor.matmul(ps[:, 2, 320:352], below_sb[:], msk[:, :, :].rearrange("p b e -> p (b e)"),
                                 start=True, stop=True)
                nc.tensor.matmul(ps[:, 2, 352:384], ones_sb[:], msk[:, :, :].rearrange("p b e -> p (b e)"),
                                 start=True, stop=True).then_inc(s_rkp, 1)

            pe.wait_ge(s_const, 16 * 12)
            pe.wait_ge(s_consts, 1)
            for q in range(NQ):
                front(q)
                for n in range(4 * q, 4 * q + 4):
                    distances(n)
                    attend(n)
                merge(q)
                route(q)

            def column(k, c):
                pe.wait_ge(s_xr[c], round_of(k, c))
                if not (isinstance(k, int) and k < 1):
                    pe.wait_ge(s_xc, k)
                nc.tensor.transpose(ps[:, 0, 0:T], xrow[c][:, 0:E], eye_sb[:]).then_inc(s_xcp, 1)

            def up(k, c):
                e = pe.value_load(tili[0:1, 1, at_tile(k)], min_val=0, max_val=NX - 1)
                pe.wait_ge(s_xc, k + 1)
                if not (isinstance(k, int) and k < 2):
                    pe.wait_ge(s_hid, k - 1)
                for n, w in ((1, wup_sb), (3, vup_sb)):
                    m = nc.tensor.matmul(ps[:, n + c % 2, :], xcol[c % 2],
                                         w[:, bass.ds(e, 1), :].rearrange("p e f -> p (e f)"), start=True, stop=True)
                    m.then_inc(s_up, 1)
                return e

            def turn(k, c):
                pe.wait_ge(s_hid, k + 1)
                if not (isinstance(k, int) and k < 2):
                    pe.wait_ge(s_ht, k - 1)
                for n in range(FC):
                    m = nc.tensor.transpose(ps[:, 5 + 2 * (c % 2), T * n:T * n + T], hid[c % 2][:, T * n:T * n + T],
                                            eye_sb[:])
                m.then_inc(s_htp, 1)

            def down(k, c):
                e = pe.value_load(tili[0:1, 1, at_tile(k)], min_val=0, max_val=NX - 1)
                pe.wait_ge(s_ht, k + 1)
                if not (isinstance(k, int) and k < 1):
                    pe.wait_ge(s_y, k)
                for n in range(FC):
                    w = wdn_sb[:, bass.ds(e, 1), E * n:E * n + E].rearrange("p e f -> p (e f)")
                    m = nc.tensor.matmul(ps[:, 6, 0:E], hidt[c % 2][:, T * n:T * n + T], w,
                                         start=(n == 0), stop=(n == FC - 1))
                m.then_inc(s_dn, 1)

            pe.wait_ge(s_wts, 48)
            pe.wait_ge(s_table, 1)

            def pe_tile(k, c, head=False, tail=0):
                if tail < 1:
                    column(k + 1, (c + 1) % 4)
                if tail < 2:
                    up(k, c)
                if not (head and k < 1) and tail < 3:
                    turn(k - 1, (c + 3) % 4)
                if not (head and k < 2):
                    down(k - 2, (c + 2) % 4)

            column(0, 0)
            for k in range(4):
                pe_tile(k, k, head=True)
            with pe.Fori(4, TILES - 4, 4) as t:
                for c in range(4):
                    pe_tile(t + c, c)
            for k in range(TILES - 4, TILES + 2):
                pe_tile(k, k % 4, tail=max(0, k - TILES + 2))

        @block.scalar
        def _(act):
            for q in range(8):
                act.wait_ge(s_gyp, q + 1)
                nc.scalar.activation(gy[:, 512 * q:512 * q + 512], ps[0:NV, q, :], ACT.Copy).then_inc(s_gy, 1)
            for q in range(8):
                act.wait_ge(s_thp, q + 1)
                nc.scalar.activation(thf[:, 4 * q:4 * q + 4, :],
                                     ps[:, q, :].rearrange("p (b j) -> p b j", j=T), ACT.Copy).then_inc(s_thf, 1)
            act.wait_ge(s_gap, 1)
            act.wait_ge(s_pad, 1)
            act.wait_ge(s_th[0], 64)
            nc.scalar.activation(TAS[:, 0:STEPS, 0:1], M[:, 0:STEPS, 0:1], ACT.Identity, bias=gap[:, 0:1],
                                 scale=0.0).then_inc(s_tas, 1)
            for c in range(BLKS):
                act.wait_ge(s_th[c], 64)
                r = slice(c * ROWS, (c + 1) * ROWS)
                nc.scalar.activation(TAS[:, r, 1:H], TH[:, r, 0:H - 1], ACT.Identity,
                                     bias=gap[:, 0:1]).then_inc(s_tas, 1)
            for i in range(BLKS):
                for g in range(NG):
                    r = slice(GR * g, GR * g + GR)
                    act.wait_ge(s_diff, i * (2 * NG) + 2 * g + 1)
                    nc.scalar.activation(C3[:, r, 0, :], C3[:, r, 0, :], ACT.Exp).then_inc(s_coef, 1)
                    act.wait_ge(s_diff, i * (2 * NG) + 2 * g + 2)
                    nc.scalar.activation(C3[:, r, 1:3, :], C3[:, r, 1:3, :], ACT.Exp,
                                         bias=gap[:, 0:1]).then_inc(s_coef, 1)
                act.wait_ge(s_lin, i * (4 * ROWS) + 4 * ROWS - 1)
                nc.scalar.activation(lrow[:, :], cells(X, i * ROWS + ROWS, 0, H + 1), ACT.Ln).then_inc(s_lnrow, 1)
                act.wait_ge(s_ren, i * 2 + 4)
                if i: act.wait_ge(s_lst, i * 64)
                nc.scalar.activation(LNX[:, :, :], X[:, bass.ds(i * ROWS + 1, ROWS), :], ACT.Ln).then_inc(s_lnx, 1)
            def root(k, n):
                act.wait_ge(s_var, k)
                nc.scalar.activation(lnv[:, 0:n, :], var[:, 0:n, :], ACT.Ln).then_inc(s_lnv, 1)
                act.wait_ge(s_lnv, k)
                nc.scalar.activation(r1[:, 0:n, :], lnv[:, 0:n, :], ACT.Exp, scale=-0.5).then_inc(s_root, 1)

            for q in range(NQ):
                b = slice(4 * q, 4 * q + 4)
                r = q % 2
                act.wait_ge(s_e2, q + 1)
                nc.scalar.activation(h0[:, b, :], h0[:, b, :], ACT.Exp).then_inc(s_h0, 1)
                root(2 * q + 1, 2)
                act.wait_ge(s_xntp, q + 1)
                nc.scalar.activation(xnt[r], ps[:, 0, :], ACT.Copy).then_inc(s_xnt, 1)
                act.wait_ge(s_vp, q + 1)
                nc.scalar.activation(va[r][:, :, :, 0:HD], ps[:, 1, :].rearrange("p (b h d) -> p b h d", h=NH, d=HD),
                                     ACT.Copy).then_inc(s_va, 1)
                for n in range(4 * q, 4 * q + 4):
                    act.wait_ge(s_d, n + 1)
                    act.wait_ge(s_mn, n + 1)
                    need(act, s_ptp, n - 1)
                    nc.scalar.activation(sq[n % 2], ps[:, 3:5, :].rearrange("p a n -> p (a n)"),
                                         ACT.Square).then_inc(s_sq, 1)
                    act.wait_ge(s_sub, n + 1)
                    nc.scalar.activation(sq[n % 2], sq[n % 2], ACT.Exp, scale=-1.0 / HD ** 0.5).then_inc(s_p, 1)
                    act.wait_ge(s_ptp, n + 1)
                    need(act, s_o, n - 1)
                    nc.scalar.activation(pt[n % 2][:, 0:512], ps[:, 5, :], ACT.Copy).then_inc(s_pta, 1)
                act.wait_ge(s_ontp, q + 1)
                nc.scalar.activation(ont[r], ps[:, 0, :], ACT.Copy).then_inc(s_ont, 1)
                root(2 * q + 2, 1)
                act.wait_ge(s_x3tp, q + 1)
                nc.scalar.activation(x3t, ps[:, 0, :], ACT.Copy).then_inc(s_x3t, 1)
                act.wait_ge(s_df, q + 1)
                nc.scalar.activation(gate[:, 1, :], gate[:, 0, :], ACT.Exp).then_inc(s_ex, 1)

            def columns(k, c):
                act.wait_ge(s_xcp, k + 1)
                if not (isinstance(k, int) and k < 2):
                    act.wait_ge(s_up, 2 * k - 2)
                nc.scalar.activation(xcol[c % 2], ps[:, 0, 0:T], ACT.Copy).then_inc(s_xc, 1)

            def silu(k, c):
                act.wait_ge(s_up, 2 * k + 1)
                if not (isinstance(k, int) and k < 2):
                    act.wait_ge(s_hid, k - 1)
                nc.scalar.activation(act_up[c % 2], ps[:, 1 + c % 2, :], ACT.Silu).then_inc(s_silu, 1)

            def gated(k, c):
                act.wait_ge(s_dn, k + 1)
                if not (isinstance(k, int) and k < 4):
                    act.wait_ge(s_ys[c], round_of(k, c) - 16)
                nc.scalar.activation(yrow[c], ps[:, 6, 0:E], ACT.Copy, scale=xrow[c][:, E + 1:ROW]).then_inc(s_y, 1)

            def act_tile(k, c, head=False, tail=0):
                if tail < 1:
                    columns(k + 1, (c + 1) % 4)
                if tail < 2:
                    silu(k, c)
                if not (head and k < 2):
                    gated(k - 2, (c + 2) % 4)

            columns(0, 0)
            for k in range(4):
                act_tile(k, k, head=True)
            with act.Fori(4, TILES - 4, 4) as t:
                for c in range(4):
                    act_tile(t + c, c)
            for k in range(TILES - 4, TILES + 2):
                act_tile(k, k % 4, tail=max(0, k - TILES + 2))

        @block.gpsimd
        def _(pool):
            pool.memset(M[:, :, 0:1], NEG)
            pool.memset(x0row[:], X0)
            pool.memset(padt[:], 0.0).then_inc(s_pad0, 1)
            pool.wait_ge(s_pad0, 1)
            pool.memset(padt[:, E:E + 1], float(2 * NB * T)).then_inc(s_pad0, 1)
            pool.iota(tili[:, 3, 0:TILES], [[1, TILES]], base=0, channel_multiplier=0)
            pool.memset(ones_sb[:], 1.0).then_inc(s_consts, 1)
            pool.iota(tokid[:], [[NB * T, 2], [T, NB]], base=0, channel_multiplier=1).then_inc(s_consts, 1)
            pool.memset(M[:, 0, 1:H + 1], NEG)
            pool.wait_ge(s_thp, 8)
            pool.wait_ge(s_thd, 16 * 16)
            pool.memset(X[:, :, 0:1], X0)
            pool.memset(X[:, 0, 1:H + 1], X0).then_inc(s_init, 1)
            pool.wait_ge(s_init, 1)
            pool.memset(M[0:64, 0, 0:1], 0.0).then_inc(s_init, 1)
            pool.wait_ge(s_thr, 8)
            pool.wait_ge(s_thp, 8)
            pool.wait_ge(s_cnt, 2)
            pool.memset(TH[64:128, 0, :], NEG)
            pool.memset(TH[0:64, T:STEPS, :], 0.0)
            pool.memset(TH[64:128, T + 1:STEPS, :], 0.0).then_inc(s_pad, 1)
            for i in range(BLKS):
                for g in range(NG):
                    r = slice(GR * g, GR * g + GR)
                    n = N[:, r, :]
                    pool.wait_ge(s_gauge, i * (4 * ROWS) + (4 * GR * (g + 1) - 1))
                    pool.nop(nofuse=True)
                    pool.tensor_tensor(C3[:, r, 0:2, :], shifted(M, i * ROWS + GR * g, GR, 2),
                                       bass.AP(tensor=n.tensor, offset=n.offset,
                                               ap=[n.ap[0], [H, GR], [0, 2], [1, H]]),
                                       ALU.subtract).then_inc(s_diff, 1)
                    pool.tensor_tensor(C3[:, r, 2, :], M[:, bass.ds(i * ROWS + GR * g + 1, GR), 0:H], n,
                                       ALU.subtract).then_inc(s_diff, 1)
                pool.wait_ge(s_lnx, i + 1)
                pool.nop(nofuse=True)
                pool.tensor_tensor(LNX[:, :, :], LNX[:, :, :], M[:, bass.ds(i * ROWS + 1, ROWS), :],
                                   ALU.add).then_inc(s_l, 1)
            for r in range(2):
                pool.memset(va[r][:, :, :, HD:HD + 1], 1.0).then_inc(s_consts, 1)
            for q in range(NQ):
                b = slice(4 * q, 4 * q + 4)
                r = q % 2
                pool.wait_ge(s_ldq[q], 32)
                pool.tensor_tensor(h0[:, b, :], h0[:, b, :], thf[:, b, :], ALU.subtract).then_inc(s_e1, 1)
                pool.wait_ge(s_xn, q + 1)
                pool.tensor_tensor(h1[:, b, :], h0[:, b, :], x1[r], ALU.add).then_inc(s_hx, 1)
                for n in range(4 * q, 4 * q + 4):
                    m = mn[:, n % 2, :]
                    v = sq[n % 2].rearrange("p (h s) -> p h s", s=T)
                    pool.wait_ge(s_sq, n + 1)
                    pool.tensor_tensor(v, v, bass.AP(tensor=m.tensor, offset=m.offset,
                                                     ap=[m.ap[0], [1, NH], [0, T]]), ALU.subtract).then_inc(s_sub, 1)
                pool.wait_ge(s_x3, q + 1)
                for k in range(8):
                    need(pool, s_sc[k], 16 * q)
                pool.tensor_copy(pay[:, :, 1, 0:E], pay[:, :, 0, 0:E]).then_inc(s_x3c, 1)
                pool.wait_ge(s_slot, q + 1)
                pool.wait_ge(s_x3c, q + 1)
                pool.wait_ge(s_pay, q + 1)
                for k in range(4):
                    for j in range(2):
                        pool.indirect_dma_start(xd_dram, bass.IndirectOffsetOnAxis(slot[:, q, j, k:k + 1], 0),
                                                pay[:, k, j, :], None).then_inc(s_sc[2 * k + j], 16)
            for k in range(8):
                pool.wait_ge(s_sc[k], 16 * NQ)

            def scatter(k, c):
                pool.wait_ge(s_dest, k + 1)
                pool.wait_ge(s_y, k + 1)
                pool.nop(nofuse=True)
                pool.indirect_dma_start(y_dram, bass.IndirectOffsetOnAxis(dest[:, c:c + 1], 0), yrow[c], None,
                                        bounds_check=2 * NB * T - 1, oob_is_err=False).then_inc(s_ys[c], 16)

            with pool.Fori(0, TILES, 4) as t:
                for c in range(4):
                    scatter(t + c, c)

        @block.vector
        def _(dve):
            dve.wait_ge(s_tok, 16)
            dve.wait_ge(s_in, 16 * 6)
            for k in range(2):
                r = slice(k * NB * T, (k + 1) * NB * T)
                nc.vector.tensor_scalar(oh[:, r], toki[:, r], iota_sb[:, 0:1], None, ALU.is_equal).then_inc(s_oh, 1)
            dve.wait_ge(s_small, 1)
            nc.vector.tensor_scalar(zt[:], ps[:, 0, 0:NV], bproj_sb[:, 0:1], None, ALU.add).then_inc(s_smallv, 1)
            dve.wait_ge(s_small, 2)
            nc.vector.tensor_copy(uv[:], ps[0:NV, 2, 0:2])
            nc.vector.tensor_copy(gm[:], ps[0:NV, 1, 0:NV]).then_inc(s_smallv, 1)
            dve.wait_ge(s_oh, 2)
            for k in range(2):
                r = slice(k * NB * T, (k + 1) * NB * T)
                nc.vector.reduce_sum(cnt[:, k, 0, :], oh[:, r].rearrange("p (b i) -> p b i", i=T),
                                     AX.X).then_inc(s_cnt, 1)
            dve.wait_ge(s_cnt, 2)
            for k in range(1, 4):
                m = nc.vector.tensor_copy(cnt[:, :, k, :], cnt[:, :, 0, :])
            m.then_inc(s_cnt, 1)
            for q in range(8):
                dve.wait_ge(s_thf, q + 1)
                nc.vector.tensor_copy(thr[:, 4 * q:4 * q + 4, :],
                                      ps[:, q, :].rearrange("p (b j) -> p b j", j=T)[:, :, ::-1]).then_inc(s_thr, 1)
            dve.wait_ge(s_small, 3)
            nc.vector.tensor_scalar(gap[:], ps[:, 0, 0:1], 1.0 / T, bgap_sb[:, 0:1], ALU.mult, ALU.add).then_inc(s_gap, 1)
            dve.wait_ge(s_gap, 1)
            dve.wait_ge(s_init, 2)
            dve.wait_ge(s_tas, 1 + BLKS)
            dve.engine_nop().then_inc(s_ren, 1)
            dve.engine_nop().then_inc(s_ren, 1)

            def row(t, s):
                return cells(t, s, 1, H + 1)

            for i in range(BLKS):
                def gauge(k):
                    s = i * ROWS + k
                    done = i * (4 * ROWS) + 4 * k
                    c = C[:, k % 2, :]

                    def best_from_above():
                        if k == 0:
                            dve.wait_ge(s_ren, i * 2 + 2)
                        else:
                            dve.wait_ge(s_gauge, done - 1)
                        nc.vector.scalar_tensor_tensor(c, row(M, s), gap[:, 0:1], cells(M, s, 0, H),
                                                       ALU.add, ALU.max).then_inc(s_gauge, 1)

                    def best_of_row():
                        dve.wait_ge(s_gauge, done + 1)
                        nc.vector.tensor_tensor_scan(N[:, k, :], cells(TAS, s, 0, H), c,
                                                     cells(M, s + 1, 0, 1), ALU.add,
                                                     ALU.max).then_inc(s_gauge, 1)

                    def add_theta():
                        dve.wait_ge(s_gauge, done + 2)
                        nc.vector.tensor_tensor(row(M, s + 1), N[:, k, :], cells(TH, s, 0, H),
                                                ALU.add).then_inc(s_gauge, 1)

                    def to_right_half():
                        if k < ROWS - 1:
                            dve.wait_ge(s_gauge, done + 3)
                            nc.vector.tensor_copy(M[64:128, bass.ds(s + 2, 1), 0:1],
                                                  M[0:64, bass.ds(s + 1, 1), H:H + 1]).then_inc(s_gauge, 1)
                    return [best_from_above, best_of_row, add_theta, to_right_half]

                def linear(k):
                    s = i * ROWS + k
                    done = i * (4 * ROWS) + 4 * k

                    def weigh():
                        if k % GR == 0:
                            dve.wait_ge(s_coef, i * (2 * NG) + 2 * (k // GR) + 2)
                        if k == 0:
                            dve.wait_ge(s_ren, i * 2 + 2)
                        else:
                            dve.wait_ge(s_lin, done - 1)
                        x = shifted(X, s, 1, 2)
                        x = bass.AP(tensor=x.tensor, offset=x.offset, ap=[x.ap[0], x.ap[2], x.ap[3]])
                        nc.vector.tensor_tensor(U[:, k % 2], x, C3[:, k, 0:2, :], ALU.mult).then_inc(s_lin, 1)

                    def add():
                        dve.wait_ge(s_lin, done + 1)
                        nc.vector.tensor_tensor(V[:, k % 2, :], U[:, k % 2, 0, :], U[:, k % 2, 1, :],
                                                ALU.add).then_inc(s_lin, 1)

                    def scan():
                        dve.wait_ge(s_lin, done + 2)
                        nc.vector.tensor_tensor_scan(row(X, s + 1), C3[:, k, 2, :], V[:, k % 2, :],
                                                     cells(X, s + 1, 0, 1), ALU.mult,
                                                     ALU.add).then_inc(s_lin, 1)

                    def to_right_half():
                        if k < ROWS - 1:
                            dve.wait_ge(s_lin, done + 3)
                            nc.vector.tensor_copy(X[64:128, bass.ds(s + 2, 1), 0:1],
                                                  X[0:64, bass.ds(s + 1, 1), H:H + 1]).then_inc(s_lin, 1)
                    return [weigh, add, scan, to_right_half]

                LAG = 4
                for k in range(ROWS + LAG):
                    a = gauge(k) if k < ROWS else []
                    b = linear(k - LAG) if k >= LAG else []
                    for n in range(4):
                        if a:
                            a[n]()
                        if b:
                            b[n]()
                last = i * ROWS + ROWS
                dve.wait_ge(s_lnrow, i + 1)
                nc.vector.scalar_tensor_tensor(cells(M, last, 0, H + 1), lrow[:, :], LNX0,
                                               cells(M, last, 0, H + 1), ALU.add, ALU.add).then_inc(s_gauge, 1)
                nc.vector.tensor_copy(cells(X, last, 0, H + 1), x0row[:]).then_inc(s_lin, 1)
                dve.wait_ge(s_gauge, i * (4 * ROWS) + 4 * ROWS)
                dve.wait_ge(s_lin, i * (4 * ROWS) + 4 * ROWS)
                nxt = last + 1
                nc.vector.tensor_copy(M[64:128, bass.ds(nxt, 1), 0:1], M[0:64, bass.ds(last, 1), H:H + 1]).then_inc(s_ren, 1)
                nc.vector.tensor_copy(X[64:128, bass.ds(nxt, 1), 0:1], X[0:64, bass.ds(last, 1), H:H + 1]).then_inc(s_ren, 1)
            chain = [0]

            def link(ins):
                chain[0] += 1
                ins.then_inc(s_dv, 1)
                dve.wait_ge(s_dv, chain[0])

            def over(a, n, outer=True):
                return bass.AP(tensor=a.tensor, offset=a.offset, ap=[a.ap[0], a.ap[1], [0, n]])

            def each(a, n):
                return bass.AP(tensor=a.tensor, offset=a.offset, ap=[a.ap[0], [0, n], a.ap[1]])

            dve.wait_ge(s_const, 16 * 12)
            dve.wait_ge(s_consts, 4)
            nc.vector.tensor_copy(tokf[:], tokid[:])
            link(nc.vector.tensor_copy(run[:, 0, :], region_sb[:]))
            dve.wait_ge(s_v, 16)
            link(nc.vector.tensor_scalar(nvt[:], vtot[:], -1.0, LNX0, ALU.mult, ALU.add))
            V_ = nc.vector

            def posterior(q):
                dve.wait_ge(s_e1, q + 1)
                for b in range(4 * q, 4 * q + 4):
                    m = V_.scalar_tensor_tensor(h0[:, b, :], h0[:, b, :], nvt[:, b:b + 1], lb[:, b, ::-1],
                                                ALU.add, ALU.add)
                m.then_inc(s_e2, 1)

            def moments(src):
                for k in range(4):
                    m = V_.bn_stats(st6[:, k, :], src(k))
                link(m)
                for k in range(4):
                    m = V_.bn_aggr(mv[:, k, :], st6[:, k, :])
                link(m)
                link(V_.tensor_scalar(var[:, 0, :], mv[:, :, 1], EPS, None, ALU.add))

            rounds = [0]

            def inverse_roots(n):
                y, r, t = var[:, 0:n, :], r1[:, 0:n, :], nwt[:, 0:n, :]
                rounds[0] += 1
                dve.wait_ge(s_root, rounds[0])
                link(V_.tensor_tensor(t, r, r, ALU.mult))
                link(V_.tensor_tensor(t, t, y, ALU.mult))
                link(V_.tensor_scalar(t, t, -0.5, 1.5, ALU.mult, ALU.add))
                link(V_.tensor_tensor(r, r, t, ALU.mult))

            def norms(q):
                r = q % 2
                dve.wait_ge(s_h0, q + 1)
                moments(lambda k: h0[:, 4 * q + k, :])
                V_.scalar_tensor_tensor(var[:, 1, :], var[:, 0, :], EPS, mv[:, :, 1], ALU.mult,
                                        ALU.add).then_inc(s_var, 1)
                inverse_roots(2)
                need(dve, s_hx, q - 1)
                need(dve, s_xntp, q - 1)
                for k in range(4):
                    m = V_.tensor_scalar(x1[r][:, k, :], h0[:, 4 * q + k, :], mv[:, k, 0:1], r1[:, 0, k:k + 1],
                                         ALU.subtract, ALU.mult)
                for k in range(4):
                    m = V_.tensor_scalar(xn[r][:, k, :], h0[:, 4 * q + k, :], mv[:, k, 0:1], r1[:, 1, k:k + 1],
                                         ALU.subtract, ALU.mult)
                m.then_inc(s_xn, 1)

            def queries_keys(q):
                r = q % 2
                dve.wait_ge(s_qkp, q + 1)
                V_.tensor_scalar(qs[r][:], ps[:, 2, 0:T], sc_sb[:, 0:1], None, ALU.add)
                a, w = ps[:, 2, T:2 * T], mask_sb[:]
                V_.scalar_tensor_tensor(kx[r].rearrange("p (h s) -> p h s", s=T), each(a, NH), mc_sb[:, 0:1],
                                        over(w, T), ALU.add, ALU.mult).then_inc(s_qk, 1)

            def nearest(n):
                dve.wait_ge(s_d, n + 1)
                need(dve, s_sub, n - 1)
                link(V_.tensor_reduce(rc[:, n % 2, :], ps[:, 3:5, :].rearrange("p a (h s) -> p (a h) s", s=T),
                                      AX.X, ALU.min, apply_absolute_value=True))
                V_.tensor_tensor(mn[:, n % 2, :], rc[:, n % 2, :], rc[:, n % 2, :], ALU.mult).then_inc(s_mn, 1)

            def evacuate(n):
                dve.wait_ge(s_ptp, n + 1)
                need(dve, s_o, n - 1)
                V_.tensor_copy(pt[n % 2][:, 512:1024], ps[:, 6, :]).then_inc(s_ptd, 1)

            def normalise(n):
                q, k = n // 4, n % 4
                dve.wait_ge(s_o, n + 1)
                need(dve, s_ontp, q - 1)
                o = ps[:, 7, 0:NH * (HD + 1)].rearrange("p (h d) -> p h d", d=HD + 1)
                link(V_.reciprocal(rc[:, n % 2, :], o[:, :, HD]))
                V_.tensor_tensor(on[q % 2][:, k, :].rearrange("p (h d) -> p h d", d=HD), o[:, :, 0:HD],
                                 over(rc[:, n % 2, :], HD), ALU.mult).then_inc(s_on, 1)

            def residual(q):
                dve.wait_ge(s_rp, q + 1)
                dve.wait_ge(s_hx, q + 1)
                b = slice(4 * q, 4 * q + 4)
                V_.tensor_tensor(h1[:, b, :], h1[:, b, :], ps[:, 1, :].rearrange("p (b j) -> p b j", j=T),
                                 ALU.add).then_inc(s_h1, 1)
                dve.wait_ge(s_h1, q + 1)
                moments(lambda k: h1[:, 4 * q + k, :])
                V_.engine_nop().then_inc(s_var, 1)
                inverse_roots(1)
                for k in range(8):
                    need(dve, s_sc[k], 16 * q)
                for k in range(4):
                    m = V_.tensor_scalar(pay[:, k, 0, 0:E], h1[:, 4 * q + k, :], mv[:, k, 0:1], r1[:, 0, k:k + 1],
                                         ALU.subtract, ALU.mult)
                m.then_inc(s_x3, 1)

            def pick(src, k):
                link(V_.tensor_reduce(top[:, k, :], src, AX.X, ALU.max))
                link(V_.tensor_tensor(eq[:], src, over(top[:, k, :], NX), ALU.is_equal))
                link(V_.tensor_tensor(eq[:], eq[:], each(rank8_sb[:], 4), ALU.mult))
                link(V_.tensor_reduce(first[:], eq[:], AX.X, ALU.max))
                link(V_.tensor_tensor(ohk[:, k], each(rank8_sb[:], 4), over(first[:], NX), ALU.is_equal))

            def routing(q):
                dve.wait_ge(s_lgp, q + 1)
                link(V_.tensor_copy(lg[:], ps[:, 2, 256:288].rearrange("p (b e) -> p b e", e=NX)))
                pick(lg[:], 0)
                link(V_.scalar_tensor_tensor(lg2[:], ohk[:, 0], -1e30, lg[:], ALU.mult, ALU.add))
                pick(lg2[:], 1)
                V_.tensor_tensor(gate[:, 0, :], top[:, 1, :], top[:, 0, :], ALU.subtract).then_inc(s_df, 1)
                V_.tensor_tensor(msk[:], ohk[:, 0], ohk[:, 1], ALU.add).then_inc(s_msk, 1)
                dve.wait_ge(s_rkp, q + 1)
                for k in range(4):
                    link(V_.tensor_tensor(run[:, 4 * q + k + 1, :], run[:, 4 * q + k, :],
                                          ps[:, 2, 352 + NX * k:360 + NX * k], ALU.add))
                link(V_.tensor_tensor(rank[:], run[:, 4 * q:4 * q + 4, :],
                                      ps[:, 2, 320:352].rearrange("p (b e) -> p b e", e=NX), ALU.add))
                for k in range(2):
                    link(V_.tensor_tensor(ohk[:, k], ohk[:, k], rank[:], ALU.mult))
                link(V_.tensor_reduce(slotf[:], ohk[:], AX.X, ALU.add))
                V_.tensor_copy(slot[:, q], slotf[:]).then_inc(s_slot, 1)
                dve.wait_ge(s_ex, q + 1)
                link(V_.tensor_scalar(gate[:, 0, :], gate[:, 1, :], 1.0, None, ALU.add))
                link(V_.reciprocal(top[:, 0, :], gate[:, 0, :]))
                link(V_.tensor_tensor(top[:, 1, :], top[:, 0, :], gate[:, 1, :], ALU.mult))
                for j in range(2):
                    V_.tensor_copy(pay[:, :, j, E:E + 1].rearrange("p b o -> p (b o)"), tokf[:, j, 4 * q:4 * q + 4])
                    m = V_.tensor_copy(pay[:, :, j, E + 1:ROW].rearrange("p b o -> p (b o)"), top[:, j, :])
                m.then_inc(s_pay, 1)

            for q in range(NQ):
                posterior(q)
                norms(q)
                queries_keys(q)
                for n in range(4 * q, 4 * q + 4):
                    nearest(n)
                    evacuate(n)
                    normalise(n)
                residual(q)
                routing(q)
            counts, tiles, ends, jump = (tl[:, k, :] for k in range(4))
            link(V_.tensor_tensor(counts, run[:, NB, :], region_sb[:], ALU.subtract))
            V_.tensor_copy(tili[:, 2, 0:NX], run[:, NB, :])
            link(V_.tensor_scalar(tili[:, 2, NX:2 * NX], counts, 127.0, None, ALU.add))
            link(V_.tensor_single_scalar(tili[:, 2, 2 * NX:3 * NX], tili[:, 2, NX:2 * NX], 7, ALU.arith_shift_right))
            link(V_.tensor_copy(tiles, tili[:, 2, 2 * NX:3 * NX]))
            link(V_.tensor_tensor_scan(ends, ones_sb[:, 0:NX], tiles, 0.0, ALU.mult, ALU.add))
            link(V_.tensor_scalar(jump, tiles, -1.0, float(REG // 128), ALU.mult, ALU.add))
            link(V_.tensor_copy(tilesf[:], tili[:, 3, 0:TILES]))
            link(V_.tensor_tensor(past[:], over(tilesf[:], NX), each(ends, TILES), ALU.is_ge))
            link(V_.tensor_reduce(tilf[:, 0, :], past[:, :, 0:NX - 1], AX.X, ALU.add))
            link(V_.tensor_tensor(past[:], past[:], each(jump, TILES), ALU.mult))
            link(V_.tensor_reduce(tilf[:, 1, :], past[:], AX.X, ALU.add))
            link(V_.tensor_tensor(tilf[:, 2, :], tilf[:, 1, :], tilesf[:], ALU.add))
            link(V_.tensor_scalar(tilf[:, 3, :], tilf[:, 2, :], 128.0, float(NX * REG), ALU.mult, ALU.min))
            V_.tensor_copy(tili[:, 1, 0:TILES], tilf[:, 0, :])
            V_.tensor_copy(tili[:, 0, 0:TILES], tilf[:, 3, :]).then_inc(s_table, 1)

            def hidden(k, c):
                dve.wait_ge(s_silu, k + 1)
                dve.wait_ge(s_up, 2 * k + 2)
                if not (isinstance(k, int) and k < 2):
                    dve.wait_ge(s_htp, k - 1)
                V_.tensor_tensor(hid[c % 2], act_up[c % 2], ps[:, 3 + c % 2, :], ALU.mult).then_inc(s_hid, 1)

            def turned(k, c):
                dve.wait_ge(s_htp, k + 1)
                if not (isinstance(k, int) and k < 2):
                    dve.wait_ge(s_dn, k - 1)
                V_.tensor_copy(hidt[c % 2], ps[:, 5 + 2 * (c % 2), :]).then_inc(s_ht, 1)

            def destination(k, c):
                dve.wait_ge(s_xr[c], round_of(k, c))
                if not (isinstance(k, int) and k < 4):
                    dve.wait_ge(s_ys[c], round_of(k, c) - 16)
                V_.tensor_copy(dest[:, c:c + 1], xrow[c][:, E:E + 1]).then_inc(s_dest, 1)

            def dve_tile(k, c, head=False, tail=0):
                if tail < 2:
                    hidden(k, c)
                    destination(k, c)
                if not (head and k < 1) and tail < 3:
                    turned(k - 1, (c + 3) % 4)

            for k in range(4):
                dve_tile(k, k, head=True)
            with dve.Fori(4, TILES - 4, 4) as t:
                for c in range(4):
                    dve_tile(t + c, c)
            for k in range(TILES - 4, TILES + 2):
                dve_tile(k, k % 4, tail=max(0, k - TILES + 2))
            for q in range(NQ):
                b = slice(4 * q, 4 * q + 4)
                dve.wait_ge(s_yl[q], 32)
                V_.tensor_tensor(h1[:, b, :], h1[:, b, :], lb[:, b, :], ALU.add).then_inc(s_fin, 1)
                dve.wait_ge(s_fin, 2 * q + 1)
                V_.tensor_tensor(h1[:, b, :], h1[:, b, :], h0[:, b, :], ALU.add).then_inc(s_fin, 1)


def kernel(**inputs):
    import numpy as np
    import concourse.bacc as bacc
    from concourse import mybir
    from concourse.bass_utils import run_bass_kernel_spmd as run

    nc = bacc.Bacc("TRN2", target_bir_lowering=False, num_devices=1)
    x = np.asarray(inputs["x"])
    y = np.asarray(inputs["itok_BS_0_21"])
    laid = {
        "tok": np.concatenate([x.reshape(-1), y.reshape(-1)]),
        "we_t": np.asarray(inputs["L0_tok_W_embed"]).T,
        "w_proj": np.asarray(inputs["L0_tok_W_proj"]),
        "b_proj": np.asarray(inputs["L0_tok_b_proj"]).reshape(-1, 1),
        "w_gap": np.asarray(inputs["L0_tok_W_gap"]).reshape(2, 128).T,
        "b_gap": np.broadcast_to(np.asarray(inputs["L0_tok_b_gap"]).reshape(1, 1), (128, 1)),
        "iota22": np.arange(22, dtype=np.float32).reshape(22, 1),
    }
    wq, wk, wv = (np.asarray(inputs["L0_attn_W" + c]) for c in "qkv")
    NH, HD = wq.shape
    wq_pl = np.zeros((4, 128, 128), wq.dtype)
    wk_pl = np.zeros((4, 128, 128), wk.dtype)
    wv_bd = np.zeros((128, 128), wv.dtype)
    for h in range(NH):
        r = slice(HD * h, HD * h + HD)
        for g in range(4):
            wq_pl[g, r, 32 * g + h] = wq[h]
            wk_pl[g, r, 32 * g + NH + h] = wk[h]
        wv_bd[r, r] = wv[h]
    p = np.arange(128)
    f = np.float32
    laid.update({
        "wq_pl": wq_pl, "wk_pl": wk_pl, "wv_bd": wv_bd,
        "w_m": np.asarray(inputs["L0_attn_Wm"]), "w_g": np.asarray(inputs["L0_ffn_Wg"]),
        "w_up": np.asarray(inputs["L0_ffn_W"]), "v_up": np.asarray(inputs["L0_ffn_V"]),
        "w_down": np.asarray(inputs["L0_ffn_W2"]),
        "eye": np.eye(128, dtype=f), "below": (p[:, None] < p[None, :]).astype(f),
        "head_mask": ((p[:, None] % 32 % NH == np.arange(NH)) & (p[:, None] % 32 < 2 * NH)).astype(f),
        "q_const": -((p % 32 >= NH) & (p % 32 < 2 * NH)).astype(f)[:, None],
        "k_const": (p % 32 < NH).astype(f)[:, None],
        "rank8": np.broadcast_to(8 - np.arange(8, dtype=f), (128, 8)),
        "region0": np.broadcast_to((32 * 128 + 128) * np.arange(8, dtype=f), (128, 8)),
    })
    arrays, args = {}, []
    for name, a in laid.items():
        a = np.ascontiguousarray(a)
        arrays["in_" + name] = a
        args.append(nc.dram_tensor("in_" + name, a.shape, mybir.dt.from_np(a.dtype), kind="ExternalInput").ap())
    args.append(nc.dram_tensor("out", (32, 128, 128), mybir.dt.float32, kind="ExternalOutput").ap())
    tower(nc, *args)
    r = run(nc, [arrays], core_ids=[0])
    return r.results[0]["out"]
```

```python
import concourse.bass as bass
from concourse import mybir
from contextlib import ExitStack


def tower(nc, tok_x, tok_y, we_t, w_proj, b_proj, w_gap, b_gap, iota66, wqk_pl, wv_bd, w_m, w_g, w_up, v_up, w_down,
          eye, below, head_mask, row_consts, rank8, region0, out):
    f32 = mybir.dt.float32
    i32 = mybir.dt.int32
    ALU = mybir.AluOpType
    ACT = mybir.ActivationFunctionType
    AX = mybir.AxisListType

    NB, T, E = 32, 128, 128
    NV = we_t.shape[1]
    H = T // 2
    ROWS = 26
    BLKS = 5
    STEPS = ROWS * BLKS
    GR = 2
    NG = ROWS // GR
    NEG = -100000000.0
    X0 = 2.0 ** -60
    LNX0 = 60.0 * 0.6931471805599453

    ctx = ExitStack()
    with ctx:
        def sb(name, shape, dt=f32):
            return ctx.enter_context(nc.sbuf_tensor(name, shape, dt))

        def pb(name, shape, dt=f32):
            return ctx.enter_context(nc.psum_tensor(name, shape, dt))

        def sem(name):
            return ctx.enter_context(nc.semaphore(name))

        th_dram = nc.dram_tensor("th_dram", (2, NB, T, T), f32).ap()
        l_dram = nc.dram_tensor("l_dram", (2, NB, T, T), f32).ap()

        v_dram = nc.dram_tensor("v_dram", (NB,), f32).ap()
        REG = NB * T + 128
        NX, F = 8, 512
        FC = F // 128
        NH, HD = 8, 16
        NQ = NB // 4
        TILES = 2 * NB * T // 128 + NX
        ROW = E + 2
        EPS = 1e-5
        xd_dram = nc.dram_tensor("xd_dram", (NX * REG + 128, ROW), f32).ap()
        y_dram = nc.dram_tensor("y_dram", (2 * NB * T, E), f32).ap()
        fr, bf16 = mybir.dt.float32r, mybir.dt.bfloat16
        V3 = 3 * NV

        wet_sb = sb("wet_sb", [E, NV])
        wproj_sb = sb("wproj_sb", [E, E])
        bproj_sb = sb("bproj_sb", [E, 1])
        wgap_sb = sb("wgap_sb", [E, 2])
        bgap_sb = sb("bgap_sb", [128, 1])
        iota_sb = sb("iota_sb", [V3, 1])
        gap = sb("gap", [128, 1])
        vtot = sb("vtot", [128, NB])
        nvt = sb("nvt", [128, NB])
        thf = sb("thf", [T, NB, T])
        h1 = thf
        wqk_hi = sb("wqk_hi", [E, 4, 128], fr)
        wqk_lo = sb("wqk_lo", [E, 4, 128], fr)
        wv_hi = sb("wv_hi", [E, E], fr)
        wv_lo = sb("wv_lo", [E, E], fr)
        wm_hi = sb("wm_hi", [E, E], fr)
        wm_lo = sb("wm_lo", [E, E], fr)
        wg_sb = sb("wg_sb", [E, NX])
        eye_sb = sb("eye_sb", [128, 128])
        below_sb = sb("below_sb", [128, 128], bf16)
        ones_sb = sb("ones_sb", [128, 128], bf16)
        mask_sb = sb("mask_sb", [128, NH])
        rowc_sb = sb("rowc_sb", [128, 5])
        rank8_sb = sb("rank8_sb", [128, NX])
        region_sb = sb("region_sb", [128, NX])
        run = sb("run", [128, NB + 1, NX])
        tokf = sb("tokf", [128, 2, NB])
        padt = sb("padt", [128, ROW])
        tili = sb("tili", [128, 4, TILES + 8], i32)
        tl = sb("tl", [128, 4, NX])
        ps = pb("ps", [128, 8, 512])

        align = ExitStack()

        def al(name, shape, dt=f32):
            return align.enter_context(nc.sbuf_tensor(name, shape, dt))

        M = al("M", [128, STEPS + 2, H + 1])
        X = al("X", [128, STEPS + 2, H + 1])
        C = al("C", [128, 2, H])
        N = al("N", [128, ROWS, H])
        first_use = ExitStack()
        toky = first_use.enter_context(nc.sbuf_tensor("toky", [NV, NB * T], i32))
        first_use.close()
        C3 = al("C3", [128, ROWS, 3, H])
        U = al("U", [128, 2, 2, H])
        V = al("V", [128, 2, H])
        LNX = al("LNX", [128, ROWS, H + 1])
        lrow = al("lrow", [128, H + 1])
        x0row = al("x0row", [128, H + 1])
        raw_qk = al("raw_qk", [E, 4, 128])
        raw_v = al("raw_v", [E, E])
        raw_m = al("raw_m", [E, E])
        raw_below = al("raw_below", [128, 128])
        tokid = al("tokid", [128, 2, NB], i32)
        zt = al("zt", [E, NV])
        gm = al("gm", [NV, NV])
        gpart = al("gpart", [NV, 3, NV], bf16)
        gleft = al("gleft", [NV, 2, NV])
        uv = al("uv", [NV, 2])
        cnt = al("cnt", [NV, 2, 4, NB])
        onehot = ExitStack()
        tokx = onehot.enter_context(nc.sbuf_tensor("tokx", [V3, NB * T], i32))
        ohx = onehot.enter_context(nc.sbuf_tensor("ohx", [V3, NB * T], bf16))
        ohy = onehot.enter_context(nc.sbuf_tensor("ohy", [NV, NB * T], bf16))
        gy = onehot.enter_context(nc.sbuf_tensor("gy", [V3, NB * T], bf16))
        onehot.enter_context(nc.sbuf_tensor("gap_to_thr", [128, 2 * STEPS * H - NB * T - 5 * NB * T // 2], f32))
        thr = onehot.enter_context(nc.sbuf_tensor("thr", [T, NB, T], f32))
        onehot.close()
        TH = al("TH", [128, STEPS, H])
        TAS = al("TAS", [128, STEPS, H])
        align.close()

        wup_hi, wup_lo, vup_hi, vup_lo, wdn_hi, wdn_lo = (
            sb(n, [128, NX, F], fr) for n in ("wup_hi", "wup_lo", "vup_hi", "vup_lo", "wdn_hi", "wdn_lo"))
        h0q = [sb(f"h0q{k}", [T, 4, T]) for k in range(3)]
        lbq = [sb(f"lbq{k}", [T, 4, T]) for k in range(2)]
        stage = [sb(f"stage{k}", [128, F]) for k in range(2)]
        x1 = [sb(f"x1{k}", [T, 4, T]) for k in range(2)]
        xn = [sb(f"xn{k}", [T, 4, T]) for k in range(1)]
        xnt_hi = [sb(f"xnt_hi{k}", [128, 512], fr) for k in range(2)]
        xnt_lo = [sb(f"xnt_lo{k}", [128, 512], fr) for k in range(2)]
        on = [sb(f"on{k}", [T, 4, T]) for k in range(2)]
        ont_hi = sb("ont_hi", [128, 512], fr)
        ont_lo = sb("ont_lo", [128, 512], fr)
        x3t = sb("x3t", [128, 512])
        sq = [sb(f"sq{k}", [128, 1024]) for k in range(4)]
        pt = [sb(f"pt{k}", [128, 1024]) for k in range(2)]
        qk_hi = sb("qk_hi", [128, 128], fr)
        qk_x = sb("qk_x", [128, 128])
        qk_k = sb("qk_k", [128, 128])
        qs = [sb(f"qs{k}", [128, 128], fr) for k in range(2)]
        kx = [sb(f"kx{k}", [128, 1024], fr) for k in range(2)]
        va = [sb(f"va{k}", [128, 4, NH, HD + 1]) for k in range(2)]
        pay = sb("pay", [128, 4, 2, ROW])
        st6 = sb("st6", [128, 4, 6])
        mv = sb("mv", [128, 2, 4, 2])
        r1 = sb("r1", [128, 2, 2, 4])
        var = sb("var", [128, 2, 2, 4])
        lnv = sb("lnv", [128, 2, 2, 4])
        nwt = sb("nwt", [128, 2, 4])
        mn = sb("mn", [128, 4, NH])
        rc = sb("rc", [128, 2, NH])
        lg = sb("lg", [128, 4, NX])
        lg2 = sb("lg2", [128, 4, NX])
        eq = sb("eq", [128, 4, NX])
        ohk = sb("ohk", [128, 2, 4, NX])
        msk = sb("msk", [128, 4, NX], bf16)
        top = sb("top", [128, 2, 4])
        first = sb("first", [128, 4])
        gate = sb("gate", [128, 2, 4])
        rank = sb("rank", [128, 4, NX])
        slotf = sb("slotf", [128, 2, 4])
        slot = sb("slot", [128, NQ, 2, 4], i32)
        tilesf = x1[0][:, :, :].rearrange("p b j -> p (b j)")[:, 0:TILES]
        tilf = x1[0][:, :, :].rearrange("p b j -> p (b j)")[:, TILES:5 * TILES].rearrange("p (a k) -> p a k", k=TILES)
        past = pt[0][:, 0:TILES * NX].rearrange("p (k e) -> p k e", e=NX)
        ones8 = x1[1][:, 0, 0:NX]
        xrow = [stage[k // 2][:, ROW * (k % 2):ROW * (k % 2) + ROW] for k in range(4)]
        yrow = [on[k // 4][:, k % 4, :] for k in range(4)]
        xcol_hi = [ont_hi[:, T * k:T * k + T] for k in range(2)]
        xcol_lo = [ont_lo[:, T * k:T * k + T] for k in range(2)]
        act_up = [sq[k][:, 0:F] for k in range(2)]
        hid = [sq[k + 2][:, 0:F] for k in range(2)]
        hidt_hi, hidt_lo = xnt_hi, xnt_lo
        dest = sb("dest", [128, 4], i32)
        rowgate = sb("rowgate", [128, 4])
        ya = [sq[q // 2][:, 512 * (q % 2):512 * (q % 2) + 512].rearrange("p (b j) -> p b j", j=T) for q in range(NQ)]
        yb = [t.rearrange("p (b j) -> p b j", j=T) if len(t.shape) == 2 else t for t in
              [pt[0][:, 0:512], pt[0][:, 512:1024], pt[1][:, 0:512], pt[1][:, 512:1024],
               h0q[0][:, :, :], h0q[1][:, :, :], h0q[2][:, :, :], lbq[0][:, :, :]]]

        s_in = sem("s_in")
        s_tok = sem("s_tok")
        s_oh = sem("s_oh")
        s_cnt = sem("s_cnt")
        s_small = sem("s_small")
        s_smallv = sem("s_smallv")
        s_gyp = sem("s_gyp")
        s_gy = sem("s_gy")
        s_thp = sem("s_thp")
        s_thf = sem("s_thf")
        s_thr = sem("s_thr")
        s_thd = sem("s_thd")
        s_th = [sem(f"s_th{c}") for c in range(BLKS)]
        s_pad = sem("s_pad")
        s_gap = sem("s_gap")
        s_tas = sem("s_tas")
        s_init = sem("s_init")
        s_gauge = sem("s_gauge")
        s_lin = sem("s_lin")
        s_diff = sem("s_diff")
        s_coef = sem("s_coef")
        s_lnrow = sem("s_lnrow")
        s_ren = sem("s_ren")
        s_lnx = sem("s_lnx")
        s_l = sem("s_l")
        s_lst = sem("s_lst")
        s_ld = sem("s_ld")
        s_vst = sem("s_vst")
        s_v = sem("s_v")
        s_nv = sem("s_nv")
        s_e1 = sem("s_e1")
        s_e2 = sem("s_e2")
        s_e3 = sem("s_e3")
        s_out = sem("s_out")
        s_ohy = sem("s_ohy")
        s_tokx = sem("s_tokx")
        s_thw = [sem(f"s_thw{c}") for c in range(BLKS)]
        s_addl = sem("s_addl")
        s_xntl = sem("s_xntl")
        s_ontl = sem("s_ontl")
        s_qkh = sem("s_qkh")
        s_stage = [sem(f"s_stage{k}") for k in range(2)]
        s_whi = sem("s_whi")
        s_wlo = sem("s_wlo")
        s_wraw = sem("s_wraw")
        s_sent = sem("s_sent")
        s_tokf = sem("s_tokf")
        s_lgx = sem("s_lgx")
        s_xcl = sem("s_xcl")
        s_htl = sem("s_htl")
        s_const = sem("s_const")
        s_consts = sem("s_consts")
        s_wts = sem("s_wts")
        s_ldq = [sem(f"s_ldq{q}") for q in range(NQ)]
        s_h0 = sem("s_h0")
        s_dv = sem("s_dv")
        s_xn = sem("s_xn")
        s_var = sem("s_var")
        s_lnv = sem("s_lnv")
        s_root = sem("s_root")
        s_hx = sem("s_hx")
        s_xntp = sem("s_xntp")
        s_xnt = sem("s_xnt")
        s_vp = sem("s_vp")
        s_va = sem("s_va")
        s_qkp = sem("s_qkp")
        s_qk = sem("s_qk")
        s_d = sem("s_d")
        s_sq = sem("s_sq")
        s_mn = sem("s_mn")
        s_sub = sem("s_sub")
        s_p = sem("s_p")
        s_ptp = sem("s_ptp")
        s_pta = sem("s_pta")
        s_ptd = sem("s_ptd")
        s_o = sem("s_o")
        s_on = sem("s_on")
        s_ontp = sem("s_ontp")
        s_ont = sem("s_ont")
        s_rp = sem("s_rp")
        s_h1 = sem("s_h1")
        s_x3 = sem("s_x3")
        s_x3c = sem("s_x3c")
        s_x3tp = sem("s_x3tp")
        s_x3t = sem("s_x3t")
        s_lgp = sem("s_lgp")
        s_df = sem("s_df")
        s_ex = sem("s_ex")
        s_msk = sem("s_msk")
        s_rkp = sem("s_rkp")
        s_slot = sem("s_slot")
        s_pay = sem("s_pay")
        s_pad0 = sem("s_pad0")
        s_table = sem("s_table")
        s_padw = sem("s_padw")
        s_xr = [sem(f"s_xr{k}") for k in range(4)]
        s_xc = sem("s_xc")
        s_xcp = sem("s_xcp")
        s_up = sem("s_up")
        s_silu = sem("s_silu")
        s_hid = sem("s_hid")
        s_htp = sem("s_htp")
        s_ht = sem("s_ht")
        s_dn = sem("s_dn")
        s_y = sem("s_y")
        s_dest = sem("s_dest")
        s_ys = [sem(f"s_ys{k}") for k in range(4)]
        s_yl = [sem(f"s_yl{q}") for q in range(NQ)]
        s_fin = sem("s_fin")
        s_sc = [sem(f"s_sc{k}") for k in range(8)]
        block = ctx.enter_context(nc.Block())

        def need(eng, s, n):
            if n > 0:
                eng.wait_ge(s, n)

        def shifted(t, row, rows, second):
            a = t[:, row:row + rows, 0:H]
            return bass.AP(tensor=a.tensor, offset=a.offset, ap=[a.ap[0], [H + 1, rows], [1, second], [1, H]])

        def cells(t, s, lo, hi):
            return t[:, s, lo:hi]

        def span(c, h):
            lo, hi = max(c * ROWS, h), min((c + 1) * ROWS, T + h)
            return lo, hi

        def lane_rows(t, d, h, lo, hi):
            a = t[d, :, lo - h:hi - h, :] if d == 0 else t[d, :, T - (hi - h):T - (lo - h), :][:, ::-1, :]
            return a[:, :, H * h:H * h + H]

        STEPS_OF_ATTENTION = range(-9, NB + 12)

        def pair(piece, n, ahead):
            if 0 <= n + ahead < NB:
                piece(n + ahead)

        def quad(piece, n, ahead):
            if (n + ahead) % 4 == 0 and 0 <= n + ahead < NB:
                piece((n + ahead) // 4)

        def pta(n):
            return n + (n + 1) // 2

        def ptd(n):
            return n // 2

        def at_tile(k):
            return slice(k, k + 1) if isinstance(k, int) else bass.ds(k, 1)

        def round_of(k, c):
            return 16 * (k // 4 + 1) if isinstance(k, int) else (k - c) * 4 + 16

        CHUNKS = 3 * NX

        @block.sync
        def _(sp):
            sp.dma_start(toky[:], tok_y.partition_broadcast(NV)).then_inc(s_tok, 16)
            sp.dma_start(tokx[:], tok_x.partition_broadcast(V3)).then_inc(s_tokx, 16)
            sp.wait_ge(s_thf, NQ)
            sp.wait_ge(s_thr, NQ)
            sp.wait_ge(s_cnt, 2)
            for c in range(BLKS):
                lo, hi = c * ROWS, min((c + 1) * ROWS, T)
                sp.dma_start(th_dram[0][:, lo:hi, :].rearrange("b i j -> i b j"), thf[lo:hi, :, :]).then_inc(s_thw[c], 16)
                sp.dma_start(th_dram[1][:, T - hi:T - lo, :].rearrange("b i j -> i b j"),
                             thr[T - hi:T - lo, :, :]).then_inc(s_thw[c], 16)
                sp.wait_ge(s_thw[c], 32)
                for h in range(2):
                    lo, hi = span(c, h)
                    for d in range(2):
                        lane = 64 * h + 32 * d
                        sp.dma_start(TH[lane:lane + 32, lo:hi, :],
                                     lane_rows(th_dram, d, h, lo, hi)).then_inc(s_th[c], 16)
            for c in range(BLKS):
                sp.wait_ge(s_l, c + 1)
                for h in range(2):
                    lo, hi = span(c, h)
                    for d in range(2):
                        lane = 64 * h + 32 * d
                        sp.dma_start(lane_rows(l_dram, d, h, lo, hi),
                                     LNX[lane:lane + 32, lo - c * ROWS:hi - c * ROWS, 1:H + 1]).then_inc(s_lst, 16)
            sp.dma_start(v_dram.rearrange("(b o) -> b o", o=1),
                         LNX[64:96, T - (BLKS - 1) * ROWS, H:H + 1]).then_inc(s_vst, 16)
            sp.wait_ge(s_vst, 16)
            sp.dma_start(vtot[:, :], v_dram.partition_broadcast(128)).then_inc(s_v, 16)
            sp.wait_ge(s_lst, 16 * 4 * BLKS)

            def load_quad(q):
                need(sp, s_hx, q - 2)
                need(sp, s_xn, q - 2)
                need(sp, s_e2, q - 1)
                b = slice(4 * q, 4 * q + 4)
                sp.dma_start(h0q[q % 3][:], l_dram[0, b].rearrange("b i j -> i b j")).then_inc(s_ldq[q], 16)
                sp.dma_start(lbq[q % 2][:], l_dram[1, b].rearrange("b i j -> i b j")).then_inc(s_ldq[q], 16)

            def load_weights(c):
                kind, e = c // NX, c % NX
                need(sp, s_whi, c - 1)
                need(sp, s_wlo, c - 1)
                if kind < 2:
                    sp.dma_start(stage[c % 2][:], (w_up, v_up)[kind][e]).then_inc(s_stage[c % 2], 16)
                else:
                    sp.dma_start(stage[c % 2][:].rearrange("p (c n) -> p c n", n=E),
                                 w_down[e].rearrange("(c p) n -> p c n", p=128)).then_inc(s_stage[c % 2], 16)

            load_quad(0)
            load_quad(1)
            for q in range(NQ):
                for c in range(3 * q, 3 * q + 3):
                    load_weights(c)
                if q + 2 < NQ:
                    load_quad(q + 2)
            sp.wait_ge(s_pad0, 2)
            sp.dma_start(xd_dram[NX * REG:NX * REG + 128, :], padt[:]).then_inc(s_padw, 16)
            sp.wait_ge(s_table, 1)
            for e in range(NX):
                row = sp.value_load(tili[0:1, 2, e:e + 1], min_val=0, max_val=NX * REG)
                sp.dma_start(xd_dram[bass.ds(row, 128), :], padt[:]).then_inc(s_padw, 16)
            for k in range(8):
                sp.wait_ge(s_sc[k], 16 * NQ)
            sp.wait_ge(s_padw, 16 * (NX + 1))
            sp.wait_ge(s_table, 1)
            sp.wait_ge(s_whi, CHUNKS)
            sp.wait_ge(s_wlo, CHUNKS)

            def load(k, c):
                row = sp.value_load(tili[0:1, 0, bass.ds(k, 1)] if not isinstance(k, int) else tili[0:1, 0, k:k + 1],
                                    min_val=0, max_val=NX * REG)
                if not (isinstance(k, int) and k < 4):
                    sp.wait_ge(s_xcp, k - 3)
                    sp.wait_ge(s_dest, k - 3)
                sp.dma_start(xrow[c], xd_dram[bass.ds(row, 128), :]).then_inc(s_xr[c], 16)

            for k in range(4):
                load(k, k)
            with sp.Fori(4, TILES, 4) as t:
                for c in range(4):
                    load(t + c, c)
            for c in range(4):
                sp.wait_ge(s_ys[c], 16 * (TILES // 4))
            for q in range(NQ):
                b = slice(4 * q, 4 * q + 4)
                y = y_dram.rearrange("(k b t) e -> k t b e", k=2, t=T)
                sp.dma_start(ya[q], y[0][:, b, :]).then_inc(s_yl[q], 16)
                sp.dma_start(yb[q], y[1][:, b, :]).then_inc(s_yl[q], 16)
            for q in range(NQ):
                b = slice(4 * q, 4 * q + 4)
                sp.wait_ge(s_fin, 2 * q + 2)
                sp.dma_start(out[b].rearrange("b i j -> i b j"), h1[:, b, :]).then_inc(s_out, 16)
            sp.wait_ge(s_out, 16 * NQ)

        @block.tensor
        def _(pe):
            def three(dst, a, b, first=True, last=True):
                nc.tensor.matmul(dst, a[0], b[0], start=first, stop=False)
                nc.tensor.matmul(dst, a[0], b[1], start=False, stop=False)
                return nc.tensor.matmul(dst, a[1], b[0], start=False, stop=last)

            pe.wait_ge(s_in, 16 * 6)
            nc.tensor.matmul(ps[:, 0, 0:NV], wproj_sb[:], wet_sb[:], start=True, stop=True).then_inc(s_small, 1)
            pe.wait_ge(s_smallv, 1)
            nc.tensor.matmul(ps[0:NV, 1, 0:NV], zt[:], zt[:], start=True, stop=True)
            nc.tensor.matmul(ps[0:NV, 2, 0:2], zt[:], wgap_sb[:], start=True, stop=True).then_inc(s_small, 1)
            pe.wait_ge(s_smallv, 2)
            pe.wait_ge(s_ohy, 1)
            for q in range(NQ):
                nc.tensor.matmul(ps[0:V3, q, :], gpart[:, :, :].rearrange("p k v -> p (k v)"), ohy[:, 512 * q:512 * q + 512],
                                 start=True, stop=True).then_inc(s_gyp, 1)
            pe.wait_ge(s_oh, 1)
            for q in range(NQ):
                pe.wait_ge(s_gy, q + 1)
                for k in range(4):
                    b = 4 * q + k
                    m = nc.tensor.matmul(ps[:, q, T * k:T * k + T], ohx[:, b * T:b * T + T], gy[:, b * T:b * T + T],
                                         start=True, stop=True)
                m.then_inc(s_thp, 1)
            pe.wait_ge(s_cnt, 3)
            pe.wait_ge(s_thf, 1)
            pe.wait_ge(s_thr, 1)
            nc.tensor.matmul(ps[:, 0, 0:1], cnt[:, 0].rearrange("p r b -> p (r b)"), uv[:, 0:1], start=True, stop=False)
            nc.tensor.matmul(ps[:, 0, 0:1], cnt[:, 1].rearrange("p r b -> p (r b)"), uv[:, 1:2],
                             start=False, stop=True).then_inc(s_small, 1)

            def turn_tokens(q):
                pe.wait_ge(s_xn, q + 1)
                need(pe, s_ont, q - 2)
                need(pe, s_ontl, q - 2)
                for k in range(4):
                    m = nc.tensor.transpose(ps[:, 0, T * k:T * k + T], xn[0][:, k, :], eye_sb[:])
                m.then_inc(s_xntp, 1)

            def project(q):
                r = q % 2
                pe.wait_ge(s_xnt, q + 1)
                pe.wait_ge(s_xntl, q + 1)
                need(pe, s_slot, q - 3)
                for k in range(4):
                    c = slice(T * k, T * k + T)
                    m = three(ps[:, 2, 0:T], (wqk_hi[:, k, :], wqk_lo[:, k, :]), (xnt_hi[r][:, c], xnt_lo[r][:, c]),
                              k == 0, k == 3)
                m.then_inc(s_qkp, 1)
                need(pe, s_h1, q - 2)
                for k in range(4):
                    c = slice(T * k, T * k + T)
                    m = three(ps[:, 1, c], (xnt_hi[r][:, c], xnt_lo[r][:, c]), (wv_hi[:], wv_lo[:]))
                m.then_inc(s_vp, 1)

            def distances(n):
                q, k = n // 4, n % 4
                g = slice(32 * k, 32 * k + 32)
                pe.wait_ge(s_qk, q + 1)
                need(pe, s_sq, n)
                need(pe, s_mn, n)
                for c in range(2):
                    m = nc.tensor.matmul(ps[:, 3 + c, :], qs[q % 2][g, :], kx[q % 2][g, 512 * c:512 * c + 512],
                                         start=True, stop=True)
                m.then_inc(s_d, 1)

            def turn_weights(n):
                pe.wait_ge(s_p, n + 1)
                need(pe, s_pta, pta(n))
                need(pe, s_ptd, ptd(n))
                for h in range(NH):
                    m = nc.tensor.transpose(ps[:, 5 + h // 4, T * (h % 4):T * (h % 4) + T],
                                            sq[n % 4][:, T * h:T * h + T], eye_sb[:])
                m.then_inc(s_ptp, 1)

            def attend(n):
                q, k = n // 4, n % 4
                need(pe, s_pta, pta(n + 1))
                need(pe, s_ptd, ptd(n + 1))
                pe.wait_ge(s_va, q + 1)
                need(pe, s_on, n)
                for h in range(NH):
                    m = nc.tensor.matmul(ps[:, 7, (HD + 1) * h:(HD + 1) * (h + 1)], pt[n % 2][:, T * h:T * h + T],
                                         va[q % 2][:, k, h, :], start=True, stop=True)
                m.then_inc(s_o, 1)

            def turn_heads(q):
                pe.wait_ge(s_on, 4 * q + 4)
                need(pe, s_x3t, q)
                for k in range(4):
                    m = nc.tensor.transpose(ps[:, 0, T * k:T * k + T], on[q % 2][:, k, :], eye_sb[:])
                m.then_inc(s_ontp, 1)

            def merge(q):
                pe.wait_ge(s_ont, q + 1)
                pe.wait_ge(s_ontl, q + 1)
                pe.wait_ge(s_va, min(q + 3, NQ))
                for k in range(4):
                    c = slice(T * k, T * k + T)
                    m = three(ps[:, 1, c], (ont_hi[:, c], ont_lo[:, c]), (wm_hi[:], wm_lo[:]))
                m.then_inc(s_rp, 1)

            def turn_inputs(q):
                pe.wait_ge(s_x3, q + 1)
                pe.wait_ge(s_xnt, min(q + 4, NQ))
                pe.wait_ge(s_xntl, min(q + 4, NQ))
                pe.wait_ge(s_ontl, q + 1)
                for k in range(4):
                    m = nc.tensor.transpose(ps[:, 0, T * k:T * k + T], pay[:, k, 0, 0:E], eye_sb[:])
                m.then_inc(s_x3tp, 1)

            def gate_logits(q):
                pe.wait_ge(s_x3t, q + 1)
                pe.wait_ge(s_qk, min(q + 4, NQ))
                for k in range(4):
                    m = nc.tensor.matmul(ps[:, 2, 256 + NX * k:256 + NX * k + NX], x3t[:, T * k:T * k + T], wg_sb[:],
                                         start=True, stop=True)
                m.then_inc(s_lgp, 1)

            def ranks(q):
                pe.wait_ge(s_msk, q + 1)
                nc.tensor.matmul(ps[:, 2, 320:352], below_sb[:], msk[:, :, :].rearrange("p b e -> p (b e)"),
                                 start=True, stop=True)
                nc.tensor.matmul(ps[:, 2, 352:384], ones_sb[:], msk[:, :, :].rearrange("p b e -> p (b e)"),
                                 start=True, stop=True).then_inc(s_rkp, 1)

            pe.wait_ge(s_const, 16 * 10)
            pe.wait_ge(s_consts, 5)
            for n in STEPS_OF_ATTENTION:
                pair(distances, n, 3)
                pair(turn_weights, n, 0)
                quad(turn_heads, n, -5)
                quad(turn_inputs, n, -8)
                quad(turn_tokens, n, 6)
                pair(attend, n, -1)
                quad(merge, n, -6)
                quad(project, n, 5)
                quad(gate_logits, n, -9)
                quad(ranks, n, -10)

            def column(k, c):
                pe.wait_ge(s_xr[c], round_of(k, c))
                if not (isinstance(k, int) and k < 1):
                    pe.wait_ge(s_xc, k)
                    pe.wait_ge(s_xcl, k)
                nc.tensor.transpose(ps[:, 0, 0:T], xrow[c][:, 0:E], eye_sb[:]).then_inc(s_xcp, 1)

            def up(k, c):
                e = pe.value_load(tili[0:1, 1, at_tile(k)], min_val=0, max_val=NX - 1)
                pe.wait_ge(s_xc, k + 1)
                pe.wait_ge(s_xcl, k + 1)
                if not (isinstance(k, int) and k < 2):
                    pe.wait_ge(s_hid, k - 1)
                for n, hi, lo in ((1, wup_hi, wup_lo), (3, vup_hi, vup_lo)):
                    m = three(ps[:, n + c % 2, :], (xcol_hi[c % 2], xcol_lo[c % 2]),
                              [w[:, bass.ds(e, 1), :].rearrange("p e f -> p (e f)") for w in (hi, lo)])
                    m.then_inc(s_up, 1)

            def turn(k, c):
                pe.wait_ge(s_hid, k + 1)
                if not (isinstance(k, int) and k < 2):
                    pe.wait_ge(s_ht, k - 1)
                    pe.wait_ge(s_htl, k - 1)
                for n in range(FC):
                    m = nc.tensor.transpose(ps[:, 5 + 2 * (c % 2), T * n:T * n + T], hid[c % 2][:, T * n:T * n + T],
                                            eye_sb[:])
                m.then_inc(s_htp, 1)

            def down(k, c):
                e = pe.value_load(tili[0:1, 1, at_tile(k)], min_val=0, max_val=NX - 1)
                pe.wait_ge(s_ht, k + 1)
                pe.wait_ge(s_htl, k + 1)
                if not (isinstance(k, int) and k < 1):
                    pe.wait_ge(s_y, k)
                for n in range(FC):
                    b = slice(T * n, T * n + T)
                    m = three(ps[:, 6, 0:E], (hidt_hi[c % 2][:, b], hidt_lo[c % 2][:, b]),
                              [w[:, bass.ds(e, 1), E * n:E * n + E].rearrange("p e f -> p (e f)")
                               for w in (wdn_hi, wdn_lo)], n == 0, n == FC - 1)
                m.then_inc(s_dn, 1)

            pe.wait_ge(s_whi, CHUNKS)
            pe.wait_ge(s_wlo, CHUNKS)
            pe.wait_ge(s_table, 1)

            def pe_tile(k, c, head=False, tail=0):
                if tail < 1:
                    column(k + 1, (c + 1) % 4)
                if tail < 2:
                    up(k, c)
                if not (head and k < 1) and tail < 3:
                    turn(k - 1, (c + 3) % 4)
                if not (head and k < 2):
                    down(k - 2, (c + 2) % 4)

            column(0, 0)
            for k in range(4):
                pe_tile(k, k, head=True)
            with pe.Fori(4, TILES - 4, 4) as t:
                for c in range(4):
                    pe_tile(t + c, c)
            for k in range(TILES - 4, TILES + 2):
                pe_tile(k, k % 4, tail=max(0, k - TILES + 2))

        @block.scalar
        def _(act):
            for dst, src in ((wet_sb[:], we_t), (wproj_sb[:], w_proj), (bproj_sb[:], b_proj),
                             (wgap_sb[:], w_gap), (bgap_sb[:], b_gap), (iota_sb[:], iota66)):
                act.dma_start(dst, src).then_inc(s_in, 16)
            for dst, src in ((raw_qk[:], wqk_pl.rearrange("g e c -> e g c")), (raw_v[:], wv_bd), (raw_m[:], w_m),
                             (wg_sb[:], w_g), (eye_sb[:], eye), (raw_below[:], below), (mask_sb[:], head_mask),
                             (rowc_sb[:], row_consts), (rank8_sb[:], rank8), (region_sb[:], region0)):
                act.dma_start(dst, src).then_inc(s_const, 16)
            for q in range(8):
                act.wait_ge(s_gyp, q + 1)
                nc.scalar.activation(gy[:, 512 * q:512 * q + 512], ps[0:V3, q, :], ACT.Copy).then_inc(s_gy, 1)
            for q in range(8):
                act.wait_ge(s_thp, q + 1)
                nc.scalar.activation(thf[:, 4 * q:4 * q + 4, :],
                                     ps[:, q, :].rearrange("p (b j) -> p b j", j=T), ACT.Copy).then_inc(s_thf, 1)
            act.wait_ge(s_const, 16 * 10)
            nc.scalar.activation(wqk_hi[:], raw_qk[:], ACT.Copy)
            nc.scalar.activation(wv_hi[:], raw_v[:], ACT.Copy)
            nc.scalar.activation(below_sb[:], raw_below[:], ACT.Copy)
            nc.scalar.activation(wm_hi[:], raw_m[:], ACT.Copy).then_inc(s_wraw, 1)
            act.wait_ge(s_gap, 1)
            act.wait_ge(s_pad, 1)
            act.wait_ge(s_cnt, 2)
            act.wait_ge(s_init, 1)

            def left_scores(c):
                act.wait_ge(s_th[c], 64)
                if c == 2:
                    for b in range(BLKS):
                        act.wait_ge(s_thw[b], 32)
                r = slice(c * ROWS, (c + 1) * ROWS)
                nc.scalar.activation(TAS[:, r, 0:1], M[:, r, 0:1], ACT.Identity, bias=gap[:, 0:1],
                                     scale=0.0).then_inc(s_tas, 1)
                nc.scalar.activation(TAS[:, r, 1:H], TH[:, r, 0:H - 1], ACT.Identity,
                                     bias=gap[:, 0:1]).then_inc(s_tas, 1)

            left_scores(0)
            left_scores(1)
            for i in range(BLKS):
                for g in range(NG):
                    r = slice(GR * g, GR * g + GR)
                    act.wait_ge(s_diff, i * (2 * NG) + 2 * g + 1)
                    nc.scalar.activation(C3[:, r, 0, :], C3[:, r, 0, :], ACT.Exp).then_inc(s_coef, 1)
                    act.wait_ge(s_diff, i * (2 * NG) + 2 * g + 2)
                    nc.scalar.activation(C3[:, r, 1:3, :], C3[:, r, 1:3, :], ACT.Exp,
                                         bias=gap[:, 0:1]).then_inc(s_coef, 1)
                act.wait_ge(s_lin, i * (4 * ROWS) + 4 * ROWS - 1)
                nc.scalar.activation(lrow[:, :], cells(X, i * ROWS + ROWS, 0, H + 1), ACT.Ln).then_inc(s_lnrow, 1)
                act.wait_ge(s_ren, i * 2 + 4)
                need(act, s_lst, i * 64)
                nc.scalar.activation(LNX[:, :, :], X[:, bass.ds(i * ROWS + 1, ROWS), :], ACT.Ln).then_inc(s_lnx, 1)
                if i + 2 < BLKS:
                    left_scores(i + 2)
            nc.scalar.preload_act_table_set("natural_log_exp_and_others")

            def root(k, c, n):
                act.wait_ge(s_var, k)
                nc.scalar.activation(lnv[:, c, 0:n, :], var[:, c, 0:n, :], ACT.Ln).then_inc(s_lnv, 1)
                act.wait_ge(s_lnv, k)
                nc.scalar.activation(r1[:, c, 0:n, :], lnv[:, c, 0:n, :], ACT.Exp, scale=-0.5).then_inc(s_root, 1)

            rounds = [0]

            def posterior(q):
                act.wait_ge(s_e2, q + 1)
                nc.scalar.activation(h0q[q % 3][:], h0q[q % 3][:], ACT.Exp).then_inc(s_h0, 1)

            def root_first(q):
                rounds[0] += 1
                root(rounds[0], 0, 2)

            def root_second(q):
                rounds[0] += 1
                root(rounds[0], 1, 1)

            def tokens_high(q):
                act.wait_ge(s_xntp, q + 1)
                need(act, s_vp, q - 1)
                nc.scalar.activation(xnt_hi[q % 2][:], ps[:, 0, :], ACT.Copy).then_inc(s_xnt, 1)

            def values(q):
                act.wait_ge(s_vp, q + 1)
                need(act, s_o, 4 * q - 4)
                nc.scalar.activation(va[q % 2][:, :, :, 0:HD], ps[:, 1, :].rearrange("p (b h d) -> p b h d", h=NH, d=HD),
                                     ACT.Copy).then_inc(s_va, 1)

            def qk_high(q):
                act.wait_ge(s_qkp, q + 1)
                need(act, s_qk, q)
                nc.scalar.activation(qk_hi[:], ps[:, 2, 0:T], ACT.Copy).then_inc(s_qkh, 1)

            def square(n):
                act.wait_ge(s_mn, n + 1)
                need(act, s_ptp, n - 3)
                nc.scalar.activation(sq[n % 4][:], ps[:, 3:5, :].rearrange("p a n -> p (a n)"),
                                     ACT.Square).then_inc(s_sq, 1)

            def exponentials(n):
                act.wait_ge(s_sub, n + 1)
                nc.scalar.activation(sq[n % 4][:], sq[n % 4][:], ACT.Exp, scale=-1.0 / HD ** 0.5).then_inc(s_p, 1)

            def turned(n):
                act.wait_ge(s_ptp, n + 1)
                need(act, s_o, n - 1)
                nc.scalar.activation(pt[n % 2][:, 0:512], ps[:, 5, :], ACT.Copy).then_inc(s_pta, 1)
                if n % 2 == 0:
                    nc.scalar.activation(pt[n % 2][:, 512:1024], ps[:, 6, :], ACT.Copy).then_inc(s_pta, 1)

            def heads_high(q):
                act.wait_ge(s_ontp, q + 1)
                need(act, s_rp, q)
                nc.scalar.activation(ont_hi[:], ps[:, 0, :], ACT.Copy).then_inc(s_ont, 1)

            def copy_inputs(q):
                act.wait_ge(s_x3, q + 1)
                need(act, s_sent, q)
                nc.scalar.activation(pay[:, :, 1, 0:E], pay[:, :, 0, 0:E], ACT.Copy).then_inc(s_x3c, 1)

            def inputs(q):
                act.wait_ge(s_x3tp, q + 1)
                need(act, s_lgp, q)
                nc.scalar.activation(x3t[:], ps[:, 0, :], ACT.Copy).then_inc(s_x3t, 1)

            def gates(q):
                act.wait_ge(s_df, q + 1)
                nc.scalar.activation(gate[:, 1, :], gate[:, 0, :], ACT.Exp).then_inc(s_ex, 1)

            def weights_high(q):
                for c in range(3 * q, 3 * q + 3):
                    dst = (wup_hi, vup_hi, wdn_hi)[c // NX]
                    act.wait_ge(s_stage[c % 2], 16 * (c // 2 + 1))
                    nc.scalar.activation(dst[:, c % NX, :], stage[c % 2][:], ACT.Copy).then_inc(s_whi, 1)

            for n in STEPS_OF_ATTENTION:
                quad(tokens_high, n, 6)
                quad(heads_high, n, -5)
                pair(turned, n, 0)
                pair(square, n, 3)
                pair(exponentials, n, 2)
                quad(inputs, n, -8)
                quad(posterior, n, 8)
                quad(root_first, n, 8)
                quad(qk_high, n, 5)
                quad(values, n, 5)
                quad(root_second, n, -6)
                quad(copy_inputs, n, -8)
                quad(gates, n, -9)
                quad(weights_high, n, 2)

            def columns(k, c):
                act.wait_ge(s_xcp, k + 1)
                if not (isinstance(k, int) and k < 2):
                    act.wait_ge(s_up, 2 * k - 2)
                nc.scalar.activation(xcol_hi[c % 2], ps[:, 0, 0:T], ACT.Copy).then_inc(s_xc, 1)

            def silu(k, c):
                act.wait_ge(s_up, 2 * k + 1)
                if not (isinstance(k, int) and k < 2):
                    act.wait_ge(s_hid, k - 1)
                nc.scalar.activation(act_up[c % 2], ps[:, 1 + c % 2, :], ACT.Silu).then_inc(s_silu, 1)

            def hidden_high(k, c):
                act.wait_ge(s_htp, k + 1)
                if not (isinstance(k, int) and k < 2):
                    act.wait_ge(s_dn, k - 1)
                nc.scalar.activation(hidt_hi[c % 2][:], ps[:, 5 + 2 * (c % 2), :], ACT.Copy).then_inc(s_ht, 1)

            def gated(k, c):
                act.wait_ge(s_dn, k + 1)
                act.wait_ge(s_dest, k + 1)
                if not (isinstance(k, int) and k < 4):
                    act.wait_ge(s_ys[c], round_of(k, c) - 16)
                nc.scalar.activation(yrow[c], ps[:, 6, 0:E], ACT.Copy, scale=rowgate[:, c:c + 1]).then_inc(s_y, 1)

            def act_tile(k, c, head=False, tail=0):
                if tail < 1:
                    columns(k + 1, (c + 1) % 4)
                if tail < 2:
                    silu(k, c)
                if not (head and k < 1) and tail < 3:
                    hidden_high(k - 1, (c + 3) % 4)
                if not (head and k < 2):
                    gated(k - 2, (c + 2) % 4)

            columns(0, 0)
            for k in range(4):
                act_tile(k, k, head=True)
            with act.Fori(4, TILES - 4, 4) as t:
                for c in range(4):
                    act_tile(t + c, c)
            for k in range(TILES - 4, TILES + 2):
                act_tile(k, k % 4, tail=max(0, k - TILES + 2))

        @block.gpsimd
        def _(pool):
            pool.memset(padt[:], 0.0).then_inc(s_pad0, 1)
            pool.wait_ge(s_pad0, 1)
            pool.memset(padt[:, E:E + 1], float(2 * NB * T)).then_inc(s_pad0, 1)
            pool.iota(tili[:, 3, 0:TILES], [[1, TILES]], base=0, channel_multiplier=0)
            pool.memset(ones_sb[:], 1.0).then_inc(s_consts, 1)
            pool.iota(tokid[:], [[NB * T, 2], [T, NB]], base=0, channel_multiplier=1).then_inc(s_consts, 1)
            pool.memset(M[:, :, 0:1], NEG)
            pool.memset(M[:, 0, 1:H + 1], NEG)
            pool.memset(x0row[:], X0)
            pool.memset(X[:, :, 0:1], X0)
            pool.memset(X[:, 0, 1:H + 1], X0).then_inc(s_init, 1)
            pool.wait_ge(s_init, 1)
            pool.memset(M[0:64, 0, 0:1], 0.0).then_inc(s_init, 1)
            pool.wait_ge(s_thp, 8)
            pool.wait_ge(s_cnt, 2)
            pool.memset(TH[64:128, 0, :], NEG)
            pool.memset(TH[0:64, T:STEPS, :], 0.0)
            pool.memset(TH[64:128, T + 1:STEPS, :], 0.0).then_inc(s_pad, 1)
            for i in range(BLKS):
                for g in range(NG):
                    r = slice(GR * g, GR * g + GR)
                    n = N[:, r, :]
                    pool.wait_ge(s_gauge, i * (4 * ROWS) + (4 * GR * (g + 1) - 1))
                    pool.tensor_tensor(C3[:, r, 0:2, :], shifted(M, i * ROWS + GR * g, GR, 2),
                                       bass.AP(tensor=n.tensor, offset=n.offset,
                                               ap=[n.ap[0], [H, GR], [0, 2], [1, H]]),
                                       ALU.subtract).then_inc(s_diff, 1)
                    pool.tensor_tensor(C3[:, r, 2, :], M[:, bass.ds(i * ROWS + GR * g + 1, GR), 0:H], n,
                                       ALU.subtract).then_inc(s_diff, 1)
                if i < BLKS - 1:
                    pool.wait_ge(s_lnx, i + 1)
                    pool.tensor_tensor(LNX[:, :, :], LNX[:, :, :], M[:, i * ROWS + 1:i * ROWS + ROWS + 1, :],
                                       ALU.add).then_inc(s_l, 1)
            pool.wait_ge(s_lst, 16 * 4 * BLKS)
            for r in range(2):
                pool.memset(va[r][:, :, :, HD:HD + 1], 1.0).then_inc(s_consts, 1)

            def below_least(n):
                m = mn[:, n % 4, :]
                v = sq[n % 4][:].rearrange("p (h s) -> p h s", s=T)
                pool.wait_ge(s_sq, n + 1)
                pool.tensor_tensor(v, v, bass.AP(tensor=m.tensor, offset=m.offset, ap=[m.ap[0], [1, NH], [0, T]]),
                                   ALU.subtract).then_inc(s_sub, 1)

            def send(q):
                pool.wait_ge(s_slot, q + 1)
                pool.wait_ge(s_x3c, q + 1)
                pool.wait_ge(s_pay, q + 1)
                for k in range(4):
                    for j in range(2):
                        pool.indirect_dma_start(xd_dram, bass.IndirectOffsetOnAxis(slot[:, q, j, k:k + 1], 0),
                                                pay[:, k, j, :], None).then_inc(s_sc[2 * k + j], 16)

            def sent(q):
                for k in range(8):
                    pool.wait_ge(s_sc[k], 16 * q + 16)
                pool.engine_nop().then_inc(s_sent, 1)

            for n in STEPS_OF_ATTENTION:
                pair(below_least, n, 3)
                quad(sent, n, -11)
                quad(send, n, -10)

            def scatter(k, c):
                pool.wait_ge(s_dest, k + 1)
                pool.wait_ge(s_y, k + 1)
                pool.nop(nofuse=True)
                pool.indirect_dma_start(y_dram, bass.IndirectOffsetOnAxis(dest[:, c:c + 1], 0), yrow[c], None,
                                        bounds_check=2 * NB * T - 1, oob_is_err=False).then_inc(s_ys[c], 16)

            with pool.Fori(0, TILES, 4) as t:
                for c in range(4):
                    scatter(t + c, c)

        @block.vector
        def _(dve):
            chain = [0]

            def link(ins):
                chain[0] += 1
                ins.then_inc(s_dv, 1)
                dve.wait_ge(s_dv, chain[0])

            V_ = nc.vector
            dve.wait_ge(s_small, 1)
            V_.tensor_scalar(zt[:], ps[:, 0, 0:NV], bproj_sb[:, 0:1], None, ALU.add).then_inc(s_smallv, 1)
            dve.wait_ge(s_in, 16 * 6)
            dve.wait_ge(s_tok, 16)
            V_.tensor_scalar(ohy[:], toky[:], iota_sb[0:NV, 0:1], None, ALU.is_equal).then_inc(s_ohy, 1)
            dve.wait_ge(s_small, 2)
            V_.tensor_copy(uv[:], ps[0:NV, 2, 0:2])
            link(V_.tensor_copy(gm[:], ps[0:NV, 1, 0:NV]))
            link(V_.tensor_copy(gpart[:, 0, :], gm[:]))
            link(V_.tensor_tensor(gleft[:, 0, :], gm[:], gpart[:, 0, :], ALU.subtract))
            link(V_.tensor_copy(gpart[:, 1, :], gleft[:, 0, :]))
            link(V_.tensor_tensor(gleft[:, 1, :], gleft[:, 0, :], gpart[:, 1, :], ALU.subtract))
            V_.tensor_copy(gpart[:, 2, :], gleft[:, 1, :]).then_inc(s_smallv, 1)
            dve.wait_ge(s_tokx, 16)
            V_.tensor_scalar(ohx[:], tokx[:], iota_sb[:, 0:1], None, ALU.is_equal).then_inc(s_oh, 1)
            for q in range(8):
                dve.wait_ge(s_thf, q + 1)
                V_.tensor_copy(thr[:, 4 * q:4 * q + 4, :],
                               ps[:, q, :].rearrange("p (b j) -> p b j", j=T)[:, :, ::-1]).then_inc(s_thr, 1)
            dve.wait_ge(s_oh, 1)
            for k, oh in enumerate((ohx, ohy)):
                V_.reduce_sum(cnt[:, k, 0, :], oh[0:NV, :].rearrange("p (b i) -> p b i", i=T), AX.X).then_inc(s_cnt, 1)
            dve.wait_ge(s_cnt, 2)
            for k in range(1, 4):
                m = V_.tensor_copy(cnt[:, :, k, :], cnt[:, :, 0, :])
            m.then_inc(s_cnt, 1)
            dve.wait_ge(s_small, 3)
            V_.tensor_scalar(gap[:], ps[:, 0, 0:1], 1.0 / T, bgap_sb[:, 0:1], ALU.mult, ALU.add).then_inc(s_gap, 1)
            dve.wait_ge(s_wraw, 1)
            V_.tensor_tensor(wqk_lo[:], raw_qk[:], wqk_hi[:].bitcast(f32), ALU.subtract)
            V_.tensor_tensor(wv_lo[:], raw_v[:], wv_hi[:].bitcast(f32), ALU.subtract)
            V_.tensor_tensor(wm_lo[:], raw_m[:], wm_hi[:].bitcast(f32), ALU.subtract)
            dve.wait_ge(s_consts, 2)
            V_.tensor_copy(tokf[:], tokid[:])
            V_.tensor_copy(run[:, 0, :], region_sb[:]).then_inc(s_consts, 1)
            dve.wait_ge(s_gap, 1)
            dve.wait_ge(s_init, 2)
            dve.wait_ge(s_consts, 3)
            dve.engine_nop().then_inc(s_ren, 1)
            dve.engine_nop().then_inc(s_ren, 1)

            def row(t, s):
                return cells(t, s, 1, H + 1)

            for i in range(BLKS):
                def gauge(k):
                    s = i * ROWS + k
                    done = i * (4 * ROWS) + 4 * k
                    c = C[:, k % 2, :]

                    def best_from_above():
                        if k == 0:
                            dve.wait_ge(s_ren, i * 2 + 2)
                            dve.wait_ge(s_tas, 2 * i + 2)
                        else:
                            dve.wait_ge(s_gauge, done - 1)
                        nc.vector.scalar_tensor_tensor(c, row(M, s), gap[:, 0:1], cells(M, s, 0, H),
                                                       ALU.add, ALU.max).then_inc(s_gauge, 1)

                    def best_of_row():
                        dve.wait_ge(s_gauge, done + 1)
                        nc.vector.tensor_tensor_scan(N[:, k, :], cells(TAS, s, 0, H), c,
                                                     cells(M, s + 1, 0, 1), ALU.add,
                                                     ALU.max).then_inc(s_gauge, 1)

                    def add_theta():
                        dve.wait_ge(s_gauge, done + 2)
                        nc.vector.tensor_tensor(row(M, s + 1), N[:, k, :], cells(TH, s, 0, H),
                                                ALU.add).then_inc(s_gauge, 1)

                    def to_right_half():
                        if k < ROWS - 1:
                            dve.wait_ge(s_gauge, done + 3)
                            nc.vector.tensor_copy(M[64:128, bass.ds(s + 2, 1), 0:1],
                                                  M[0:64, bass.ds(s + 1, 1), H:H + 1]).then_inc(s_gauge, 1)
                    return [best_from_above, best_of_row, add_theta, to_right_half]

                def linear(k):
                    s = i * ROWS + k
                    done = i * (4 * ROWS) + 4 * k

                    def weigh():
                        if k % GR == 0:
                            dve.wait_ge(s_coef, i * (2 * NG) + 2 * (k // GR) + 2)
                        if k == 0:
                            dve.wait_ge(s_ren, i * 2 + 2)
                        else:
                            dve.wait_ge(s_lin, done - 1)
                        x = shifted(X, s, 1, 2)
                        x = bass.AP(tensor=x.tensor, offset=x.offset, ap=[x.ap[0], x.ap[2], x.ap[3]])
                        nc.vector.tensor_tensor(U[:, k % 2], x, C3[:, k, 0:2, :], ALU.mult).then_inc(s_lin, 1)

                    def add():
                        dve.wait_ge(s_lin, done + 1)
                        nc.vector.tensor_tensor(V[:, k % 2, :], U[:, k % 2, 0, :], U[:, k % 2, 1, :],
                                                ALU.add).then_inc(s_lin, 1)

                    def scan():
                        dve.wait_ge(s_lin, done + 2)
                        nc.vector.tensor_tensor_scan(row(X, s + 1), C3[:, k, 2, :], V[:, k % 2, :],
                                                     cells(X, s + 1, 0, 1), ALU.mult,
                                                     ALU.add).then_inc(s_lin, 1)

                    def to_right_half():
                        if k < ROWS - 1:
                            dve.wait_ge(s_lin, done + 3)
                            nc.vector.tensor_copy(X[64:128, bass.ds(s + 2, 1), 0:1],
                                                  X[0:64, bass.ds(s + 1, 1), H:H + 1]).then_inc(s_lin, 1)
                    return [weigh, add, scan, to_right_half]

                LAG = 4
                for k in range(ROWS + LAG):
                    a = gauge(k) if k < ROWS else []
                    b = linear(k - LAG) if k >= LAG else []
                    for n in range(4):
                        if a:
                            a[n]()
                        if b:
                            b[n]()
                last = i * ROWS + ROWS
                dve.wait_ge(s_lnrow, i + 1)
                nc.vector.scalar_tensor_tensor(cells(M, last, 0, H + 1), lrow[:, :], LNX0,
                                               cells(M, last, 0, H + 1), ALU.add, ALU.add).then_inc(s_gauge, 1)
                nc.vector.tensor_copy(cells(X, last, 0, H + 1), x0row[:]).then_inc(s_lin, 1)
                dve.wait_ge(s_gauge, i * (4 * ROWS) + 4 * ROWS)
                dve.wait_ge(s_lin, i * (4 * ROWS) + 4 * ROWS)
                nxt = last + 1
                nc.vector.tensor_copy(M[64:128, bass.ds(nxt, 1), 0:1], M[0:64, bass.ds(last, 1), H:H + 1]).then_inc(s_ren, 1)
                nc.vector.tensor_copy(X[64:128, bass.ds(nxt, 1), 0:1], X[0:64, bass.ds(last, 1), H:H + 1]).then_inc(s_ren, 1)
            dve.wait_ge(s_lnx, BLKS)
            V_.tensor_tensor(LNX[:, :, :], LNX[:, :, :], M[:, STEPS - ROWS + 1:STEPS + 1, :], ALU.add).then_inc(s_l, 1)

            def over(a, n):
                return bass.AP(tensor=a.tensor, offset=a.offset, ap=[a.ap[0], a.ap[1], [0, n]])

            def each(a, n):
                return bass.AP(tensor=a.tensor, offset=a.offset, ap=[a.ap[0], [0, n], a.ap[1]])

            dve.wait_ge(s_v, 16)
            link(V_.tensor_scalar(nvt[:], vtot[:], -1.0, LNX0, ALU.mult, ALU.add))

            def log_posterior(q):
                b = slice(4 * q, 4 * q + 4)
                h = h0q[q % 3]
                dve.wait_ge(s_ldq[q], 32)
                link(V_.tensor_tensor(h[:], h[:], thf[:, b, :], ALU.subtract))
                for k in range(4):
                    m = V_.scalar_tensor_tensor(h[:, k, :], h[:, k, :], nvt[:, 4 * q + k:4 * q + k + 1],
                                                lbq[q % 2][:, k, ::-1], ALU.add, ALU.add)
                m.then_inc(s_e2, 1)

            def moments(c, src):
                for k in range(4):
                    m = V_.bn_stats(st6[:, k, :], src(k))
                link(m)
                for k in range(4):
                    m = V_.bn_aggr(mv[:, c, k, :], st6[:, k, :])
                link(m)
                m = V_.tensor_scalar(var[:, c, 0, :], mv[:, c, :, 1], EPS, None, ALU.add)
                if c == 0:
                    link(m)
                    m = V_.scalar_tensor_tensor(var[:, 0, 1, :], var[:, 0, 0, :], EPS, mv[:, 0, :, 1], ALU.mult, ALU.add)
                m.then_inc(s_var, 1)

            rounds = [0]

            def inverse_roots(c, n):
                y, r, t = var[:, c, 0:n, :], r1[:, c, 0:n, :], nwt[:, 0:n, :]
                rounds[0] += 1
                dve.wait_ge(s_root, rounds[0])
                link(V_.tensor_tensor(t, r, r, ALU.mult))
                link(V_.tensor_tensor(t, t, y, ALU.mult))
                link(V_.tensor_scalar(t, t, -0.5, 1.5, ALU.mult, ALU.add))
                link(V_.tensor_tensor(r, r, t, ALU.mult))

            def first_moments(q):
                dve.wait_ge(s_h0, q + 1)
                moments(0, lambda k: h0q[q % 3][:, k, :])

            def first_norms(q):
                h = h0q[q % 3]
                inverse_roots(0, 2)
                for k in range(4):
                    m = V_.tensor_scalar(x1[q % 2][:, k, :], h[:, k, :], mv[:, 0, k, 0:1], r1[:, 0, 0, k:k + 1],
                                         ALU.subtract, ALU.mult)
                link(m)
                need(dve, s_xntp, q)
                for k in range(4):
                    m = V_.tensor_scalar(xn[0][:, k, :], h[:, k, :], mv[:, 0, k, 0:1], r1[:, 0, 1, k:k + 1],
                                         ALU.subtract, ALU.mult)
                m.then_inc(s_xn, 1)
                V_.tensor_tensor(h1[:, 4 * q:4 * q + 4, :], h[:], x1[q % 2][:], ALU.add).then_inc(s_hx, 1)

            def tokens_low(q):
                dve.wait_ge(s_xnt, q + 1)
                need(dve, s_vp, q - 1)
                V_.tensor_tensor(xnt_lo[q % 2][:], ps[:, 0, :], xnt_hi[q % 2][:].bitcast(f32),
                                 ALU.subtract).then_inc(s_xntl, 1)

            def queries_keys(q):
                dve.wait_ge(s_qkh, q + 1)
                need(dve, s_d, 4 * q - 4)
                link(V_.scalar_tensor_tensor(qk_x[:], qk_hi[:].bitcast(f32), rowc_sb[:, 0:1], ps[:, 2, 0:T],
                                             ALU.mult, ALU.add))
                V_.tensor_scalar(qs[q % 2][:], qk_x[:], rowc_sb[:, 1:2], rowc_sb[:, 2:3], ALU.mult, ALU.add)
                link(V_.tensor_scalar(qk_k[:], qk_x[:], rowc_sb[:, 3:4], rowc_sb[:, 4:5], ALU.mult, ALU.add))
                V_.tensor_tensor(kx[q % 2][:].rearrange("p (h s) -> p h s", s=T), each(qk_k[:], NH),
                                 over(mask_sb[:], T), ALU.mult).then_inc(s_qk, 1)

            def nearest(n):
                dve.wait_ge(s_d, n + 1)
                need(dve, s_sub, n - 3)
                link(V_.tensor_reduce(rc[:, 0, :], ps[:, 3:5, :].rearrange("p a (h s) -> p (a h) s", s=T),
                                      AX.X, ALU.min, apply_absolute_value=True))
                V_.tensor_tensor(mn[:, n % 4, :], rc[:, 0, :], rc[:, 0, :], ALU.mult).then_inc(s_mn, 1)

            def turned(n):
                if n % 2:
                    dve.wait_ge(s_ptp, n + 1)
                    need(dve, s_o, n - 1)
                    V_.tensor_copy(pt[n % 2][:, 512:1024], ps[:, 6, :]).then_inc(s_ptd, 1)

            def normalise(n):
                q, k = n // 4, n % 4
                dve.wait_ge(s_o, n + 1)
                need(dve, s_ontp, q - 1)
                o = ps[:, 7, 0:NH * (HD + 1)].rearrange("p (h d) -> p h d", d=HD + 1)
                link(V_.reciprocal(rc[:, 1, :], o[:, :, HD]))
                V_.tensor_tensor(on[q % 2][:, k, :].rearrange("p (h d) -> p h d", d=HD), o[:, :, 0:HD],
                                 over(rc[:, 1, :], HD), ALU.mult).then_inc(s_on, 1)

            def heads_low(q):
                dve.wait_ge(s_ont, q + 1)
                need(dve, s_rp, q)
                V_.tensor_tensor(ont_lo[:], ps[:, 0, :], ont_hi[:].bitcast(f32), ALU.subtract).then_inc(s_ontl, 1)

            def residual(q):
                dve.wait_ge(s_rp, q + 1)
                b = slice(4 * q, 4 * q + 4)
                V_.tensor_tensor(h1[:, b, :], h1[:, b, :], ps[:, 1, :].rearrange("p (b j) -> p b j", j=T),
                                 ALU.add).then_inc(s_h1, 1)
                dve.wait_ge(s_h1, q + 1)
                moments(1, lambda k: h1[:, 4 * q + k, :])

            def second_norms(q):
                inverse_roots(1, 1)
                need(dve, s_sent, q)
                for k in range(4):
                    m = V_.tensor_scalar(pay[:, k, 0, 0:E], h1[:, 4 * q + k, :], mv[:, 1, k, 0:1], r1[:, 1, 0, k:k + 1],
                                         ALU.subtract, ALU.mult)
                m.then_inc(s_x3, 1)

            def pick(src, k):
                link(V_.tensor_reduce(top[:, k, :], src, AX.X, ALU.max))
                link(V_.tensor_tensor(eq[:], src, over(top[:, k, :], NX), ALU.is_equal))
                link(V_.tensor_tensor(eq[:], eq[:], each(rank8_sb[:], 4), ALU.mult))
                link(V_.tensor_reduce(first[:], eq[:], AX.X, ALU.max))
                link(V_.tensor_tensor(ohk[:, k], each(rank8_sb[:], 4), over(first[:], NX), ALU.is_equal))

            def choose(q):
                dve.wait_ge(s_lgp, q + 1)
                link(V_.tensor_copy(lg[:], ps[:, 2, 256:288].rearrange("p (b e) -> p b e", e=NX)))
                pick(lg[:], 0)
                link(V_.scalar_tensor_tensor(lg2[:], ohk[:, 0], -1e30, lg[:], ALU.mult, ALU.add))
                pick(lg2[:], 1)
                V_.tensor_tensor(msk[:], ohk[:, 0], ohk[:, 1], ALU.add).then_inc(s_msk, 1)
                V_.tensor_tensor(gate[:, 0, :], top[:, 1, :], top[:, 0, :], ALU.subtract).then_inc(s_df, 1)

            def places(q):
                dve.wait_ge(s_rkp, q + 1)
                for k in range(4):
                    link(V_.tensor_tensor(run[:, 4 * q + k + 1, :], run[:, 4 * q + k, :],
                                          ps[:, 2, 352 + NX * k:360 + NX * k], ALU.add))
                link(V_.tensor_tensor(rank[:], run[:, 4 * q:4 * q + 4, :],
                                      ps[:, 2, 320:352].rearrange("p (b e) -> p b e", e=NX), ALU.add))
                V_.tensor_tensor(ohk[:, 0], ohk[:, 0], rank[:], ALU.mult)
                link(V_.tensor_tensor(ohk[:, 1], ohk[:, 1], rank[:], ALU.mult))
                link(V_.tensor_reduce(slotf[:], ohk[:], AX.X, ALU.add))
                V_.tensor_copy(slot[:, q], slotf[:]).then_inc(s_slot, 1)
                dve.wait_ge(s_ex, q + 1)
                link(V_.tensor_scalar(gate[:, 0, :], gate[:, 1, :], 1.0, None, ALU.add))
                link(V_.reciprocal(top[:, 0, :], gate[:, 0, :]))
                link(V_.tensor_tensor(top[:, 1, :], top[:, 0, :], gate[:, 1, :], ALU.mult))
                for j in range(2):
                    V_.tensor_copy(pay[:, :, j, E:E + 1].rearrange("p b o -> p (b o)"), tokf[:, j, 4 * q:4 * q + 4])
                    m = V_.tensor_copy(pay[:, :, j, E + 1:ROW].rearrange("p b o -> p (b o)"), top[:, j, :])
                m.then_inc(s_pay, 1)

            def weights_low(q):
                for c in range(3 * q, 3 * q + 3):
                    hi, lo = ((wup_hi, wup_lo), (vup_hi, vup_lo), (wdn_hi, wdn_lo))[c // NX]
                    dve.wait_ge(s_whi, c + 1)
                    V_.tensor_tensor(lo[:, c % NX, :], stage[c % 2][:], hi[:, c % NX, :].bitcast(f32),
                                     ALU.subtract).then_inc(s_wlo, 1)

            for n in STEPS_OF_ATTENTION:
                pair(nearest, n, 3)
                quad(tokens_low, n, 6)
                quad(heads_low, n, -5)
                pair(turned, n, 0)
                quad(log_posterior, n, 9)
                quad(first_moments, n, 8)
                quad(first_norms, n, 7)
                quad(queries_keys, n, 5)
                pair(normalise, n, -1)
                quad(residual, n, -6)
                quad(second_norms, n, -7)
                quad(choose, n, -9)
                quad(places, n, -10)
                quad(weights_low, n, 2)
            counts, tiles, ends, jump = (tl[:, k, :] for k in range(4))
            link(V_.tensor_tensor(counts, run[:, NB, :], region_sb[:], ALU.subtract))
            V_.tensor_copy(tili[:, 2, 0:NX], run[:, NB, :])
            link(V_.memset(ones8, 1.0))
            link(V_.tensor_scalar(tili[:, 2, NX:2 * NX], counts, 127.0, None, ALU.add))
            link(V_.tensor_single_scalar(tili[:, 2, 2 * NX:3 * NX], tili[:, 2, NX:2 * NX], 7, ALU.arith_shift_right))
            link(V_.tensor_copy(tiles, tili[:, 2, 2 * NX:3 * NX]))
            link(V_.tensor_tensor_scan(ends, ones8, tiles, 0.0, ALU.mult, ALU.add))
            link(V_.tensor_scalar(jump, tiles, -1.0, float(REG // 128), ALU.mult, ALU.add))
            link(V_.tensor_copy(tilesf, tili[:, 3, 0:TILES]))
            link(V_.tensor_tensor(past, over(tilesf, NX), each(ends, TILES), ALU.is_ge))
            link(V_.tensor_reduce(tilf[:, 0, :], past[:, :, 0:NX - 1], AX.X, ALU.add))
            link(V_.tensor_tensor(past, past, each(jump, TILES), ALU.mult))
            link(V_.tensor_reduce(tilf[:, 1, :], past, AX.X, ALU.add))
            link(V_.tensor_tensor(tilf[:, 2, :], tilf[:, 1, :], tilesf, ALU.add))
            link(V_.tensor_scalar(tilf[:, 3, :], tilf[:, 2, :], 128.0, float(NX * REG), ALU.mult, ALU.min))
            V_.tensor_copy(tili[:, 1, 0:TILES], tilf[:, 0, :])
            V_.tensor_copy(tili[:, 0, 0:TILES], tilf[:, 3, :]).then_inc(s_table, 1)

            def hidden(k, c):
                dve.wait_ge(s_silu, k + 1)
                dve.wait_ge(s_up, 2 * k + 2)
                if not (isinstance(k, int) and k < 2):
                    dve.wait_ge(s_htp, k - 1)
                V_.tensor_tensor(hid[c % 2], act_up[c % 2], ps[:, 3 + c % 2, :], ALU.mult).then_inc(s_hid, 1)

            def destination(k, c):
                dve.wait_ge(s_xr[c], round_of(k, c))
                if not (isinstance(k, int) and k < 4):
                    dve.wait_ge(s_ys[c], round_of(k, c) - 16)
                V_.tensor_copy(rowgate[:, c:c + 1], xrow[c][:, E + 1:ROW])
                V_.tensor_copy(dest[:, c:c + 1], xrow[c][:, E:E + 1]).then_inc(s_dest, 1)

            def column_low(k, c):
                dve.wait_ge(s_xc, k + 1)
                if not (isinstance(k, int) and k < 2):
                    dve.wait_ge(s_up, 2 * k - 2)
                V_.tensor_tensor(xcol_lo[c % 2], ps[:, 0, 0:T], xcol_hi[c % 2].bitcast(f32),
                                 ALU.subtract).then_inc(s_xcl, 1)

            def hidden_low(k, c):
                dve.wait_ge(s_ht, k + 1)
                if not (isinstance(k, int) and k < 2):
                    dve.wait_ge(s_dn, k - 1)
                V_.tensor_tensor(hidt_lo[c % 2][:], ps[:, 5 + 2 * (c % 2), :], hidt_hi[c % 2][:].bitcast(f32),
                                 ALU.subtract).then_inc(s_htl, 1)

            def dve_tile(k, c, head=False, tail=0):
                if tail < 1:
                    column_low(k + 1, (c + 1) % 4)
                if tail < 2:
                    hidden(k, c)
                    destination(k, c)
                if not (head and k < 1) and tail < 3:
                    hidden_low(k - 1, (c + 3) % 4)

            column_low(0, 0)

            for k in range(4):
                dve_tile(k, k, head=True)
            with dve.Fori(4, TILES - 4, 4) as t:
                for c in range(4):
                    dve_tile(t + c, c)
            for k in range(TILES - 4, TILES + 2):
                dve_tile(k, k % 4, tail=max(0, k - TILES + 2))
            for q in range(NQ):
                b = slice(4 * q, 4 * q + 4)
                dve.wait_ge(s_yl[q], 32)
                V_.tensor_tensor(h1[:, b, :], h1[:, b, :], ya[q], ALU.add).then_inc(s_fin, 1)
                dve.wait_ge(s_fin, 2 * q + 1)
                V_.tensor_tensor(h1[:, b, :], h1[:, b, :], yb[q], ALU.add).then_inc(s_fin, 1)


def kernel(**inputs):
    import numpy as np
    import concourse.bacc as bacc
    from concourse import mybir
    from concourse.bass_utils import run_bass_kernel_spmd as run

    nc = bacc.Bacc("TRN2", target_bir_lowering=False, num_devices=1)
    x = np.asarray(inputs["x"])
    y = np.asarray(inputs["itok_BS_0_21"])
    laid = {
        "tok_x": x.reshape(-1), "tok_y": y.reshape(-1),
        "we_t": np.asarray(inputs["L0_tok_W_embed"]).T,
        "w_proj": np.asarray(inputs["L0_tok_W_proj"]),
        "b_proj": np.asarray(inputs["L0_tok_b_proj"]).reshape(-1, 1),
        "w_gap": np.asarray(inputs["L0_tok_W_gap"]).reshape(2, 128).T,
        "b_gap": np.broadcast_to(np.asarray(inputs["L0_tok_b_gap"]).reshape(1, 1), (128, 1)),
        "iota66": (np.arange(66, dtype=np.float32) % 22).reshape(66, 1),
    }
    wq, wk, wv = (np.asarray(inputs["L0_attn_W" + c]) for c in "qkv")
    NH, HD = wq.shape
    wqk_pl = np.zeros((4, 128, 128), wq.dtype)
    wv_bd = np.zeros((128, 128), wv.dtype)
    for h in range(NH):
        r = slice(HD * h, HD * h + HD)
        for g in range(4):
            for part in range(2):
                wqk_pl[g, r, 32 * g + NH * part + h] = wq[h]
                wqk_pl[g, r, 32 * g + NH * (2 + part) + h] = wk[h]
        wv_bd[r, r] = wv[h]
    p = np.arange(128)
    f = np.float32
    part = p % 32 // NH
    q_or_k = part // 2
    laid.update({
        "wqk_pl": wqk_pl, "wv_bd": wv_bd,
        "w_m": np.asarray(inputs["L0_attn_Wm"]), "w_g": np.asarray(inputs["L0_ffn_Wg"]),
        "w_up": np.asarray(inputs["L0_ffn_W"]), "v_up": np.asarray(inputs["L0_ffn_V"]),
        "w_down": np.asarray(inputs["L0_ffn_W2"]),
        "eye": np.eye(128, dtype=f), "below": (p[:, None] < p[None, :]).astype(f),
        "head_mask": (p[:, None] % NH == np.arange(NH)).astype(f),
        "row_consts": np.stack([-(part % 2), 1 - q_or_k, -q_or_k, q_or_k, 1 - q_or_k], 1).astype(f),
        "rank8": np.broadcast_to(8 - np.arange(8, dtype=f), (128, 8)),
        "region0": np.broadcast_to((32 * 128 + 128) * np.arange(8, dtype=f), (128, 8)),
    })
    arrays, args = {}, []
    for name, a in laid.items():
        a = np.ascontiguousarray(a)
        arrays["in_" + name] = a
        args.append(nc.dram_tensor("in_" + name, a.shape, mybir.dt.from_np(a.dtype), kind="ExternalInput").ap())
    args.append(nc.dram_tensor("out", (32, 128, 128), mybir.dt.float32, kind="ExternalOutput").ap())
    tower(nc, *args)
    r = run(nc, [arrays], core_ids=[0])
    return r.results[0]["out"]
```

```python
import concourse.bass as bass
from concourse import mybir
from contextlib import ExitStack


def tower(nc, tok_x, tok_y, we_t, w_proj, b_proj, w_gap, b_gap, iota66, wqk_pl, wv_bd, w_m, w_g, w_up, v_up, w_down,
          eye, below, head_mask, row_consts, rank8, region0, out):
    f32 = mybir.dt.float32
    i32 = mybir.dt.int32
    ALU = mybir.AluOpType
    ACT = mybir.ActivationFunctionType
    AX = mybir.AxisListType

    NB, T, E = 32, 128, 128
    NV = we_t.shape[1]
    H = T // 2
    ROWS = 26
    BLKS = 5
    STEPS = ROWS * BLKS
    GR = 1
    NG = ROWS // GR
    NEG = -100000000.0
    X0 = 2.0 ** -60
    LNX0 = 60.0 * 0.6931471805599453

    ctx = ExitStack()
    with ctx:
        def sb(name, shape, dt=f32):
            return ctx.enter_context(nc.sbuf_tensor(name, shape, dt))

        def pb(name, shape, dt=f32):
            return ctx.enter_context(nc.psum_tensor(name, shape, dt))

        def sem(name):
            return ctx.enter_context(nc.semaphore(name))

        th_dram = nc.dram_tensor("th_dram", (2, NB, T, T), f32).ap()
        l_dram = nc.dram_tensor("l_dram", (2, NB, T, T), f32).ap()

        v_dram = nc.dram_tensor("v_dram", (NB,), f32).ap()
        REG = NB * T + 128
        NX, F = 8, 512
        FC = F // 128
        NH, HD = 8, 16
        NQ = NB // 4
        TILES = 2 * NB * T // 128 + NX
        ROW = E + 2
        EPS = 1e-5
        xd_dram = nc.dram_tensor("xd_dram", (NX * REG + 128, ROW), f32).ap()
        y_dram = nc.dram_tensor("y_dram", (2 * NB * T, E), f32).ap()
        fr, bf16 = mybir.dt.float32r, mybir.dt.bfloat16
        V3 = 3 * NV

        wet_sb = sb("wet_sb", [E, NV])
        wproj_sb = sb("wproj_sb", [E, E])
        bproj_sb = sb("bproj_sb", [E, 1])
        wgap_sb = sb("wgap_sb", [E, 2])
        bgap_sb = sb("bgap_sb", [128, 1])
        iota_sb = sb("iota_sb", [V3, 1])
        gap = sb("gap", [128, 1])
        vtot = sb("vtot", [128, NB])
        nvt = sb("nvt", [128, NB])
        thf = sb("thf", [T, NB, T])
        h1 = thf
        wqk_hi = sb("wqk_hi", [E, 4, 128], fr)
        wqk_lo = sb("wqk_lo", [E, 4, 128], fr)
        wm_hi = sb("wm_hi", [E, E], fr)
        wm_lo = sb("wm_lo", [E, E], fr)
        wg_sb = sb("wg_sb", [E, NX])
        eye_sb = sb("eye_sb", [128, 128])
        below_sb = sb("below_sb", [128, 128], bf16)
        ones_sb = sb("ones_sb", [128, 128], bf16)
        mask_sb = sb("mask_sb", [128, NH])
        rowc_sb = sb("rowc_sb", [128, 5])
        rank8_sb = sb("rank8_sb", [128, NX])
        region_sb = sb("region_sb", [128, NX])
        run = sb("run", [128, NB + 1, NX])
        tokf = sb("tokf", [128, 2, NB])
        padt = sb("padt", [128, ROW])
        tili = sb("tili", [128, 4, TILES + 8], i32)
        tl = sb("tl", [128, 4, NX])
        ps = pb("ps", [128, 8, 512])

        align = ExitStack()

        def al(name, shape, dt=f32):
            return align.enter_context(nc.sbuf_tensor(name, shape, dt))

        M = al("M", [128, STEPS + 2, H + 1])
        X = al("X", [128, STEPS + 2, H + 1])
        C = al("C", [128, 2, H])
        N = al("N", [128, ROWS, H])
        first_use = ExitStack()
        toky = first_use.enter_context(nc.sbuf_tensor("toky", [NV, NB * T], i32))
        first_use.close()
        C3 = al("C3", [128, ROWS, 3, H])
        U = al("U", [128, 2, 2, H])
        V = al("V", [128, 2, H])
        LNX = al("LNX", [128, ROWS, H + 1])
        lrow = al("lrow", [128, H + 1])
        x0row = al("x0row", [128, H + 1])
        raw_qk = al("raw_qk", [E, 4, 128])
        raw_v = al("raw_v", [E, E])
        raw_m = al("raw_m", [E, E])
        raw_below = al("raw_below", [128, 128])
        tokid = al("tokid", [128, 2, NB], i32)
        zt = al("zt", [E, NV])
        gm = al("gm", [NV, NV])
        gpart = al("gpart", [NV, 3, NV], bf16)
        gleft = al("gleft", [NV, 2, NV])
        uv = al("uv", [NV, 2])
        cnt = al("cnt", [NV, 2, 4, NB])
        onehot = ExitStack()
        tokx = onehot.enter_context(nc.sbuf_tensor("tokx", [V3, NB * T], i32))
        ohx = onehot.enter_context(nc.sbuf_tensor("ohx", [V3, NB * T], bf16))
        ohy = onehot.enter_context(nc.sbuf_tensor("ohy", [NV, NB * T], bf16))
        gy = onehot.enter_context(nc.sbuf_tensor("gy", [V3, NB * T], bf16))
        onehot.enter_context(nc.sbuf_tensor("gap_to_thr", [128, 2 * STEPS * H - NB * T - 5 * NB * T // 2], f32))
        thr = onehot.enter_context(nc.sbuf_tensor("thr", [T, NB, T], f32))
        onehot.close()
        TH = al("TH", [128, STEPS, H])
        TAS = al("TAS", [128, STEPS, H])
        align.close()

        wup_hi, wup_lo, vup_hi, vup_lo = (
            sb(n, [128, NX, F], fr) for n in ("wup_hi", "wup_lo", "vup_hi", "vup_lo"))
        wdn = sb("wdn", [128, NX, FC, 2, E], fr)

        def parts_of(c):
            kind, e = c // NX, c % NX
            staged = stage[c % 2][:]
            if kind == 2:
                return wdn[:, e, :, 0, :], wdn[:, e, :, 1, :], staged.rearrange("p (c n) -> p c n", n=E)
            hi, lo = ((wup_hi, wup_lo), (vup_hi, vup_lo))[kind]
            return hi[:, e, :], lo[:, e, :], staged

        h0q = [sb(f"h0q{k}", [T, 4, T]) for k in range(3)]
        lbq = [sb(f"lbq{k}", [T, 4, T]) for k in range(2)]
        stage = [sb(f"stage{k}", [128, F]) for k in range(2)]
        x1 = [sb(f"x1{k}", [T, 4, T]) for k in range(2)]
        xn = [sb(f"xn{k}", [T, 4, T]) for k in range(2)]
        xnt_hi = [sb(f"xnt_hi{k}", [128, 512], fr) for k in range(2)]
        xnt_lo = [sb(f"xnt_lo{k}", [128, 512], fr) for k in range(2)]
        on = [sb(f"on{k}", [T, 4, T]) for k in range(2)]
        ont_hi = sb("ont_hi", [128, 512], fr)
        ont_lo = sb("ont_lo", [128, 512], fr)
        x3t = sb("x3t", [128, 512])
        sq = [sb(f"sq{k}", [128, 1024]) for k in range(3)]
        pt = [sb(f"pt{k}", [128, 1024]) for k in range(2)]
        qk_hi = sb("qk_hi", [128, 128], fr)
        qk_x = sb("qk_x", [128, 128])
        qk_k = sb("qk_k", [128, 128])
        qs = [sb(f"qs{k}", [128, 128], fr) for k in range(2)]
        kx = [sb(f"kx{k}", [128, 1024], fr) for k in range(2)]
        va = [sb(f"va{k}", [128, 4, NH, HD + 1]) for k in range(2)]
        pay = [sb(f"pay{k}", [128, 4, 2, ROW]) for k in range(2)]
        st6 = sb("st6", [128, 4, 6])
        mv = sb("mv", [128, 2, 4, 2])
        r1 = sb("r1", [128, 2, 2, 4])
        var = sb("var", [128, 2, 2, 4])
        lnv = sb("lnv", [128, 2, 2, 4])
        nwt = sb("nwt", [128, 2, 4])
        mn = sb("mn", [128, 3, NH])
        rc = sb("rc", [128, 2, NH])
        lg = sb("lg", [128, 4, NX])
        lg2 = sb("lg2", [128, 4, NX])
        eq = sb("eq", [128, 4, NX])
        ohk = sb("ohk", [128, 2, 4, NX])
        msk = sb("msk", [128, 4, NX], bf16)
        top = sb("top", [128, 2, 4])
        first = sb("first", [128, 4])
        gate = sb("gate", [128, 2, 4])
        ranks = sb("ranks", [128, 2 * 4 * NX])
        rank = sb("rank", [128, 4, NX])
        slotf = sb("slotf", [128, 2, 4])
        slot = sb("slot", [128, NQ, 2, 4], i32)
        tilesf = x1[0][:, :, :].rearrange("p b j -> p (b j)")[:, 0:TILES]
        tilf = x1[0][:, :, :].rearrange("p b j -> p (b j)")[:, TILES:5 * TILES].rearrange("p (a k) -> p a k", k=TILES)
        past = pt[0][:, 0:TILES * NX].rearrange("p (k e) -> p k e", e=NX)
        ones8 = x1[1][:, 0, 0:NX]
        xrow = [stage[k // 2][:, ROW * (k % 2):ROW * (k % 2) + ROW] for k in range(4)]
        yrow = [on[k // 4][:, k % 4, :] for k in range(4)]
        xcol_hi = [ont_hi[:, T * k:T * k + T] for k in range(2)]
        xcol_lo = [ont_lo[:, T * k:T * k + T] for k in range(2)]
        act_up = [sq[0][:, F * k:F * k + F] for k in range(2)]
        hid = [sq[1][:, F * k:F * k + F] for k in range(2)]
        hidt_hi, hidt_lo = xnt_hi, xnt_lo
        dest = sb("dest", [128, 4], i32)
        ylow = [on[1][:, k, :] for k in range(2)]
        rowgate = sb("rowgate", [128, 4])
        ya = [sq[q // 2][:, 512 * (q % 2):512 * (q % 2) + 512].rearrange("p (b j) -> p b j", j=T)
              for q in range(NQ - 2)] + [t[:, :, :] for t in x1]
        yb = [t.rearrange("p (b j) -> p b j", j=T) if len(t.shape) == 2 else t for t in
              [pt[0][:, 0:512], pt[0][:, 512:1024], pt[1][:, 0:512], pt[1][:, 512:1024],
               h0q[0][:, :, :], h0q[1][:, :, :], h0q[2][:, :, :], lbq[0][:, :, :]]]

        s_in = sem("s_in")
        s_tok = sem("s_tok")
        s_oh = sem("s_oh")
        s_cnt = sem("s_cnt")
        s_small = sem("s_small")
        s_smallv = sem("s_smallv")
        s_gyp = sem("s_gyp")
        s_gy = sem("s_gy")
        s_thp = sem("s_thp")
        s_thf = sem("s_thf")
        s_thr = sem("s_thr")
        s_th = [sem(f"s_th{c}") for c in range(BLKS)]
        s_pad = sem("s_pad")
        s_gap = sem("s_gap")
        s_tas = sem("s_tas")
        s_init = sem("s_init")
        s_gauge = sem("s_gauge")
        s_lin = sem("s_lin")
        s_diff = sem("s_diff")
        s_coef = sem("s_coef")
        s_lnrow = sem("s_lnrow")
        s_ren = sem("s_ren")
        s_lnx = sem("s_lnx")
        s_l = sem("s_l")
        s_lst = sem("s_lst")
        s_vst = sem("s_vst")
        s_v = sem("s_v")
        s_e2 = sem("s_e2")
        s_out = sem("s_out")
        s_ohy = sem("s_ohy")
        s_tokx = sem("s_tokx")
        s_thw = [sem(f"s_thw{c}") for c in range(BLKS)]
        s_xntl = sem("s_xntl")
        s_ontl = sem("s_ontl")
        s_qkh = sem("s_qkh")
        s_stage = [sem(f"s_stage{k}") for k in range(2)]
        s_whi = sem("s_whi")
        s_wlo = sem("s_wlo")
        s_wraw = sem("s_wraw")
        s_sent = sem("s_sent")
        s_rkc = sem("s_rkc")
        s_xcl = sem("s_xcl")
        s_htl = sem("s_htl")
        s_const = sem("s_const")
        s_consts = sem("s_consts")
        s_ldq = [sem(f"s_ldq{q}") for q in range(NQ)]
        s_h0 = sem("s_h0")
        s_dv = sem("s_dv")
        s_xn = sem("s_xn")
        s_var = sem("s_var")
        s_lnv = sem("s_lnv")
        s_root = sem("s_root")
        s_hx = sem("s_hx")
        s_xntp = sem("s_xntp")
        s_xnt = sem("s_xnt")
        s_va = sem("s_va")
        s_qkp = sem("s_qkp")
        s_qk = sem("s_qk")
        s_d = sem("s_d")
        s_sq = sem("s_sq")
        s_mn = sem("s_mn")
        s_sub = sem("s_sub")
        s_p = sem("s_p")
        s_ptp = sem("s_ptp")
        s_pta = sem("s_pta")
        s_ptd = sem("s_ptd")
        s_o = sem("s_o")
        s_on = sem("s_on")
        s_ontp = sem("s_ontp")
        s_ont = sem("s_ont")
        s_rp = sem("s_rp")
        s_h1 = sem("s_h1")
        s_x3 = sem("s_x3")
        s_x3c = sem("s_x3c")
        s_x3tp = sem("s_x3tp")
        s_x3t = sem("s_x3t")
        s_lgp = sem("s_lgp")
        s_df = sem("s_df")
        s_ex = sem("s_ex")
        s_msk = sem("s_msk")
        s_rkp = sem("s_rkp")
        s_slot = sem("s_slot")
        s_pay = sem("s_pay")
        s_pad0 = sem("s_pad0")
        s_table = sem("s_table")
        s_counts = sem("s_counts")
        s_padw = sem("s_padw")
        s_xr = [sem(f"s_xr{k}") for k in range(4)]
        s_xc = sem("s_xc")
        s_xcp = sem("s_xcp")
        s_up = sem("s_up")
        s_silu = sem("s_silu")
        s_hid = sem("s_hid")
        s_htp = sem("s_htp")
        s_ht = sem("s_ht")
        s_dn = sem("s_dn")
        s_y = sem("s_y")
        s_ylow = sem("s_ylow")
        s_dest = sem("s_dest")
        s_ys = [sem(f"s_ys{k}") for k in range(4)]
        s_yl = [sem(f"s_yl{q}") for q in range(NQ)]
        s_fin = sem("s_fin")
        s_sc = [sem(f"s_sc{k}") for k in range(8)]
        block = ctx.enter_context(nc.Block())

        def need(eng, s, n):
            if n > 0:
                eng.wait_ge(s, n)

        def shifted(t, row, rows, second):
            a = t[:, row:row + rows, 0:H]
            return bass.AP(tensor=a.tensor, offset=a.offset, ap=[a.ap[0], [H + 1, rows], [1, second], [1, H]])

        def cells(t, s, lo, hi):
            return t[:, s, lo:hi]

        def span(c, h):
            lo, hi = max(c * ROWS, h), min((c + 1) * ROWS, T + h)
            return lo, hi

        def lane_rows(t, d, h, lo, hi):
            a = t[d, :, lo - h:hi - h, :] if d == 0 else t[d, :, T - (hi - h):T - (lo - h), :][:, ::-1, :]
            return a[:, :, H * h:H * h + H]

        STEPS_OF_ATTENTION = range(-18, NB + 19)

        def pair(piece, n, ahead):
            if 0 <= n + ahead < NB:
                piece(n + ahead)

        def quad(piece, n, ahead):
            if (n + ahead) % 4 == 0 and 0 <= n + ahead < NB:
                piece((n + ahead) // 4)

        def pta(n):
            return n + (n + 1) // 2

        def ptd(n):
            return n // 2

        def at_tile(k):
            return slice(k, k + 1) if isinstance(k, int) else bass.ds(k, 1)

        def round_of(k, c):
            return 16 * (k // 4 + 1) if isinstance(k, int) else (k - c) * 4 + 16

        CHUNKS = 3 * NX

        @block.sync
        def _(sp):
            sp.dma_start(toky[:], tok_y.partition_broadcast(NV)).then_inc(s_tok, 16)
            sp.dma_start(tokx[:], tok_x.partition_broadcast(V3)).then_inc(s_tokx, 16)
            sp.wait_ge(s_thf, NQ)
            sp.wait_ge(s_thr, NQ)
            for c in range(BLKS):
                lo, hi = c * ROWS, min((c + 1) * ROWS, T)
                sp.dma_start(th_dram[0][:, lo:hi, :].rearrange("b i j -> i b j"), thf[lo:hi, :, :]).then_inc(s_thw[c], 16)
                sp.dma_start(th_dram[1][:, T - hi:T - lo, :].rearrange("b i j -> i b j"),
                             thr[T - hi:T - lo, :, :]).then_inc(s_thw[c], 16)
                sp.wait_ge(s_thw[c], 32)
                sp.wait_ge(s_cnt, 2)
                for h in range(2):
                    lo, hi = span(c, h)
                    for d in range(2):
                        lane = 64 * h + 32 * d
                        sp.dma_start(TH[lane:lane + 32, lo:hi, :],
                                     lane_rows(th_dram, d, h, lo, hi)).then_inc(s_th[c], 16)
            for c in range(BLKS):
                sp.wait_ge(s_l, c + 1)
                for h in range(2):
                    lo, hi = span(c, h)
                    for d in range(2):
                        lane = 64 * h + 32 * d
                        sp.dma_start(lane_rows(l_dram, d, h, lo, hi),
                                     LNX[lane:lane + 32, lo - c * ROWS:hi - c * ROWS, 1:H + 1]).then_inc(s_lst, 16)
            sp.dma_start(v_dram.rearrange("(b o) -> b o", o=1),
                         LNX[64:96, T - (BLKS - 1) * ROWS, H:H + 1]).then_inc(s_vst, 16)
            sp.wait_ge(s_vst, 16)
            sp.dma_start(vtot[:, :], v_dram.partition_broadcast(128)).then_inc(s_v, 16)
            sp.wait_ge(s_lst, 16 * 4 * BLKS)

            def load_quad(q):
                need(sp, s_hx, q - 2)
                need(sp, s_xn, q - 2)
                need(sp, s_e2, q - 1)
                b = slice(4 * q, 4 * q + 4)
                sp.dma_start(h0q[q % 3][:], l_dram[0, b].rearrange("b i j -> i b j")).then_inc(s_ldq[q], 16)
                sp.dma_start(lbq[q % 2][:], l_dram[1, b].rearrange("b i j -> i b j")).then_inc(s_ldq[q], 16)

            def load_weights(c):
                kind, e = c // NX, c % NX
                need(sp, s_whi, c - 1)
                need(sp, s_wlo, c - 1)
                if kind < 2:
                    sp.dma_start(stage[c % 2][:], (w_up, v_up)[kind][e]).then_inc(s_stage[c % 2], 16)
                else:
                    sp.dma_start(stage[c % 2][:].rearrange("p (c n) -> p c n", n=E),
                                 w_down[e].rearrange("(c p) n -> p c n", p=128)).then_inc(s_stage[c % 2], 16)

            for n in STEPS_OF_ATTENTION:
                quad(load_quad, n, 18)
                if 0 <= n + 3 < CHUNKS:
                    load_weights(n + 3)
            sp.wait_ge(s_pad0, 2)
            sp.dma_start(xd_dram[NX * REG:NX * REG + 128, :], padt[:]).then_inc(s_padw, 16)
            sp.wait_ge(s_counts, 1)
            for e in range(NX):
                row = sp.value_load(tili[0:1, 2, e:e + 1], min_val=0, max_val=NX * REG)
                sp.dma_start(xd_dram[bass.ds(row, 128), :], padt[:]).then_inc(s_padw, 16)
            for k in range(8):
                sp.wait_ge(s_sc[k], 16 * NQ)
            sp.wait_ge(s_padw, 16 * (NX + 1))
            sp.wait_ge(s_table, 1)
            sp.wait_ge(s_whi, CHUNKS)
            sp.wait_ge(s_wlo, CHUNKS)

            def load(k, c):
                row = sp.value_load(tili[0:1, 0, bass.ds(k, 1)] if not isinstance(k, int) else tili[0:1, 0, k:k + 1],
                                    min_val=0, max_val=NX * REG)
                if not (isinstance(k, int) and k < 4):
                    sp.wait_ge(s_xcp, k - 3)
                    sp.wait_ge(s_dest, k - 3)
                sp.dma_start(xrow[c], xd_dram[bass.ds(row, 128), :]).then_inc(s_xr[c], 16)

            for k in range(4):
                load(k, k)
            with sp.Fori(4, TILES, 4) as t:
                for c in range(4):
                    load(t + c, c)
            for c in range(4):
                sp.wait_ge(s_ys[c], 16 * (TILES // 4))
            for q in range(NQ):
                b = slice(4 * q, 4 * q + 4)
                y = y_dram.rearrange("(k b t) e -> k t b e", k=2, t=T)
                sp.dma_start(ya[q], y[0][:, b, :]).then_inc(s_yl[q], 16)
                sp.dma_start(yb[q], y[1][:, b, :]).then_inc(s_yl[q], 16)
            for q in range(NQ):
                b = slice(4 * q, 4 * q + 4)
                sp.wait_ge(s_fin, 2 * q + 2)
                sp.dma_start(out[b].rearrange("b i j -> i b j"), h1[:, b, :]).then_inc(s_out, 16)
            sp.wait_ge(s_out, 16 * NQ)

        @block.tensor
        def _(pe):
            def three(dst, a, b, first=True, last=True):
                nc.tensor.matmul(dst, a[0], b[0], start=first, stop=False)
                nc.tensor.matmul(dst, a[0], b[1], start=False, stop=False)
                return nc.tensor.matmul(dst, a[1], b[0], start=False, stop=last)

            pe.wait_ge(s_in, 16 * 6)
            nc.tensor.matmul(ps[:, 0, 0:NV], wproj_sb[:], wet_sb[:], start=True, stop=True).then_inc(s_small, 1)
            pe.wait_ge(s_smallv, 1)
            nc.tensor.matmul(ps[0:NV, 1, 0:NV], zt[:], zt[:], start=True, stop=True)
            nc.tensor.matmul(ps[0:NV, 2, 0:2], zt[:], wgap_sb[:], start=True, stop=True).then_inc(s_small, 1)
            pe.wait_ge(s_smallv, 2)
            pe.wait_ge(s_ohy, 1)
            for q in range(NQ):
                nc.tensor.matmul(ps[0:V3, q, :], gpart[:, :, :].rearrange("p k v -> p (k v)"), ohy[:, 512 * q:512 * q + 512],
                                 start=True, stop=True).then_inc(s_gyp, 1)
            pe.wait_ge(s_oh, 1)
            for q in range(NQ):
                pe.wait_ge(s_gy, q + 1)
                for k in range(4):
                    b = 4 * q + k
                    m = nc.tensor.matmul(ps[:, q, T * k:T * k + T], ohx[:, b * T:b * T + T], gy[:, b * T:b * T + T],
                                         start=True, stop=True)
                m.then_inc(s_thp, 1)
            pe.wait_ge(s_cnt, 3)
            pe.wait_ge(s_thf, 1)
            pe.wait_ge(s_thr, 1)
            pe.wait_ge(s_const, 16 * 10)
            pe.wait_ge(s_thf, 2)
            pe.wait_ge(s_thr, 2)
            nc.tensor.matmul(ps[:, 1, 0:E], raw_v[:], raw_m[:], start=True, stop=True)
            nc.tensor.matmul(ps[:, 0, 0:1], cnt[:, 0].rearrange("p r b -> p (r b)"), uv[:, 0:1], start=True, stop=False)
            nc.tensor.matmul(ps[:, 0, 0:1], cnt[:, 1].rearrange("p r b -> p (r b)"), uv[:, 1:2],
                             start=False, stop=True).then_inc(s_small, 1)

            def turn_tokens(q):
                pe.wait_ge(s_xn, q + 1)
                need(pe, s_x3t, q - 4)
                for k in range(4):
                    m = nc.tensor.transpose(ps[:, 0, T * k:T * k + T], xn[q % 2][:, k, :], eye_sb[:])
                m.then_inc(s_xntp, 1)

            def project(q):
                r = q % 2
                pe.wait_ge(s_xnt, q + 1)
                pe.wait_ge(s_xntl, q + 1)
                need(pe, s_msk, q - 4)
                for k in range(4):
                    c = slice(T * k, T * k + T)
                    m = three(ps[:, 2, 0:T], (wqk_hi[:, k, :], wqk_lo[:, k, :]), (xnt_hi[r][:, c], xnt_lo[r][:, c]),
                              k == 0, k == 3)
                m.then_inc(s_qkp, 1)

            def distances(n):
                q, k = n // 4, n % 4
                g = slice(32 * k, 32 * k + 32)
                pe.wait_ge(s_qk, q + 1)
                need(pe, s_sq, n)
                need(pe, s_mn, n)
                for c in range(2):
                    m = nc.tensor.matmul(ps[:, 3 + c, :], qs[q % 2][g, :], kx[q % 2][g, 512 * c:512 * c + 512],
                                         start=True, stop=True)
                m.then_inc(s_d, 1)

            def turn_and_attend(n):
                turned = n - 1
                q, k = turned // 4, turned % 4
                if n < NB:
                    pe.wait_ge(s_p, n + 1)
                    need(pe, s_pta, pta(n))
                    need(pe, s_ptd, ptd(n))
                if n > 0:
                    need(pe, s_pta, pta(n))
                    need(pe, s_ptd, ptd(n))
                    pe.wait_ge(s_va, q + 1)
                    need(pe, s_on, turned)
                for h in range(NH):
                    if n < NB:
                        last = nc.tensor.transpose(ps[:, 5 + h // 4, T * (h % 4):T * (h % 4) + T],
                                                   sq[n % 3][:, T * h:T * h + T], eye_sb[:])
                        if h == NH - 1:
                            last.then_inc(s_ptp, 1)
                    if n > 0:
                        m = nc.tensor.matmul(ps[:, 7, (HD + 1) * h:(HD + 1) * (h + 1)],
                                             pt[turned % 2][:, T * h:T * h + T], va[q % 2][:, k, h, :],
                                             start=True, stop=True)
                        if h == NH - 1:
                            m.then_inc(s_o, 1)

            def turn_heads(q):
                pe.wait_ge(s_on, 4 * q + 4)
                pe.wait_ge(s_xnt, min(q + 4, NQ))
                pe.wait_ge(s_xntl, min(q + 4, NQ))
                need(pe, s_x3t, q - 1)
                for k in range(4):
                    m = nc.tensor.transpose(ps[:, 0, T * k:T * k + T], on[q % 2][:, k, :], eye_sb[:])
                m.then_inc(s_ontp, 1)

            def merge(q):
                pe.wait_ge(s_ont, q + 1)
                pe.wait_ge(s_ontl, q + 1)
                need(pe, s_h1, q)
                for k in range(4):
                    c = slice(T * k, T * k + T)
                    m = three(ps[:, 1, c], (ont_hi[:, c], ont_lo[:, c]), (wm_hi[:], wm_lo[:]))
                m.then_inc(s_rp, 1)

            def turn_inputs(q):
                pe.wait_ge(s_x3, q + 1)
                pe.wait_ge(s_ont, min(q + 2, NQ))
                pe.wait_ge(s_ontl, min(q + 2, NQ))
                need(pe, s_rkc, q)
                for k in range(4):
                    m = nc.tensor.transpose(ps[:, 0, T * k:T * k + T], pay[q % 2][:, k, 0, 0:E], eye_sb[:])
                m.then_inc(s_x3tp, 1)

            def gate_logits(q):
                pe.wait_ge(s_x3t, q + 1)
                pe.wait_ge(s_qk, min(q + 5, NQ))
                need(pe, s_msk, q)
                for k in range(4):
                    m = nc.tensor.matmul(ps[:, 2, 256 + NX * k:256 + NX * k + NX], x3t[:, T * k:T * k + T], wg_sb[:],
                                         start=True, stop=True)
                m.then_inc(s_lgp, 1)

            def ranks(q):
                pe.wait_ge(s_msk, q + 1)
                pe.wait_ge(s_ont, min(q + 3, NQ))
                pe.wait_ge(s_ontl, min(q + 3, NQ))
                nc.tensor.matmul(ps[:, 0, 0:32], below_sb[:], msk[:, :, :].rearrange("p b e -> p (b e)"),
                                 start=True, stop=True)
                nc.tensor.matmul(ps[:, 0, 32:64], ones_sb[:], msk[:, :, :].rearrange("p b e -> p (b e)"),
                                 start=True, stop=True).then_inc(s_rkp, 1)

            pe.wait_ge(s_const, 16 * 10)
            pe.wait_ge(s_consts, 5)
            for n in STEPS_OF_ATTENTION:
                pair(distances, n, 2)
                if 0 <= n <= NB:
                    turn_and_attend(n)
                quad(turn_tokens, n, 8)
                quad(gate_logits, n, -12)
                quad(turn_heads, n, -5)
                quad(ranks, n, -14)
                quad(project, n, 6)
                quad(turn_inputs, n, -11)
                quad(merge, n, -7)

            def column(k, c):
                pe.wait_ge(s_xr[c], round_of(k, c))
                if not (isinstance(k, int) and k < 1):
                    pe.wait_ge(s_xc, k)
                    pe.wait_ge(s_xcl, k)
                nc.tensor.transpose(ps[:, 0, 0:T], xrow[c][:, 0:E], eye_sb[:]).then_inc(s_xcp, 1)

            def up(k, c, e):
                pe.wait_ge(s_xc, k + 1)
                pe.wait_ge(s_xcl, k + 1)
                if not (isinstance(k, int) and k < 2):
                    pe.wait_ge(s_hid, k - 1)
                for n, hi, lo in ((1, wup_hi, wup_lo), (3, vup_hi, vup_lo)):
                    m = three(ps[:, n + c % 2, :], (xcol_hi[c % 2], xcol_lo[c % 2]),
                              [w[:, bass.ds(e, 1), :].rearrange("p e f -> p (e f)") for w in (hi, lo)])
                    m.then_inc(s_up, 1)

            def turn(k, c):
                pe.wait_ge(s_hid, k + 1)
                if not (isinstance(k, int) and k < 2):
                    pe.wait_ge(s_ht, k - 1)
                    pe.wait_ge(s_htl, k - 1)
                for n in range(FC):
                    m = nc.tensor.transpose(ps[:, 5 + 2 * (c % 2), T * n:T * n + T], hid[c % 2][:, T * n:T * n + T],
                                            eye_sb[:])
                m.then_inc(s_htp, 1)

            def down(k, c, e):
                pe.wait_ge(s_ht, k + 1)
                pe.wait_ge(s_htl, k + 1)
                if not (isinstance(k, int) and k < 1):
                    pe.wait_ge(s_y, k)
                for n in range(FC):
                    b = slice(T * n, T * n + T)
                    low = [hidt_lo[c % 2][:, b], wdn[:, bass.ds(e, 1), n, 0, :].rearrange("p e n -> p (e n)")]
                    both = wdn[:, bass.ds(e, 1), n, :, :].rearrange("p e j n -> p (e j n)")
                    if n == 0:
                        nc.tensor.matmul(ps[:, 6, 0:2 * E], hidt_hi[c % 2][:, b], both, start=True, stop=False)
                        nc.tensor.matmul(ps[:, 6, 0:E], *low, start=False, stop=False)
                    else:
                        nc.tensor.matmul(ps[:, 6, 0:E], *low, start=False, stop=False)
                        m = nc.tensor.matmul(ps[:, 6, 0:2 * E], hidt_hi[c % 2][:, b], both, start=False,
                                             stop=(n == FC - 1))
                m.then_inc(s_dn, 1)

            pe.wait_ge(s_whi, CHUNKS)
            pe.wait_ge(s_wlo, CHUNKS)
            pe.wait_ge(s_table, 1)

            def expert_of(k):
                return pe.value_load(tili[0:1, 1, at_tile(k)], min_val=0, max_val=NX - 1)

            def pe_tiles(first, count):
                places = range(count)
                expert = {0: expert_of(first)}
                for n in places:
                    k, c = first + n, n % 4
                    if not isinstance(k, int) or k < TILES:
                        up(k, c, expert[n])
                    if not isinstance(k, int) or k + 1 < TILES:
                        column(k + 1, (c + 1) % 4)
                    if n < 2 and (not isinstance(k, int) or k >= 2):
                        expert[n - 2] = expert_of(k - 2)
                    if not isinstance(k, int) or 1 <= k < TILES + 1:
                        turn(k - 1, (c + 3) % 4)
                    if n + 1 < count and (not isinstance(k, int) or k + 1 < TILES):
                        expert[n + 1] = expert_of(k + 1)
                    if not isinstance(k, int) or k >= 2:
                        down(k - 2, (c + 2) % 4, expert[n - 2])

            column(0, 0)
            pe_tiles(0, 4)
            with pe.Fori(4, TILES - 4, 8) as t:
                pe_tiles(t, 8)
            pe_tiles(TILES - 4, 6)

        @block.scalar
        def _(act):
            for dst, src in ((wet_sb[:], we_t), (wproj_sb[:], w_proj), (bproj_sb[:], b_proj),
                             (wgap_sb[:], w_gap), (bgap_sb[:], b_gap), (iota_sb[:], iota66)):
                act.dma_start(dst, src).then_inc(s_in, 16)
            for dst, src in ((raw_qk[:], wqk_pl.rearrange("g e c -> e g c")), (raw_v[:], wv_bd), (raw_m[:], w_m),
                             (wg_sb[:], w_g), (eye_sb[:], eye), (raw_below[:], below), (mask_sb[:], head_mask),
                             (rowc_sb[:], row_consts), (rank8_sb[:], rank8), (region_sb[:], region0)):
                act.dma_start(dst, src).then_inc(s_const, 16)
            for q in range(8):
                act.wait_ge(s_gyp, q + 1)
                nc.scalar.activation(gy[:, 512 * q:512 * q + 512], ps[0:V3, q, :], ACT.Copy).then_inc(s_gy, 1)
            for q in range(8):
                act.wait_ge(s_thp, q + 1)
                nc.scalar.activation(thf[:, 4 * q:4 * q + 4, :],
                                     ps[:, q, :].rearrange("p (b j) -> p b j", j=T), ACT.Copy).then_inc(s_thf, 1)
            act.wait_ge(s_const, 16 * 10)
            nc.scalar.activation(wqk_hi[:], raw_qk[:], ACT.Copy)
            nc.scalar.activation(below_sb[:], raw_below[:], ACT.Copy)
            act.wait_ge(s_small, 3)
            nc.scalar.activation(wm_hi[:], ps[:, 1, 0:E], ACT.Copy).then_inc(s_wraw, 1)
            act.wait_ge(s_gap, 1)
            act.wait_ge(s_pad, 1)
            act.wait_ge(s_cnt, 2)
            act.wait_ge(s_init, 1)

            def left_scores(c):
                act.wait_ge(s_th[c], 64)
                if c == 2:
                    for b in range(BLKS):
                        act.wait_ge(s_thw[b], 32)
                r = slice(c * ROWS, (c + 1) * ROWS)
                nc.scalar.activation(TAS[:, r, 0:1], M[:, r, 0:1], ACT.Identity, bias=gap[:, 0:1],
                                     scale=0.0).then_inc(s_tas, 1)
                nc.scalar.activation(TAS[:, r, 1:H], TH[:, r, 0:H - 1], ACT.Identity,
                                     bias=gap[:, 0:1]).then_inc(s_tas, 1)

            left_scores(0)
            left_scores(1)
            for i in range(BLKS):
                for g in range(NG):
                    r = slice(GR * g, GR * g + GR)
                    act.wait_ge(s_diff, i * (2 * NG) + 2 * g + 1)
                    nc.scalar.activation(C3[:, r, 0, :], C3[:, r, 0, :], ACT.Exp).then_inc(s_coef, 1)
                    act.wait_ge(s_diff, i * (2 * NG) + 2 * g + 2)
                    nc.scalar.activation(C3[:, r, 1:3, :], C3[:, r, 1:3, :], ACT.Exp,
                                         bias=gap[:, 0:1]).then_inc(s_coef, 1)
                act.wait_ge(s_lin, i * (4 * ROWS) + 4 * ROWS - 1)
                nc.scalar.activation(lrow[:, :], cells(X, i * ROWS + ROWS, 0, H + 1), ACT.Ln).then_inc(s_lnrow, 1)
                act.wait_ge(s_ren, i * 2 + 4)
                need(act, s_lst, i * 64)
                nc.scalar.activation(LNX[:, :, :], X[:, bass.ds(i * ROWS + 1, ROWS), :], ACT.Ln).then_inc(s_lnx, 1)
                if i + 2 < BLKS:
                    left_scores(i + 2)
            nc.scalar.preload_act_table_set("natural_log_exp_and_others")

            def root(k, c, n):
                act.wait_ge(s_var, k)
                nc.scalar.activation(lnv[:, c, 0:n, :], var[:, c, 0:n, :], ACT.Ln).then_inc(s_lnv, 1)
                act.wait_ge(s_lnv, k)
                nc.scalar.activation(r1[:, c, 0:n, :], lnv[:, c, 0:n, :], ACT.Exp, scale=-0.5).then_inc(s_root, 1)

            rounds = [0]

            def posterior(q):
                act.wait_ge(s_e2, q + 1)
                nc.scalar.activation(h0q[q % 3][:], h0q[q % 3][:], ACT.Exp).then_inc(s_h0, 1)

            def root_first(q):
                rounds[0] += 1
                root(rounds[0], 0, 2)

            def root_second(q):
                rounds[0] += 1
                root(rounds[0], 1, 1)

            def tokens_high(q):
                act.wait_ge(s_xntp, q + 1)
                need(act, s_qkp, q - 1)
                nc.scalar.activation(xnt_hi[q % 2][:], ps[:, 0, :], ACT.Copy).then_inc(s_xnt, 1)

            def values(q):
                need(act, s_o, 4 * q - 4)
                act.wait_ge(s_xn, q + 1)
                nc.scalar.activation(va[q % 2][:, :, :, 0:HD], xn[q % 2][:].rearrange("p b (h d) -> p b h d", d=HD),
                                     ACT.Copy).then_inc(s_va, 1)

            def qk_high(q):
                act.wait_ge(s_qkp, q + 1)
                need(act, s_qk, q)
                nc.scalar.activation(qk_hi[:], ps[:, 2, 0:T], ACT.Copy).then_inc(s_qkh, 1)

            def square(n):
                act.wait_ge(s_mn, n + 1)
                need(act, s_ptp, n - 2)
                nc.scalar.activation(sq[n % 3][:], ps[:, 3:5, :].rearrange("p a n -> p (a n)"),
                                     ACT.Square).then_inc(s_sq, 1)

            def exponentials(n):
                act.wait_ge(s_sub, n + 1)
                nc.scalar.activation(sq[n % 3][:], sq[n % 3][:], ACT.Exp, scale=-1.0 / HD ** 0.5).then_inc(s_p, 1)

            def turned(n):
                act.wait_ge(s_ptp, n + 1)
                need(act, s_o, n - 1)
                nc.scalar.activation(pt[n % 2][:, 0:512], ps[:, 5, :], ACT.Copy).then_inc(s_pta, 1)
                if n % 2 == 0:
                    nc.scalar.activation(pt[n % 2][:, 512:1024], ps[:, 6, :], ACT.Copy).then_inc(s_pta, 1)

            def heads_high(q):
                act.wait_ge(s_ontp, q + 1)
                need(act, s_rp, q)
                nc.scalar.activation(ont_hi[:], ps[:, 0, :], ACT.Copy).then_inc(s_ont, 1)

            def copy_inputs(q):
                act.wait_ge(s_x3, q + 1)
                need(act, s_sent, q - 1)
                nc.scalar.activation(pay[q % 2][:, :, 1, 0:E], pay[q % 2][:, :, 0, 0:E], ACT.Copy).then_inc(s_x3c, 1)

            def inputs(q):
                act.wait_ge(s_x3tp, q + 1)
                need(act, s_lgp, q)
                nc.scalar.activation(x3t[:], ps[:, 0, :], ACT.Copy).then_inc(s_x3t, 1)

            def gates(q):
                act.wait_ge(s_df, q + 1)
                nc.scalar.activation(gate[:, 1, :], gate[:, 0, :], ACT.Exp).then_inc(s_ex, 1)

            def weights_high(c):
                hi, _, staged = parts_of(c)
                act.wait_ge(s_stage[c % 2], 16 * (c // 2 + 1))
                nc.scalar.activation(hi, staged, ACT.Copy).then_inc(s_whi, 1)

            for n in STEPS_OF_ATTENTION:
                quad(heads_high, n, -6)
                quad(tokens_high, n, 7)
                quad(inputs, n, -12)
                pair(exponentials, n, 1)
                quad(posterior, n, 12)
                quad(root_first, n, 10)
                quad(qk_high, n, 5)
                quad(values, n, 2)
                pair(square, n, 2)
                pair(turned, n, 0)
                quad(root_second, n, -9)
                quad(copy_inputs, n, -11)
                quad(gates, n, -14)
                if 0 <= n + 1 < CHUNKS:
                    weights_high(n + 1)

            def columns(k, c):
                act.wait_ge(s_xcp, k + 1)
                if not (isinstance(k, int) and k < 2):
                    act.wait_ge(s_up, 2 * k - 2)
                nc.scalar.activation(xcol_hi[c % 2], ps[:, 0, 0:T], ACT.Copy).then_inc(s_xc, 1)

            def silu(k, c):
                act.wait_ge(s_up, 2 * k + 1)
                if not (isinstance(k, int) and k < 2):
                    act.wait_ge(s_hid, k - 1)
                nc.scalar.activation(act_up[c % 2], ps[:, 1 + c % 2, :], ACT.Silu).then_inc(s_silu, 1)

            def hidden_high(k, c):
                act.wait_ge(s_htp, k + 1)
                if not (isinstance(k, int) and k < 2):
                    act.wait_ge(s_dn, k - 1)
                nc.scalar.activation(hidt_hi[c % 2][:], ps[:, 5 + 2 * (c % 2), :], ACT.Copy).then_inc(s_ht, 1)

            def gated_low(k, c):
                act.wait_ge(s_dn, k + 1)
                act.wait_ge(s_dest, k + 1)
                if not (isinstance(k, int) and k < 2):
                    act.wait_ge(s_y, k - 1)
                nc.scalar.activation(ylow[c % 2], ps[:, 6, E:2 * E], ACT.Copy,
                                     scale=rowgate[:, c:c + 1]).then_inc(s_ylow, 1)

            def act_tile(k, c, head=False, tail=0):
                if tail < 2:
                    silu(k, c)
                if tail < 1:
                    columns(k + 1, (c + 1) % 4)
                if not (head and k < 1) and tail < 3:
                    hidden_high(k - 1, (c + 3) % 4)
                if not (head and k < 2):
                    gated_low(k - 2, (c + 2) % 4)

            columns(0, 0)
            for k in range(4):
                act_tile(k, k, head=True)
            with act.Fori(4, TILES - 4, 4) as t:
                for c in range(4):
                    act_tile(t + c, c)
            for k in range(TILES - 4, TILES + 2):
                act_tile(k, k % 4, tail=max(0, k - TILES + 2))

        @block.gpsimd
        def _(pool):
            pool.memset(padt[:], 0.0).then_inc(s_pad0, 1)
            pool.wait_ge(s_pad0, 1)
            pool.memset(padt[:, E:E + 1], float(2 * NB * T)).then_inc(s_pad0, 1)
            pool.iota(tili[:, 3, 0:TILES], [[1, TILES]], base=0, channel_multiplier=0)
            pool.memset(ones_sb[:], 1.0).then_inc(s_consts, 1)
            pool.iota(tokid[:], [[NB * T, 2], [T, NB]], base=0, channel_multiplier=1).then_inc(s_consts, 1)
            pool.memset(M[:, :, 0:1], NEG)
            pool.memset(M[:, 0, 1:H + 1], NEG)
            pool.memset(x0row[:], X0)
            pool.memset(X[:, :, 0:1], X0)
            pool.memset(X[:, 0, 1:H + 1], X0).then_inc(s_init, 1)
            pool.wait_ge(s_init, 1)
            pool.memset(M[0:64, 0, 0:1], 0.0).then_inc(s_init, 1)
            pool.wait_ge(s_thp, 8)
            pool.wait_ge(s_cnt, 2)
            pool.memset(TH[64:128, 0, :], NEG)
            pool.memset(TH[0:64, T:STEPS, :], 0.0)
            pool.memset(TH[64:128, T + 1:STEPS, :], 0.0).then_inc(s_pad, 1)
            for i in range(BLKS):
                for g in range(NG):
                    r = slice(GR * g, GR * g + GR)
                    n = N[:, r, :]
                    pool.wait_ge(s_gauge, i * (4 * ROWS) + (4 * GR * (g + 1) - 1))
                    pool.tensor_tensor(C3[:, r, 0:2, :], shifted(M, i * ROWS + GR * g, GR, 2),
                                       bass.AP(tensor=n.tensor, offset=n.offset,
                                               ap=[n.ap[0], [H, GR], [0, 2], [1, H]]),
                                       ALU.subtract).then_inc(s_diff, 1)
                    pool.tensor_tensor(C3[:, r, 2, :], M[:, bass.ds(i * ROWS + GR * g + 1, GR), 0:H], n,
                                       ALU.subtract).then_inc(s_diff, 1)
                if i < BLKS - 1:
                    pool.wait_ge(s_lnx, i + 1)
                    pool.tensor_tensor(LNX[:, :, :], LNX[:, :, :], M[:, i * ROWS + 1:i * ROWS + ROWS + 1, :],
                                       ALU.add).then_inc(s_l, 1)
            pool.wait_ge(s_lst, 16 * 4 * BLKS)
            for r in range(2):
                pool.memset(va[r][:, :, :, HD:HD + 1], 1.0).then_inc(s_consts, 1)

            def below_least(n):
                m = mn[:, n % 3, :]
                v = sq[n % 3][:].rearrange("p (h s) -> p h s", s=T)
                pool.wait_ge(s_sq, n + 1)
                pool.tensor_tensor(v, v, bass.AP(tensor=m.tensor, offset=m.offset, ap=[m.ap[0], [1, NH], [0, T]]),
                                   ALU.subtract).then_inc(s_sub, 1)

            def send(q, pairs):
                pool.wait_ge(s_slot, q + 1)
                pool.wait_ge(s_x3c, q + 1)
                pool.wait_ge(s_pay, q + 1)
                for k in pairs:
                    for j in range(2):
                        pool.indirect_dma_start(xd_dram, bass.IndirectOffsetOnAxis(slot[:, q, j, k:k + 1], 0),
                                                pay[q % 2][:, k, j, :], None).then_inc(s_sc[2 * k + j], 16)

            def send_two(q):
                send(q, (0, 1))

            def send_others(q):
                send(q, (2, 3))

            def sent(q):
                if q + 2 >= NQ:
                    return
                for k in range(8):
                    pool.wait_ge(s_sc[k], 16 * q + 16)
                pool.engine_nop().then_inc(s_sent, 1)

            for n in STEPS_OF_ATTENTION:
                quad(sent, n, -18)
                pair(below_least, n, 2)
                quad(send_two, n, -16)
                quad(send_others, n, -17)

            def scatter(k, c):
                pool.wait_ge(s_dest, k + 1)
                pool.wait_ge(s_y, k + 1)
                pool.nop(nofuse=True)
                pool.indirect_dma_start(y_dram, bass.IndirectOffsetOnAxis(dest[:, c:c + 1], 0), yrow[c], None,
                                        bounds_check=2 * NB * T - 1, oob_is_err=False).then_inc(s_ys[c], 16)

            with pool.Fori(0, TILES, 4) as t:
                for c in range(4):
                    scatter(t + c, c)

        @block.vector
        def _(dve):
            chain = [0]

            def link(ins):
                chain[0] += 1
                ins.then_inc(s_dv, 1)
                dve.wait_ge(s_dv, chain[0])

            V_ = nc.vector
            dve.wait_ge(s_small, 1)
            V_.tensor_scalar(zt[:], ps[:, 0, 0:NV], bproj_sb[:, 0:1], None, ALU.add).then_inc(s_smallv, 1)
            dve.wait_ge(s_in, 16 * 6)
            dve.wait_ge(s_tok, 16)
            V_.tensor_scalar(ohy[:], toky[:], iota_sb[0:NV, 0:1], None, ALU.is_equal).then_inc(s_ohy, 1)
            dve.wait_ge(s_small, 2)
            V_.tensor_copy(uv[:], ps[0:NV, 2, 0:2])
            link(V_.tensor_copy(gm[:], ps[0:NV, 1, 0:NV]))
            link(V_.tensor_copy(gpart[:, 0, :], gm[:]))
            link(V_.tensor_tensor(gleft[:, 0, :], gm[:], gpart[:, 0, :], ALU.subtract))
            link(V_.tensor_copy(gpart[:, 1, :], gleft[:, 0, :]))
            link(V_.tensor_tensor(gleft[:, 1, :], gleft[:, 0, :], gpart[:, 1, :], ALU.subtract))
            V_.tensor_copy(gpart[:, 2, :], gleft[:, 1, :]).then_inc(s_smallv, 1)
            dve.wait_ge(s_tokx, 16)
            V_.tensor_scalar(ohx[:], tokx[:], iota_sb[:, 0:1], None, ALU.is_equal).then_inc(s_oh, 1)
            dve.wait_ge(s_ohy, 1)
            V_.reduce_sum(cnt[:, 1, 0, :], ohy[:, :].rearrange("p (b i) -> p b i", i=T), AX.X).then_inc(s_cnt, 1)
            for q in range(8):
                dve.wait_ge(s_thf, q + 1)
                V_.tensor_copy(thr[:, 4 * q:4 * q + 4, :],
                               ps[:, q, :].rearrange("p (b j) -> p b j", j=T)[:, :, ::-1]).then_inc(s_thr, 1)
            dve.wait_ge(s_oh, 1)
            V_.reduce_sum(cnt[:, 0, 0, :], ohx[0:NV, :].rearrange("p (b i) -> p b i", i=T), AX.X).then_inc(s_cnt, 1)
            dve.wait_ge(s_cnt, 2)
            for k in range(1, 4):
                m = V_.tensor_copy(cnt[:, :, k, :], cnt[:, :, 0, :])
            m.then_inc(s_cnt, 1)
            dve.wait_ge(s_small, 3)
            V_.tensor_scalar(gap[:], ps[:, 0, 0:1], 1.0 / T, bgap_sb[:, 0:1], ALU.mult, ALU.add).then_inc(s_gap, 1)
            dve.wait_ge(s_wraw, 1)
            V_.tensor_tensor(wqk_lo[:], raw_qk[:], wqk_hi[:].bitcast(f32), ALU.subtract)
            V_.tensor_tensor(wm_lo[:], ps[:, 1, 0:E], wm_hi[:].bitcast(f32), ALU.subtract)
            dve.wait_ge(s_consts, 2)
            V_.tensor_copy(tokf[:], tokid[:])
            V_.tensor_copy(run[:, 0, :], region_sb[:]).then_inc(s_consts, 1)
            dve.wait_ge(s_gap, 1)
            dve.wait_ge(s_init, 2)
            dve.wait_ge(s_consts, 3)
            dve.engine_nop().then_inc(s_ren, 1)
            dve.engine_nop().then_inc(s_ren, 1)

            def row(t, s):
                return cells(t, s, 1, H + 1)

            for i in range(BLKS):
                def gauge(k):
                    s = i * ROWS + k
                    done = i * (4 * ROWS) + 4 * k
                    c = C[:, k % 2, :]

                    def best_from_above():
                        if k == 0:
                            dve.wait_ge(s_ren, i * 2 + 2)
                            dve.wait_ge(s_tas, 2 * i + 2)
                        else:
                            dve.wait_ge(s_gauge, done - 1)
                        nc.vector.scalar_tensor_tensor(c, row(M, s), gap[:, 0:1], cells(M, s, 0, H),
                                                       ALU.add, ALU.max).then_inc(s_gauge, 1)

                    def best_of_row():
                        dve.wait_ge(s_gauge, done + 1)
                        nc.vector.tensor_tensor_scan(N[:, k, :], cells(TAS, s, 0, H), c,
                                                     cells(M, s + 1, 0, 1), ALU.add,
                                                     ALU.max).then_inc(s_gauge, 1)

                    def add_theta():
                        dve.wait_ge(s_gauge, done + 2)
                        nc.vector.tensor_tensor(row(M, s + 1), N[:, k, :], cells(TH, s, 0, H),
                                                ALU.add).then_inc(s_gauge, 1)

                    def to_right_half():
                        if k < ROWS - 1:
                            dve.wait_ge(s_gauge, done + 3)
                            nc.vector.tensor_copy(M[64:128, bass.ds(s + 2, 1), 0:1],
                                                  M[0:64, bass.ds(s + 1, 1), H:H + 1]).then_inc(s_gauge, 1)
                    return [best_from_above, best_of_row, add_theta, to_right_half]

                def linear(k):
                    s = i * ROWS + k
                    done = i * (4 * ROWS) + 4 * k

                    def weigh():
                        if k % GR == 0:
                            dve.wait_ge(s_coef, i * (2 * NG) + 2 * (k // GR) + 2)
                        if k == 0:
                            dve.wait_ge(s_ren, i * 2 + 2)
                        else:
                            dve.wait_ge(s_lin, done - 1)
                        x = shifted(X, s, 1, 2)
                        x = bass.AP(tensor=x.tensor, offset=x.offset, ap=[x.ap[0], x.ap[2], x.ap[3]])
                        nc.vector.tensor_tensor(U[:, k % 2], x, C3[:, k, 0:2, :], ALU.mult).then_inc(s_lin, 1)

                    def add():
                        dve.wait_ge(s_lin, done + 1)
                        nc.vector.tensor_tensor(V[:, k % 2, :], U[:, k % 2, 0, :], U[:, k % 2, 1, :],
                                                ALU.add).then_inc(s_lin, 1)

                    def scan():
                        dve.wait_ge(s_lin, done + 2)
                        nc.vector.tensor_tensor_scan(row(X, s + 1), C3[:, k, 2, :], V[:, k % 2, :],
                                                     cells(X, s + 1, 0, 1), ALU.mult,
                                                     ALU.add).then_inc(s_lin, 1)

                    def to_right_half():
                        if k < ROWS - 1:
                            dve.wait_ge(s_lin, done + 3)
                            nc.vector.tensor_copy(X[64:128, bass.ds(s + 2, 1), 0:1],
                                                  X[0:64, bass.ds(s + 1, 1), H:H + 1]).then_inc(s_lin, 1)
                    return [weigh, add, scan, to_right_half]

                LAG = 3
                for k in range(ROWS + LAG):
                    a = gauge(k) if k < ROWS else []
                    b = linear(k - LAG) if k >= LAG else []
                    for n in range(4):
                        if a:
                            a[n]()
                        if b:
                            b[n]()
                last = i * ROWS + ROWS
                dve.wait_ge(s_lnrow, i + 1)
                nc.vector.scalar_tensor_tensor(cells(M, last, 0, H + 1), lrow[:, :], LNX0,
                                               cells(M, last, 0, H + 1), ALU.add, ALU.add).then_inc(s_gauge, 1)
                nc.vector.tensor_copy(cells(X, last, 0, H + 1), x0row[:]).then_inc(s_lin, 1)
                dve.wait_ge(s_gauge, i * (4 * ROWS) + 4 * ROWS)
                dve.wait_ge(s_lin, i * (4 * ROWS) + 4 * ROWS)
                nxt = last + 1
                nc.vector.tensor_copy(M[64:128, bass.ds(nxt, 1), 0:1], M[0:64, bass.ds(last, 1), H:H + 1]).then_inc(s_ren, 1)
                nc.vector.tensor_copy(X[64:128, bass.ds(nxt, 1), 0:1], X[0:64, bass.ds(last, 1), H:H + 1]).then_inc(s_ren, 1)
            dve.wait_ge(s_lnx, BLKS)
            V_.tensor_tensor(LNX[:, :, :], LNX[:, :, :], M[:, STEPS - ROWS + 1:STEPS + 1, :], ALU.add).then_inc(s_l, 1)

            def over(a, n):
                return bass.AP(tensor=a.tensor, offset=a.offset, ap=[a.ap[0], a.ap[1], [0, n]])

            def each(a, n):
                return bass.AP(tensor=a.tensor, offset=a.offset, ap=[a.ap[0], [0, n], a.ap[1]])

            dve.wait_ge(s_v, 16)
            link(V_.tensor_scalar(nvt[:], vtot[:], -1.0, LNX0, ALU.mult, ALU.add))

            def log_posterior(q):
                b = slice(4 * q, 4 * q + 4)
                h = h0q[q % 3]
                dve.wait_ge(s_ldq[q], 32)
                link(V_.tensor_tensor(h[:], h[:], thf[:, b, :], ALU.subtract))
                for k in range(4):
                    m = V_.scalar_tensor_tensor(h[:, k, :], h[:, k, :], nvt[:, 4 * q + k:4 * q + k + 1],
                                                lbq[q % 2][:, k, ::-1], ALU.add, ALU.add)
                m.then_inc(s_e2, 1)

            def moments(c, src):
                for k in range(4):
                    m = V_.bn_stats(st6[:, k, :], src(k))
                link(m)
                for k in range(4):
                    m = V_.bn_aggr(mv[:, c, k, :], st6[:, k, :])
                link(m)
                m = V_.tensor_scalar(var[:, c, 0, :], mv[:, c, :, 1], EPS, None, ALU.add)
                if c == 0:
                    link(m)
                    m = V_.scalar_tensor_tensor(var[:, 0, 1, :], var[:, 0, 0, :], EPS, mv[:, 0, :, 1], ALU.mult, ALU.add)
                m.then_inc(s_var, 1)

            rounds = [0]

            def inverse_roots(c, n):
                y, r, t = var[:, c, 0:n, :], r1[:, c, 0:n, :], nwt[:, 0:n, :]
                rounds[0] += 1
                dve.wait_ge(s_root, rounds[0])
                link(V_.tensor_tensor(t, r, r, ALU.mult))
                link(V_.tensor_tensor(t, t, y, ALU.mult))
                link(V_.tensor_scalar(t, t, -0.5, 1.5, ALU.mult, ALU.add))
                link(V_.tensor_tensor(r, r, t, ALU.mult))

            def first_moments(q):
                dve.wait_ge(s_h0, q + 1)
                moments(0, lambda k: h0q[q % 3][:, k, :])

            def first_norms(q):
                h = h0q[q % 3]
                inverse_roots(0, 2)
                for k in range(4):
                    m = V_.tensor_scalar(x1[q % 2][:, k, :], h[:, k, :], mv[:, 0, k, 0:1], r1[:, 0, 0, k:k + 1],
                                         ALU.subtract, ALU.mult)
                link(m)
                need(dve, s_va, q - 1)
                need(dve, s_xntp, q - 1)
                for k in range(4):
                    m = V_.tensor_scalar(xn[q % 2][:, k, :], h[:, k, :], mv[:, 0, k, 0:1], r1[:, 0, 1, k:k + 1],
                                         ALU.subtract, ALU.mult)
                m.then_inc(s_xn, 1)
                V_.tensor_tensor(h1[:, 4 * q:4 * q + 4, :], h[:], x1[q % 2][:], ALU.add).then_inc(s_hx, 1)

            def tokens_low(q):
                dve.wait_ge(s_xnt, q + 1)
                need(dve, s_qkp, q - 1)
                V_.tensor_tensor(xnt_lo[q % 2][:], ps[:, 0, :], xnt_hi[q % 2][:].bitcast(f32),
                                 ALU.subtract).then_inc(s_xntl, 1)

            def queries_keys(q):
                dve.wait_ge(s_qkh, q + 1)
                need(dve, s_d, 4 * q - 4)
                link(V_.scalar_tensor_tensor(qk_x[:], qk_hi[:].bitcast(f32), rowc_sb[:, 0:1], ps[:, 2, 0:T],
                                             ALU.mult, ALU.add))
                V_.tensor_scalar(qs[q % 2][:], qk_x[:], rowc_sb[:, 1:2], rowc_sb[:, 2:3], ALU.mult, ALU.add)
                link(V_.tensor_scalar(qk_k[:], qk_x[:], rowc_sb[:, 3:4], rowc_sb[:, 4:5], ALU.mult, ALU.add))
                V_.tensor_tensor(kx[q % 2][:].rearrange("p (h s) -> p h s", s=T), each(qk_k[:], NH),
                                 over(mask_sb[:], T), ALU.mult).then_inc(s_qk, 1)

            def nearest(n):
                dve.wait_ge(s_d, n + 1)
                need(dve, s_sub, n - 2)
                link(V_.tensor_reduce(rc[:, 0, :], ps[:, 3:5, :].rearrange("p a (h s) -> p (a h) s", s=T),
                                      AX.X, ALU.min, apply_absolute_value=True))
                V_.tensor_tensor(mn[:, n % 3, :], rc[:, 0, :], rc[:, 0, :], ALU.mult).then_inc(s_mn, 1)

            def turned(n):
                if n % 2:
                    dve.wait_ge(s_ptp, n + 1)
                    need(dve, s_o, n - 1)
                    V_.tensor_copy(pt[n % 2][:, 512:1024], ps[:, 6, :]).then_inc(s_ptd, 1)

            def normalise(n):
                q, k = n // 4, n % 4
                dve.wait_ge(s_o, n + 1)
                need(dve, s_ontp, q - 1)
                o = ps[:, 7, 0:NH * (HD + 1)].rearrange("p (h d) -> p h d", d=HD + 1)
                link(V_.reciprocal(rc[:, 1, :], o[:, :, HD]))
                V_.tensor_tensor(on[q % 2][:, k, :].rearrange("p (h d) -> p h d", d=HD), o[:, :, 0:HD],
                                 over(rc[:, 1, :], HD), ALU.mult).then_inc(s_on, 1)

            def heads_low(q):
                dve.wait_ge(s_ont, q + 1)
                need(dve, s_rp, q)
                V_.tensor_tensor(ont_lo[:], ps[:, 0, :], ont_hi[:].bitcast(f32), ALU.subtract).then_inc(s_ontl, 1)

            def residual(q):
                dve.wait_ge(s_rp, q + 1)
                b = slice(4 * q, 4 * q + 4)
                V_.tensor_tensor(h1[:, b, :], h1[:, b, :], ps[:, 1, :].rearrange("p (b j) -> p b j", j=T),
                                 ALU.add).then_inc(s_h1, 1)
                dve.wait_ge(s_h1, q + 1)
                moments(1, lambda k: h1[:, 4 * q + k, :])

            def second_norms(q):
                inverse_roots(1, 1)
                need(dve, s_sent, q - 1)
                for k in range(4):
                    m = V_.tensor_scalar(pay[q % 2][:, k, 0, 0:E], h1[:, 4 * q + k, :], mv[:, 1, k, 0:1], r1[:, 1, 0, k:k + 1],
                                         ALU.subtract, ALU.mult)
                m.then_inc(s_x3, 1)

            def pick(src, k):
                link(V_.tensor_reduce(top[:, k, :], src, AX.X, ALU.max))
                link(V_.tensor_tensor(eq[:], src, over(top[:, k, :], NX), ALU.is_equal))
                link(V_.tensor_tensor(eq[:], eq[:], each(rank8_sb[:], 4), ALU.mult))
                link(V_.tensor_reduce(first[:], eq[:], AX.X, ALU.max))
                link(V_.tensor_tensor(ohk[:, k], each(rank8_sb[:], 4), over(first[:], NX), ALU.is_equal))

            def choose(q):
                dve.wait_ge(s_lgp, q + 1)
                link(V_.tensor_copy(lg[:], ps[:, 2, 256:288].rearrange("p (b e) -> p b e", e=NX)))
                pick(lg[:], 0)
                link(V_.scalar_tensor_tensor(lg2[:], ohk[:, 0], -1e30, lg[:], ALU.mult, ALU.add))
                pick(lg2[:], 1)
                V_.tensor_tensor(msk[:], ohk[:, 0], ohk[:, 1], ALU.add).then_inc(s_msk, 1)
                V_.tensor_tensor(gate[:, 0, :], top[:, 1, :], top[:, 0, :], ALU.subtract).then_inc(s_df, 1)

            def read_ranks(q):
                dve.wait_ge(s_rkp, q + 1)
                V_.tensor_copy(ranks[:], ps[:, 0, 0:64]).then_inc(s_rkc, 1)

            def places(q):
                dve.wait_ge(s_rkc, q + 1)
                for k in range(4):
                    link(V_.tensor_tensor(run[:, 4 * q + k + 1, :], run[:, 4 * q + k, :],
                                          ranks[:, 32 + NX * k:40 + NX * k], ALU.add))
                link(V_.tensor_tensor(rank[:], run[:, 4 * q:4 * q + 4, :],
                                      ranks[:, 0:32].rearrange("p (b e) -> p b e", e=NX), ALU.add))
                V_.tensor_tensor(ohk[:, 0], ohk[:, 0], rank[:], ALU.mult)
                link(V_.tensor_tensor(ohk[:, 1], ohk[:, 1], rank[:], ALU.mult))
                link(V_.tensor_reduce(slotf[:], ohk[:], AX.X, ALU.add))
                V_.tensor_copy(slot[:, q], slotf[:]).then_inc(s_slot, 1)
                dve.wait_ge(s_ex, q + 1)
                link(V_.tensor_scalar(gate[:, 0, :], gate[:, 1, :], 1.0, None, ALU.add))
                link(V_.reciprocal(top[:, 0, :], gate[:, 0, :]))
                link(V_.tensor_tensor(top[:, 1, :], top[:, 0, :], gate[:, 1, :], ALU.mult))
                for j in range(2):
                    V_.tensor_copy(pay[q % 2][:, :, j, E:E + 1].rearrange("p b o -> p (b o)"), tokf[:, j, 4 * q:4 * q + 4])
                    m = V_.tensor_copy(pay[q % 2][:, :, j, E + 1:ROW].rearrange("p b o -> p (b o)"), top[:, j, :])
                m.then_inc(s_pay, 1)

            def weights_low(c):
                hi, lo, staged = parts_of(c)
                dve.wait_ge(s_whi, c + 1)
                V_.tensor_tensor(lo, staged, hi.bitcast(f32), ALU.subtract).then_inc(s_wlo, 1)

            for n in STEPS_OF_ATTENTION:
                quad(heads_low, n, -6)
                quad(tokens_low, n, 7)
                quad(read_ranks, n, -15)
                pair(nearest, n, 2)
                quad(queries_keys, n, 4)
                quad(residual, n, -8)
                quad(first_moments, n, 11)
                pair(turned, n, 0)
                quad(second_norms, n, -10)
                quad(first_norms, n, 9)
                pair(normalise, n, -1)
                quad(choose, n, -13)
                quad(places, n, -15)
                quad(log_posterior, n, 14)
                if 0 <= n < CHUNKS:
                    weights_low(n)
            counts, tiles, ends, jump = (tl[:, k, :] for k in range(4))
            link(V_.tensor_tensor(counts, run[:, NB, :], region_sb[:], ALU.subtract))
            V_.tensor_copy(tili[:, 2, 0:NX], run[:, NB, :]).then_inc(s_counts, 1)
            link(V_.memset(ones8, 1.0))
            link(V_.tensor_scalar(tili[:, 2, NX:2 * NX], counts, 127.0, None, ALU.add))
            link(V_.tensor_single_scalar(tili[:, 2, 2 * NX:3 * NX], tili[:, 2, NX:2 * NX], 7, ALU.arith_shift_right))
            link(V_.tensor_copy(tiles, tili[:, 2, 2 * NX:3 * NX]))
            link(V_.tensor_tensor_scan(ends, ones8, tiles, 0.0, ALU.mult, ALU.add))
            link(V_.tensor_scalar(jump, tiles, -1.0, float(REG // 128), ALU.mult, ALU.add))
            link(V_.tensor_copy(tilesf, tili[:, 3, 0:TILES]))
            link(V_.tensor_tensor(past, over(tilesf, NX), each(ends, TILES), ALU.is_ge))
            link(V_.tensor_reduce(tilf[:, 0, :], past[:, :, 0:NX - 1], AX.X, ALU.add))
            link(V_.tensor_tensor(past, past, each(jump, TILES), ALU.mult))
            link(V_.tensor_reduce(tilf[:, 1, :], past, AX.X, ALU.add))
            link(V_.tensor_tensor(tilf[:, 2, :], tilf[:, 1, :], tilesf, ALU.add))
            link(V_.tensor_scalar(tilf[:, 3, :], tilf[:, 2, :], 128.0, float(NX * REG), ALU.mult, ALU.min))
            V_.tensor_copy(tili[:, 1, 0:TILES], tilf[:, 0, :])
            V_.tensor_copy(tili[:, 0, 0:TILES], tilf[:, 3, :]).then_inc(s_table, 1)

            def hidden(k, c):
                dve.wait_ge(s_silu, k + 1)
                dve.wait_ge(s_up, 2 * k + 2)
                if not (isinstance(k, int) and k < 2):
                    dve.wait_ge(s_htp, k - 1)
                V_.tensor_tensor(hid[c % 2], act_up[c % 2], ps[:, 3 + c % 2, :], ALU.mult).then_inc(s_hid, 1)

            def destination(k, c):
                dve.wait_ge(s_xr[c], round_of(k, c))
                if not (isinstance(k, int) and k < 4):
                    dve.wait_ge(s_ys[c], round_of(k, c) - 16)
                V_.tensor_copy(rowgate[:, c:c + 1], xrow[c][:, E + 1:ROW])
                V_.tensor_copy(dest[:, c:c + 1], xrow[c][:, E:E + 1]).then_inc(s_dest, 1)

            def column_low(k, c):
                dve.wait_ge(s_xc, k + 1)
                if not (isinstance(k, int) and k < 2):
                    dve.wait_ge(s_up, 2 * k - 2)
                V_.tensor_tensor(xcol_lo[c % 2], ps[:, 0, 0:T], xcol_hi[c % 2].bitcast(f32),
                                 ALU.subtract).then_inc(s_xcl, 1)

            def hidden_low(k, c):
                dve.wait_ge(s_ht, k + 1)
                if not (isinstance(k, int) and k < 2):
                    dve.wait_ge(s_dn, k - 1)
                V_.tensor_tensor(hidt_lo[c % 2][:], ps[:, 5 + 2 * (c % 2), :], hidt_hi[c % 2][:].bitcast(f32),
                                 ALU.subtract).then_inc(s_htl, 1)

            def gated(k, c):
                dve.wait_ge(s_ylow, k + 1)
                if not (isinstance(k, int) and k < 4):
                    dve.wait_ge(s_ys[c], round_of(k, c) - 16)
                V_.scalar_tensor_tensor(yrow[c], ps[:, 6, 0:E], rowgate[:, c:c + 1], ylow[c % 2], ALU.mult,
                                        ALU.add).then_inc(s_y, 1)

            def dve_tile(k, c, head=False, tail=0):
                if tail < 2:
                    hidden(k, c)
                if tail < 1:
                    column_low(k + 1, (c + 1) % 4)
                if tail < 2:
                    destination(k, c)
                if not (head and k < 1) and tail < 3:
                    hidden_low(k - 1, (c + 3) % 4)
                if not (head and k < 2):
                    gated(k - 2, (c + 2) % 4)

            column_low(0, 0)

            for k in range(4):
                dve_tile(k, k, head=True)
            with dve.Fori(4, TILES - 4, 4) as t:
                for c in range(4):
                    dve_tile(t + c, c)
            for k in range(TILES - 4, TILES + 2):
                dve_tile(k, k % 4, tail=max(0, k - TILES + 2))
            for q in range(NQ):
                b = slice(4 * q, 4 * q + 4)
                dve.wait_ge(s_yl[q], 32)
                V_.tensor_tensor(h1[:, b, :], h1[:, b, :], ya[q], ALU.add).then_inc(s_fin, 1)
                dve.wait_ge(s_fin, 2 * q + 1)
                V_.tensor_tensor(h1[:, b, :], h1[:, b, :], yb[q], ALU.add).then_inc(s_fin, 1)


def kernel(**inputs):
    import numpy as np
    import concourse.bacc as bacc
    from concourse import mybir
    from concourse.bass_utils import run_bass_kernel_spmd as run

    nc = bacc.Bacc("TRN2", target_bir_lowering=False, num_devices=1)
    x = np.asarray(inputs["x"])
    y = np.asarray(inputs["itok_BS_0_21"])
    laid = {
        "tok_x": x.reshape(-1), "tok_y": y.reshape(-1),
        "we_t": np.asarray(inputs["L0_tok_W_embed"]).T,
        "w_proj": np.asarray(inputs["L0_tok_W_proj"]),
        "b_proj": np.asarray(inputs["L0_tok_b_proj"]).reshape(-1, 1),
        "w_gap": np.asarray(inputs["L0_tok_W_gap"]).reshape(2, 128).T,
        "b_gap": np.broadcast_to(np.asarray(inputs["L0_tok_b_gap"]).reshape(1, 1), (128, 1)),
        "iota66": (np.arange(66, dtype=np.float32) % 22).reshape(66, 1),
    }
    wq, wk, wv = (np.asarray(inputs["L0_attn_W" + c]) for c in "qkv")
    NH, HD = wq.shape
    wqk_pl = np.zeros((4, 128, 128), wq.dtype)
    wv_bd = np.zeros((128, 128), wv.dtype)
    for h in range(NH):
        r = slice(HD * h, HD * h + HD)
        for g in range(4):
            for part in range(2):
                wqk_pl[g, r, 32 * g + NH * part + h] = wq[h]
                wqk_pl[g, r, 32 * g + NH * (2 + part) + h] = wk[h]
        wv_bd[r, r] = wv[h].T
    p = np.arange(128)
    f = np.float32
    part = p % 32 // NH
    q_or_k = part // 2
    laid.update({
        "wqk_pl": wqk_pl, "wv_bd": wv_bd,
        "w_m": np.asarray(inputs["L0_attn_Wm"]), "w_g": np.asarray(inputs["L0_ffn_Wg"]),
        "w_up": np.asarray(inputs["L0_ffn_W"]), "v_up": np.asarray(inputs["L0_ffn_V"]),
        "w_down": np.asarray(inputs["L0_ffn_W2"]),
        "eye": np.eye(128, dtype=f), "below": (p[:, None] < p[None, :]).astype(f),
        "head_mask": (p[:, None] % NH == np.arange(NH)).astype(f),
        "row_consts": np.stack([-(part % 2), 1 - q_or_k, -q_or_k, q_or_k, 1 - q_or_k], 1).astype(f),
        "rank8": np.broadcast_to(8 - np.arange(8, dtype=f), (128, 8)),
        "region0": np.broadcast_to((32 * 128 + 128) * np.arange(8, dtype=f), (128, 8)),
    })
    arrays, args = {}, []
    for name, a in laid.items():
        a = np.ascontiguousarray(a)
        arrays["in_" + name] = a
        args.append(nc.dram_tensor("in_" + name, a.shape, mybir.dt.from_np(a.dtype), kind="ExternalInput").ap())
    args.append(nc.dram_tensor("out", (32, 128, 128), mybir.dt.float32, kind="ExternalOutput").ap())
    tower(nc, *args)
    r = run(nc, [arrays], core_ids=[0])
    return r.results[0]["out"]
```
